# Optimizing a Trainium2 kernel written in Bass

```python
import numpy as np
import jax
import jax.numpy as jnp

def _softmax(x, axis=-1):
    return jax.nn.softmax(x, axis=axis)

def _gelu(x):
    return jax.nn.gelu(x, approximate=True)

def _silu(x):
    return jax.nn.silu(x)

def _sigmoid(x):
    return jax.nn.sigmoid(x)

def _layernorm(x, axis=-1, eps=1e-05):
    m = jnp.mean(x, axis=axis, keepdims=True)
    v = jnp.var(x, axis=axis, keepdims=True)
    return (x - m) / jnp.sqrt(v + eps)

def _scatter_add(tgt, idx, src, axis=0):
    return tgt.at[idx].add(src)

def _segment_sum(src, seg, n):
    return jax.ops.segment_sum(src, seg, n)
kernel_name = 'mk_vit_tower_d2_tok_img256_r4_6ba091'

def setup_inputs(seed: int=0):
    np.random.seed(seed)
    _w = jnp.asarray

    def _rec_inputs():
        import jax
        import jax.numpy as jnp
        _rk = jax.random.key(seed)
        x = -0.000222058 + 0.999998 * jax.random.normal(jax.random.fold_in(_rk, 1), (64, 3, 224, 224), jnp.float32)
        return x
    x = _rec_inputs()

    def _L0_tok_setup():
        import jax, jax.numpy as jnp
        import numpy as np
        IMAGE_SIZE = 64
        PATCH = 16
        EMBED_DIM = 64
        IN_CH = 3
        BATCH = 128
        IN_DIM = IN_CH * PATCH * PATCH

        def _patchify(x, p):
            B, C, H, Wd = x.shape
            x = x.reshape(B, C, H // p, p, Wd // p, p)
            x = x.transpose(0, 2, 4, 1, 3, 5)
            return x.reshape(B, H // p * (Wd // p), C * p * p)
        key = jax.random.key(seed)
        kx, kw, kb = jax.random.split(key, 3)
        x = jax.random.normal(kx, (BATCH, IN_CH, IMAGE_SIZE, IMAGE_SIZE), dtype=jnp.float32)
        W = jax.random.normal(kw, (EMBED_DIM, IN_DIM), dtype=jnp.float32) * (1.0 / np.sqrt(IN_DIM))
        b = jax.random.normal(kb, (EMBED_DIM,), dtype=jnp.float32) * 0.01
        return {'x': x, 'W': W, 'b': b}
    _L0_tok_all = _L0_tok_setup()
    _L0_tok_in = {k: v for k, v in _L0_tok_all.items() if k in ('W', 'b')}
    del _L0_tok_all

    def _L0_attn_setup():
        import jax, jax.numpy as jnp
        import numpy as np
        B, S, C = (8, 256, 64)
        H, KD = (8, 64)
        HEAD_DIM = KD // H
        key = jax.random.key(seed)
        ks = jax.random.split(key, 5)
        sc = 0.02
        return {'x': jax.random.normal(ks[0], (B, S, C), dtype=jnp.float32), 'Wq': jax.random.normal(ks[1], (H * KD, C), dtype=jnp.float32) * sc, 'Wk': jax.random.normal(ks[2], (KD, C), dtype=jnp.float32) * sc, 'Wv': jax.random.normal(ks[3], (KD, C), dtype=jnp.float32) * sc, 'Wo': jax.random.normal(ks[4], (C, H * KD), dtype=jnp.float32) * sc}
    _L0_attn_all = _L0_attn_setup()
    _L0_attn_in = {k: v for k, v in _L0_attn_all.items() if k in ('Wq', 'Wk', 'Wv', 'Wo')}
    del _L0_attn_all

    def _L0_ffn_setup():
        import jax, jax.numpy as jnp
        import numpy as np
        B, S, D, H, E, K = (8, 2048, 64, 256, 8, 2)
        key = jax.random.key(seed)
        ks = jax.random.split(key, 7)
        s_in = 1.0 / np.sqrt(D)
        s_hid = 1.0 / np.sqrt(H)
        return {'x': jax.random.normal(ks[0], (B, S, D), dtype=jnp.float32), 'Wg': jax.random.uniform(ks[1], (E, D), jnp.float32, -s_in, s_in), 'bg': jax.random.uniform(ks[2], (E,), jnp.float32, -s_in, s_in), 'W1': jax.random.uniform(ks[3], (E, H, D), jnp.float32, -s_in, s_in), 'b1': jax.random.uniform(ks[4], (E, H), jnp.float32, -s_in, s_in), 'W2': jax.random.uniform(ks[5], (E, D, H), jnp.float32, -s_hid, s_hid), 'b2': jax.random.uniform(ks[6], (E, D), jnp.float32, -s_hid, s_hid)}
    _L0_ffn_all = _L0_ffn_setup()
    _L0_ffn_in = {k: v for k, v in _L0_ffn_all.items() if k in ('Wg', 'bg', 'W1', 'b1', 'W2', 'b2')}
    del _L0_ffn_all

    def _L1_attn_setup():
        import jax, jax.numpy as jnp
        import numpy as np
        B, N, C = (8, 2048, 64)
        HEADS, DH, KR = (8, 32, 4)
        INNER = HEADS * DH
        FF = 4 * C
        EPS = 1e-05

        def layernorm(x, g, b):
            mu = jnp.mean(x, axis=-1, keepdims=True)
            var = jnp.mean((x - mu) ** 2, axis=-1, keepdims=True)
            return (x - mu) * jax.lax.rsqrt(var + EPS) * g + b
        key = jax.random.key(seed)
        ks = jax.random.split(key, 16)
        s = 0.02
        return {'x': jax.random.normal(ks[0], (B, N, C), jnp.float32), 'ln1_g': jnp.ones((C,), jnp.float32), 'ln1_b': jnp.zeros((C,), jnp.float32), 'Wx': jax.random.normal(ks[1], (C, INNER), jnp.float32) * s, 'bx': jnp.zeros((INNER,), jnp.float32), 'Wq': jax.random.normal(ks[2], (DH, KR), jnp.float32) * s, 'Wk': jax.random.normal(ks[3], (DH, KR), jnp.float32) * s, 'Wv': jax.random.normal(ks[4], (DH, DH), jnp.float32) * s, 'Wo': jax.random.normal(ks[5], (INNER, C), jnp.float32) * s, 'bo': jnp.zeros((C,), jnp.float32), 'ln2_g': jnp.ones((C,), jnp.float32), 'ln2_b': jnp.zeros((C,), jnp.float32), 'W1': jax.random.normal(ks[6], (C, FF), jnp.float32) * s, 'b1': jnp.zeros((FF,), jnp.float32), 'W2': jax.random.normal(ks[7], (FF, C), jnp.float32) * s, 'b2': jnp.zeros((C,), jnp.float32)}
    _L1_attn_all = _L1_attn_setup()
    _L1_attn_in = {k: v for k, v in _L1_attn_all.items() if k in ('ln1_g', 'ln1_b', 'Wx', 'bx', 'Wq', 'Wk', 'Wv', 'Wo', 'bo', 'ln2_g', 'ln2_b', 'W1', 'b1', 'W2', 'b2')}
    del _L1_attn_all

    def _L1_ffn_setup():
        import jax, jax.numpy as jnp
        import numpy as np
        B, S, D = (8, 1024, 64)
        H = 4 * D
        CAPACITY = 0.5
        key = jax.random.key(seed)
        ks = jax.random.split(key, 6)
        x = jax.random.normal(ks[0], (B, S, D), dtype=jnp.float32)
        attention_mask = jnp.zeros((B, 1, 1, S), dtype=jnp.float32)
        wr = jax.random.normal(ks[1], (D, 1), dtype=jnp.float32) * 0.02
        br = jnp.zeros((1,), dtype=jnp.float32)
        w1 = jax.random.normal(ks[2], (D, H), dtype=jnp.float32) * 0.02
        b1 = jnp.zeros((H,), dtype=jnp.float32)
        w2 = jax.random.normal(ks[3], (H, D), dtype=jnp.float32) * 0.02
        b2 = jnp.zeros((D,), dtype=jnp.float32)
        return {'x': x, 'attention_mask': attention_mask, 'wr': wr, 'br': br, 'w1': w1, 'b1': b1, 'w2': w2, 'b2': b2}
    _L1_ffn_all = _L1_ffn_setup()
    _L1_ffn_in = {k: v for k, v in _L1_ffn_all.items() if k in ('attention_mask', 'wr', 'br', 'w1', 'b1', 'w2', 'b2')}
    del _L1_ffn_all
    return {'x': x, 'L0_tok_W': _L0_tok_in['W'], 'L0_tok_b': _L0_tok_in['b'], 'L0_attn_Wq': _L0_attn_in['Wq'], 'L0_attn_Wk': _L0_attn_in['Wk'], 'L0_attn_Wv': _L0_attn_in['Wv'], 'L0_attn_Wo': _L0_attn_in['Wo'], 'L0_ffn_Wg': _L0_ffn_in['Wg'], 'L0_ffn_bg': _L0_ffn_in['bg'], 'L0_ffn_W1': _L0_ffn_in['W1'], 'L0_ffn_b1': _L0_ffn_in['b1'], 'L0_ffn_W2': _L0_ffn_in['W2'], 'L0_ffn_b2': _L0_ffn_in['b2'], 'L1_attn_ln1_g': _L1_attn_in['ln1_g'], 'L1_attn_ln1_b': _L1_attn_in['ln1_b'], 'L1_attn_Wx': _L1_attn_in['Wx'], 'L1_attn_bx': _L1_attn_in['bx'], 'L1_attn_Wq': _L1_attn_in['Wq'], 'L1_attn_Wk': _L1_attn_in['Wk'], 'L1_attn_Wv': _L1_attn_in['Wv'], 'L1_attn_Wo': _L1_attn_in['Wo'], 'L1_attn_bo': _L1_attn_in['bo'], 'L1_attn_ln2_g': _L1_attn_in['ln2_g'], 'L1_attn_ln2_b': _L1_attn_in['ln2_b'], 'L1_attn_W1': _L1_attn_in['W1'], 'L1_attn_b1': _L1_attn_in['b1'], 'L1_attn_W2': _L1_attn_in['W2'], 'L1_attn_b2': _L1_attn_in['b2'], 'L1_ffn_attention_mask': _L1_ffn_in['attention_mask'], 'L1_ffn_wr': _L1_ffn_in['wr'], 'L1_ffn_br': _L1_ffn_in['br'], 'L1_ffn_w1': _L1_ffn_in['w1'], 'L1_ffn_b1': _L1_ffn_in['b1'], 'L1_ffn_w2': _L1_ffn_in['w2'], 'L1_ffn_b2': _L1_ffn_in['b2']}

def reference(x, L0_tok_W, L0_tok_b, L0_attn_Wq, L0_attn_Wk, L0_attn_Wv, L0_attn_Wo, L0_ffn_Wg, L0_ffn_bg, L0_ffn_W1, L0_ffn_b1, L0_ffn_W2, L0_ffn_b2, L1_attn_ln1_g, L1_attn_ln1_b, L1_attn_Wx, L1_attn_bx, L1_attn_Wq, L1_attn_Wk, L1_attn_Wv, L1_attn_Wo, L1_attn_bo, L1_attn_ln2_g, L1_attn_ln2_b, L1_attn_W1, L1_attn_b1, L1_attn_W2, L1_attn_b2, L1_ffn_attention_mask, L1_ffn_wr, L1_ffn_br, L1_ffn_w1, L1_ffn_b1, L1_ffn_w2, L1_ffn_b2):
    import jax
    import jax.numpy as jnp

    def _L0_tok_ref(x, W, b):
        import jax, jax.numpy as jnp
        import numpy as np
        IMAGE_SIZE = 64
        PATCH = 16
        EMBED_DIM = 64
        IN_CH = 3
        BATCH = 128
        IN_DIM = IN_CH * PATCH * PATCH

        def _patchify(x, p):
            B, C, H, Wd = x.shape
            x = x.reshape(B, C, H // p, p, Wd // p, p)
            x = x.transpose(0, 2, 4, 1, 3, 5)
            return x.reshape(B, H // p * (Wd // p), C * p * p)
        patches = _patchify(x, PATCH)
        return jnp.einsum('bnk,ek->bne', patches, W) + b

    def _L0_attn_ref(x, Wq, Wk, Wv, Wo):
        import jax, jax.numpy as jnp
        import numpy as np
        B, S, C = (8, 256, 64)
        H, KD = (8, 64)
        HEAD_DIM = KD // H
        b, s, c = x.shape
        q = jnp.einsum('bsc,oc->bso', x, Wq).reshape(b, s, H, KD).transpose(0, 2, 1, 3)
        k = jnp.einsum('bsc,oc->bos', x, Wk)
        v_conv = jnp.einsum('bsc,oc->bos', x, Wv)
        v = v_conv.reshape(b, s, KD)
        scale = 1.0 / np.sqrt(HEAD_DIM).astype(np.float32)
        scores = jnp.einsum('bhsd,bdt->bhst', q, k) * scale
        attn = jax.nn.softmax(scores, axis=-1)
        ctx = jnp.einsum('bhst,btd->bhsd', attn, v)
        ctx = ctx.transpose(0, 2, 1, 3).reshape(b, H * KD, s)
        out = jnp.einsum('bcp,oc->bop', ctx, Wo)
        return out.transpose(0, 2, 1)

    def _L0_ffn_ref(x, Wg, bg, W1, b1, W2, b2):
        import jax, jax.numpy as jnp
        import numpy as np
        B, S, D, H, E, K = (8, 2048, 64, 256, 8, 2)
        gate_scores = jnp.einsum('bsd,ed->bse', x, Wg) + bg
        topk_scores, topk_idx = jax.lax.top_k(gate_scores, K)
        topk_probs = jax.nn.softmax(topk_scores, axis=-1)
        combine = jnp.sum(topk_probs[..., None] * jax.nn.one_hot(topk_idx, E, dtype=x.dtype), axis=-2)
        out = jnp.zeros_like(x)
        for e in range(E):
            h = jax.nn.relu(jnp.einsum('bsd,hd->bsh', x, W1[e]) + b1[e])
            y = jnp.einsum('bsh,dh->bsd', h, W2[e]) + b2[e]
            out = out + combine[..., e:e + 1] * y
        return out

    def _L1_attn_ref(x, ln1_g, ln1_b, Wx, bx, Wq, Wk, Wv, Wo, bo, ln2_g, ln2_b, W1, b1, W2, b2):
        import jax, jax.numpy as jnp
        import numpy as np
        B, N, C = (8, 2048, 64)
        HEADS, DH, KR = (8, 32, 4)
        INNER = HEADS * DH
        FF = 4 * C
        EPS = 1e-05

        def layernorm(x, g, b):
            mu = jnp.mean(x, axis=-1, keepdims=True)
            var = jnp.mean((x - mu) ** 2, axis=-1, keepdims=True)
            return (x - mu) * jax.lax.rsqrt(var + EPS) * g + b
        b, n, c = x.shape
        h = layernorm(x, ln1_g, ln1_b)
        xm = h @ Wx + bx
        xm = xm.reshape(b, n, HEADS, DH).transpose(0, 2, 1, 3)
        q = jax.nn.softmax(xm @ Wq, axis=-1)
        k = jax.nn.softmax(xm @ Wk, axis=-2)
        v = xm @ Wv
        kv = jnp.einsum('bhnr,bhnd->bhrd', k, v)
        qkv = jnp.einsum('bhnr,bhrd->bhnd', q, kv)
        attn = qkv.transpose(0, 2, 1, 3).reshape(b, n, INNER) @ Wo + bo
        fx = attn + x
        h2 = layernorm(fx, ln2_g, ln2_b)
        m = jax.nn.gelu(h2 @ W1 + b1, approximate=False) @ W2 + b2
        return m + fx

    def _L1_ffn_ref(x, attention_mask, wr, br, w1, b1, w2, b2):
        import jax, jax.numpy as jnp
        import numpy as np
        B, S, D = (8, 1024, 64)
        H = 4 * D
        CAPACITY = 0.5
        b, s, d = x.shape
        weights = (jnp.einsum('bsd,do->bso', x, wr) + br)[..., 0]
        k = max(1, int(CAPACITY * s))
        kk = k - 1 if k > 1 else 1
        _, idx = jax.lax.top_k(weights, k)
        sel_idx = idx[:, :kk]
        sel = jnp.take_along_axis(x, sel_idx[:, :, None], axis=1)
        h = jax.nn.gelu(jnp.einsum('bkd,dh->bkh', sel, w1) + b1)
        y = jnp.einsum('bkh,hd->bkd', h, w2) + b2
        w_sel = jnp.take_along_axis(weights, sel_idx, axis=1)
        y = y * w_sel[..., None]
        batch_idx = jnp.arange(b)[:, None]
        processed = jnp.zeros_like(x).at[batch_idx, sel_idx].set(y)
        return processed + x
    h = _L0_tok_ref(x, L0_tok_W, L0_tok_b)
    h = h + _L0_attn_ref(_layernorm(h, axis=-1), L0_attn_Wq, L0_attn_Wk, L0_attn_Wv, L0_attn_Wo)
    h = h + _L0_ffn_ref(_layernorm(h, axis=-1), L0_ffn_Wg, L0_ffn_bg, L0_ffn_W1, L0_ffn_b1, L0_ffn_W2, L0_ffn_b2)
    h = h + _L1_attn_ref(_layernorm(h, axis=-1), L1_attn_ln1_g, L1_attn_ln1_b, L1_attn_Wx, L1_attn_bx, L1_attn_Wq, L1_attn_Wk, L1_attn_Wv, L1_attn_Wo, L1_attn_bo, L1_attn_ln2_g, L1_attn_ln2_b, L1_attn_W1, L1_attn_b1, L1_attn_W2, L1_attn_b2)
    h = h + _L1_ffn_ref(_layernorm(h, axis=-1), L1_ffn_attention_mask, L1_ffn_wr, L1_ffn_br, L1_ffn_w1, L1_ffn_b1, L1_ffn_w2, L1_ffn_b2)
    return h

_drawn_inputs = setup_inputs


def setup_inputs(seed=0):
    import zlib

    import numpy as np

    out = dict(_drawn_inputs(seed))
    spreads = {'L1_attn_ln1_g': (1.0, 0.6),
     'L1_attn_ln1_b': (0.0, 0.8),
     'L1_attn_bx': (0.0, 0.8),
     'L1_attn_bo': (0.0, 0.1),
     'L1_attn_ln2_g': (1.0, 0.6),
     'L1_attn_ln2_b': (0.0, 0.8),
     'L1_attn_b1': (0.0, 0.8),
     'L1_attn_b2': (0.0, 0.271),
     'L1_ffn_b1': (0.0, 0.8),
     'L1_ffn_b2': (0.0, 0.8)}
    factors = {'L0_tok_b': 3.109,
     'L0_attn_Wq': 8.0,
     'L0_attn_Wk': 8.0,
     'L0_attn_Wv': 5.346,
     'L0_attn_Wo': 5.285,
     'L0_ffn_b1': 2.752,
     'L1_attn_Wx': 8.0,
     'L1_attn_Wq': 8.0,
     'L1_attn_Wk': 8.0,
     'L1_attn_Wv': 8.0,
     'L1_attn_Wo': 8.0,
     'L1_attn_W1': 4.216,
     'L1_attn_W2': 3.592,
     'L1_ffn_wr': 8.0,
     'L1_ffn_w1': 8.0,
     'L1_ffn_w2': 8.0}
    for name, (base, spread) in spreads.items():
        noise = np.random.default_rng([zlib.crc32(name.encode()), seed]).standard_normal(out[name].shape)
        drawn = base * np.exp(spread * noise) if base else spread * noise
        out[name] = jnp.asarray(drawn.astype(out[name].dtype))
    for name, factor in factors.items():
        out[name] = (out[name] * factor).astype(out[name].dtype)
    return out
```

```python
from contextlib import ExitStack

import numpy as np

import concourse.bass as bass
from concourse import mybir

F32 = mybir.dt.float32
F32R = mybir.dt.float32r
ALU = mybir.AluOpType
ACT = mybir.ActivationFunctionType
AX_X = mybir.AxisListType.X

C = 64
PATCH = 16
SIDE = 14
TOK = SIDE * SIDE
CH = TOK // 2
G = 4
PAIR = 2 * TOK
IMG_ROW = 64
XROWS = IMG_ROW + 48
HEADS = 8
EXPERTS = 8
EP = EXPERTS // 2
HCH = 2 * EXPERTS
LH, LR, LD = 8, 4, 32
KEEP = TOK // 2 - 1
EPS = 1e-5


def at_least(eng, sem, value):
    if isinstance(value, int) and value <= 0:
        return
    eng.wait_ge(sem, value)


def wait_apart(eng, waits, sem, value):
    eng.wait_ge(sem, value)
    if not isinstance(value, int):
        eng.sem_inc(waits, 1)


class Links:

    def __init__(self, eng, sem, j, n):
        self.eng, self.sem, self.base, self.n, self.k = eng, sem, j * n, n, 0

    def mark(self, ins):
        self.k += 1
        ins.then_inc(self.sem, 1)

    def wait(self):
        self.eng.wait_ge(self.sem, self.base + self.k)

    def link(self, ins):
        self.mark(ins)
        self.wait()

    def end(self):
        assert self.k == self.n, (self.k, self.n)


def run_lagged(eng, pairs, depth, body):
    for i in range(depth + 1):
        body(i, lambda lag, i=i: i - lag >= 0)
    with eng.Fori(depth + 1, pairs) as i:
        body(i, lambda lag: True)
    for i in range(pairs, pairs + depth):
        body(i, lambda lag, i=i: i - lag < pairs)


def vit_tower(nc, a, out):
    B = a["x"].shape[0]
    NP = B // 2
    with ExitStack() as ctx:
        def sb(name, shape, dt=F32):
            return ctx.enter_context(nc.sbuf_tensor(name, shape, dt))

        def sem(name):
            return ctx.enter_context(nc.semaphore(name))

        bank = [ctx.enter_context(nc.psum_tensor(f"bank{i}", [128, 512], F32)) for i in range(8)]

        v_dram = nc.dram_tensor("v_scratch", (NP, 2, C, TOK), F32, kind="Internal").ap()
        ctx_dram = nc.dram_tensor("ctx_scratch", (NP, 2, TOK, HEADS * C), F32, kind="Internal").ap()

        ident = sb("ident", [128, 128])
        ident2 = sb("ident2", [128, C])
        pick = sb("pick", [C, EP, 2, C])
        pick_r = sb("pick_r", [C, EP, 2 * C], F32R)
        tie_tok = sb("tie_tok", [CH, 2, TOK])
        tie_exp = sb("tie_exp", [CH, EXPERTS, EXPERTS])
        half = sb("half", [CH, G])
        w_tok = sb("w_tok", [XROWS, PATCH, 2 * C])
        a_hi = sb("a_hi", [128, HEADS * 128], F32R)
        a_lo = sb("a_lo", [128, HEADS * 128], F32R)
        wv_hi, wv_lo = sb("wv_hi", [128, C], F32R), sb("wv_lo", [128, C], F32R)
        wo_t = sb("wo_t", [128, 4, C])
        wg_hi, wg_lo = sb("wg_hi", [128, EXPERTS], F32R), sb("wg_lo", [128, EXPERTS], F32R)
        w1_hi = sb("w1_hi", [128, HCH, 128], F32R)
        w1_lo = sb("w1_lo", [128, HCH, 128], F32R)
        w2_t = sb("w2_t", [128, EP, 2, 128])
        wqk_hi, wqk_lo = sb("wqk_hi", [128, 64], F32R), sb("wqk_lo", [128, 64], F32R)
        wxa = sb("wxa", [128, 2, C + 1])
        wx_dup = sb("wx_dup", [128, 2, 2 * C])
        bdq, bdk = sb("bdq", [128, 2, 32]), sb("bdk", [128, 2, 32])
        bdv = sb("bdv", [128, 128])
        vt = sb("vt", [128, 2, C + 1])
        u_w = sb("u_w", [C + 1, LH, C])
        q_bias = sb("q_bias", [CH, 32])
        k_bias = sb("k_bias", [32, 1])
        m1_hi, m1_lo = sb("m1_hi", [128, 256], F32R), sb("m1_lo", [128, 256], F32R)
        f1_hi, f1_lo = sb("f1_hi", [128, 256], F32R), sb("f1_lo", [128, 256], F32R)
        m1_s = sb("m1_s", [128, 256])
        m1_bias = sb("m1_bias", [128, 2])
        wr_hi, wr_lo = sb("wr_hi", [128, CH], F32R), sb("wr_lo", [128, CH], F32R)
        m2_w, f2_w = sb("m2_w", [128, 2, C]), sb("f2_w", [128, 2, C])
        tok_b = sb("tok_b", [128, 1])
        g1_dup, g2_dup = sb("g1_dup", [128, 1]), sb("g2_dup", [128, 1])
        g1_aug = sb("g1_aug", [C + 1, 1])
        ln1b, ln2b = sb("ln1b", [C, 1]), sb("ln2b", [C, 1])
        bx_c = sb("bx_c", [128, 2])
        mb1_c, fb1_c = sb("mb1_c", [128, 2]), sb("fb1_c", [128, 2])
        b1_c = sb("b1_c", [128, HCH])
        b2_c = sb("b2_c", [128, EP])
        bg_b = sb("bg_b", [CH, EXPERTS])
        bo_b, mb2_b, fb2_b = sb("bo_b", [CH, C]), sb("mb2_b", [CH, C]), sb("fb2_b", [CH, C])
        br_b = sb("br_b", [CH, 1])
        wk_dup = sb("wk_dup", [C, 128])
        wv_n, wg_n = sb("wv_n", [C, 2 * C]), sb("wg_n", [EXPERTS, 2 * C])
        wx_n = sb("wx_n", [C, 256])
        wo1_n = sb("wo1_n", [128, 2, C])
        q1_n, k1_n, v1_n = sb("q1_n", [128, LR]), sb("k1_n", [128, LR]), sb("v1_n", [128, LD])
        m1_n, f1_n = sb("m1_n", [128, 256]), sb("f1_n", [128, 256])
        wr_n = sb("wr_n", [128, 1])

        h = sb("h", [CH, NP, G, C])

        x_sb = sb("x_sb", [XROWS, SIDE, SIDE * PATCH])
        h_t = sb("h_t", [128, TOK])
        NORMS = "am3456"
        st = {n: sb(f"st_{n}", [CH, G, 6]) for n in NORMS}
        mv = {n: sb(f"mv_{n}", [CH, G, 2]) for n in NORMS}
        ve = {n: sb(f"ve_{n}", [CH, G]) for n in NORMS}
        rstd = {n: sb(f"rstd_{n}", [CH, G]) for n in NORMS}
        y_a = sb("y_a", [CH, G, 2, C])
        x_a = sb("x_a", [128, PAIR], F32R)
        v_lin = sb("v_lin", [C, 2, TOK])
        v_tok = sb("v_tok", [CH, 2, 2, C])
        g_hi = [sb(f"g_hi{m}", [128, HEADS, TOK], F32R) for m in range(2)]
        g_lo = [sb(f"g_lo{m}", [128, HEADS, TOK], F32R) for m in range(2)]
        nmax = [sb(f"nmax{c}", [CH, HEADS]) for c in range(2)]
        psum_ = [sb(f"psums{c}", [CH, HEADS]) for c in range(2)]
        rsum = [sb(f"rsum{c}", [CH, HEADS]) for c in range(2)]
        prob = [sb(f"prob{c}", [128, HEADS * TOK]) for c in range(2)]
        prob_t = [sb(f"prob_t{c}", [128, 2 * HEADS * CH]) for c in range(2)]
        ctx_sb = [sb(f"ctx_sb{c}", [CH, HEADS * C]) for c in range(2)]
        ctx_r = [sb(f"ctx_r{m}", [128, 4, TOK]) for m in range(2)]
        hid = sb("hid", [128, 2, 4, PAIR])
        w1_n = hid[:, :, :, :].rearrange("p a b t -> p (a b t)")[:, 0:HCH * 2 * C].rearrange("p (q c) -> p q c", q=HCH)
        w2_n = prob_t[1][:, 0:EP * 256].rearrange("p (q n) -> p q n", q=EP)
        wtok_n = prob[0][0:C, 0:3 * PATCH * PATCH]
        wq_n = prob[1][0:C, 0:2 * HEADS * C].rearrange("p (n c) -> p n c", n=HEADS)
        wo_n = prob_t[0][0:C, 0:512]

        gs = sb("gs", [CH, G, EXPERTS])
        above = sb("above", [CH, G, EXPERTS, EXPERTS])
        tied = sb("tied", [CH, G, EXPERTS, EXPERTS])
        rank_e = sb("rank_e", [CH, G, EXPERTS])
        gmax = sb("gmax", [CH, G])
        gexp = sb("gexp", [CH, G, EXPERTS])
        gsum = sb("gsum", [CH, G])
        comb = sb("comb", [CH, G, EXPERTS])
        comb2 = sb("comb2", [CH, G, C])
        comb_t = sb("comb_t", [C, PAIR], F32R)
        comb_b = prob[0][:, :].rearrange("p (q t) -> p q t", q=EP)
        prod = prob[1][:, :].rearrange("p (q t) -> p q t", q=EP)
        x_parts = g_lo[1][:, :, :].rearrange("p n t -> p (n t)")
        x_m, x_l1, x_l2, x_l3 = (x_parts[:, k * PAIR:(k + 1) * PAIR] for k in range(4))
        turned = prob_t[0][0:CH, 0:3 * G * 2 * C].rearrange("p (k g d c) -> p k g d c", k=3, g=G, d=2)
        y_m, y_2, x4 = (turned[:, k] for k in range(3))
        tie_w = prob_t[1][0:CH, 0:G * TOK].rearrange("p (g t) -> p g t", g=G)
        w_b = prob_t[1][0:CH, G * TOK:G * TOK + PAIR]
        base3 = prob_t[1][0:CH, G * TOK + PAIR:G * TOK + PAIR + G * C].rearrange("p (g c) -> p g c", g=G)
        fx, h4, o_t, o_sb = (ctx_sb[k // 2][:, :].rearrange("p (k g c) -> p k g c", k=2, g=G)[:, k % 2] for k in range(4))
        hid2, hid3 = (ctx_r[m][:, :, :].rearrange("p (k m) t -> p k (m t)", k=2) for m in range(2))
        x3 = sb("x3", [CH, G, C])
        x3b = sb("x3b", [CH, G, C])
        n3 = sb("n3", [CH, G, 2 * C + 1])
        kl = sb("kl", [32, 2, TOK])
        kmax, ksum, krec = sb("kmax", [32, 2]), sb("ksum", [32, 2]), sb("krec", [32, 2])
        k_t = sb("k_t", [CH, G, 32])
        ql = sb("ql", [CH, G * LH, LR])
        qmax = sb("qmax", [CH, G * LH])
        q_t = sb("q_t", [C, 2, CH])
        kx = sb("kx", [C + 1, 2, 32])
        m_t = sb("m_t", [C, 2, LH, LR])
        m_bd = sb("m_bd", [C, 2, C])
        base2 = sb("base2", [CH, G, C])
        w_i = sb("w_i", [CH, G])
        rank_w = sb("rank_w", [CH, G])
        w_sel = sb("w_sel", [CH, G])

        S = {}

        def sems(names):
            for n in names.split():
                S[n] = sem(n)

        sems("w_loaded consts_ready zeroed setup_mm setup_done setup_link")
        for n in NORMS:
            sems(f"ln_{n} pow_{n}")
        sems("x_loaded tok_ready tok_stored h0_ready h0_stored xt_ready xt_hi xt_split v_ready v_stored "
             "v_written v_ld0 v_ld1 g_ready g_hi_ready g_split scores_ready max_ready exp_done pt_ready pt_dve pt_act "
             "pv_ready ctx_norm ctx_wr0 ctx_wr1 ctx_ld0 ctx_ld1 wo_ready wo_added recip_done")
        sems("sp_waits pe_waits dve_waits")
        sems("xm_t xm_hi xm_split gate_ready gate_link gate_exp comb_ready comb_stored cb_ready cb_stored ff1_ready "
             "relu_act relu_dve ff2_ready prod_done prod_sum moe_ready moe_added")
        sems("l1_xt l1_hi l1_split l1_k l1_kb l1_klink l1_kexp l1_kt l1_kts l1_q l1_qlink l1_qexp "
             "l1_qts l1_g l1_gs l1_m l1_ms l1_mt l1_mts l1_attn l1_fx l1_x3b l1_zero")
        sems("l2_xt l2_hi l2_split l2_ff l2_gelu l2_out l2_h4 l2_base")
        sems("l3_xt l3_hi l3_split l3_w l3_wb l3_wi l3_wis l3_rank l3_ff l3_gelu l3_out l3_t l3_mul l3_fin l3_base "
             "l3_stored")
        v_ld = (S["v_ld0"], S["v_ld1"])
        ctx_wr, ctx_ld = (S["ctx_wr0"], S["ctx_wr1"]), (S["ctx_ld0"], S["ctx_ld1"])

        GATE_LINKS, KLINKS, QLINKS = 14, 3, 6

        SETUP = ["tok0", "tok1", "a0", "a1", "wv", "wo", "wg", "w1_0", "w1_1", "w1_2", "w1_3", "w2_0", "w2_1",
                 "wx", "bfull", "wqk", "qb", "kb", "vt", "u0", "u1", "u2", "u3", "b1m"]
        idx = {n: k for k, n in enumerate(SETUP)}

        def sbank(name):
            return bank[idx[name] % 8]

        def g_cols(g):
            c, m = g // 2, g % 2
            return slice(m * TOK + c * CH, m * TOK + (c + 1) * CH)

        def weight_loads():
            col = lambda v: v.rearrange("(p a) -> p a", a=1)
            L = []
            L.append((wtok_n, a["L0_tok_W"]))
            for k in range(2):
                w = slice(k * C, (k + 1) * C)
                L.append((wq_n[:, :, w], a["L0_attn_Wq"].rearrange("(n o) c -> o n c", n=HEADS)))
                L.append((wv_n[:, w], a["L0_attn_Wv"]))
                L.append((wg_n[:, w], a["L0_ffn_Wg"]))
                L.append((w1_n[:, :, w], a["L0_ffn_W1"].rearrange("e (k p) c -> p (e k) c", k=2)))
                L.append((wk_dup[:, k * C:(k + 1) * C], a["L0_attn_Wk"]))
                L.append((tok_b[k * C:(k + 1) * C, :], col(a["L0_tok_b"])))
                L.append((g1_dup[k * C:(k + 1) * C, :], col(a["L1_attn_ln1_g"])))
                L.append((g2_dup[k * C:(k + 1) * C, :], col(a["L1_attn_ln2_g"])))
                L.append((m1_n[k * C:(k + 1) * C, :], a["L1_attn_W1"]))
                L.append((f1_n[k * C:(k + 1) * C, :], a["L1_ffn_w1"]))
                L.append((wr_n[k * C:(k + 1) * C, :], a["L1_ffn_wr"]))
            L.append((wo_n, a["L0_attn_Wo"]))
            L.append((w2_n, a["L0_ffn_W2"].rearrange("(q r) d n -> (r d) q n", r=2)))
            L.append((b1_c[:, :], a["L0_ffn_b1"].rearrange("e (k p) -> p (e k)", k=2)))
            L.append((b2_c[:, :], a["L0_ffn_b2"].rearrange("(q r) d -> (r d) q", r=2)))
            L.append((bg_b[:, :], a["L0_ffn_bg"].partition_broadcast(CH)))
            L.append((wx_n[:, :], a["L1_attn_Wx"]))
            L.append((bx_c[:, :], a["L1_attn_bx"].rearrange("(k p) -> p k", k=2)))
            L.append((g1_aug[0:C, :], col(a["L1_attn_ln1_g"])))
            L.append((ln1b[:, :], col(a["L1_attn_ln1_b"])))
            L.append((ln2b[:, :], col(a["L1_attn_ln2_b"])))
            for i in range(4):
                r = slice(LD * i, LD * (i + 1))
                L.append((q1_n[r, :], a["L1_attn_Wq"]))
                L.append((k1_n[r, :], a["L1_attn_Wk"]))
                L.append((v1_n[r, :], a["L1_attn_Wv"]))
            L.append((wo1_n[:, :, :], a["L1_attn_Wo"].rearrange("(k p) o -> p k o", k=2)))
            L.append((bo_b[:, :], a["L1_attn_bo"].partition_broadcast(CH)))
            L.append((mb1_c[:, :], a["L1_attn_b1"].rearrange("(k p) -> p k", k=2)))
            L.append((m2_w[:, :, :], a["L1_attn_W2"].rearrange("(k p) o -> p k o", k=2)))
            L.append((mb2_b[:, :], a["L1_attn_b2"].partition_broadcast(CH)))
            L.append((fb1_c[:, :], a["L1_ffn_b1"].rearrange("(k p) -> p k", k=2)))
            L.append((f2_w[:, :, :], a["L1_ffn_w2"].rearrange("(k p) o -> p k o", k=2)))
            L.append((fb2_b[:, :], a["L1_ffn_b2"].partition_broadcast(CH)))
            L.append((br_b[:, :], a["L1_ffn_br"].partition_broadcast(CH)))
            return L

        N_LOADS = len(weight_loads())
        block = ctx.enter_context(nc.Block())

        @block.sync
        def _(sp):
            with nc.allow_non_contiguous_dma(reason="bias vectors, a few kB in all"):
                for dst, src in weight_loads()[0::2]:
                    sp.dma_start(dst, src).then_inc(S["w_loaded"], 16)
            sp.wait_ge(S["zeroed"], 1)

            def load_x(j):
                at_least(sp, S["tok_ready"], j)
                for m in range(2):
                    for ch in range(3):
                        p = IMG_ROW * m + PATCH * ch
                        src = a["x"].rearrange("(j m) c (r q) w -> j m c q r w", m=2, q=PATCH)[j, m, ch]
                        sp.dma_start(x_sb[p:p + PATCH, :, :], src).then_inc(S["x_loaded"], 16)

            def write_ctx(j, u):
                m, c = u // 2, u % 2
                at_least(sp, S["ctx_norm"], 4 * j + u + 1)
                sp.dma_start(ctx_dram[j, m, c * CH:(c + 1) * CH, :], ctx_sb[c][:, :]).then_inc(ctx_wr[c], 16)

            def read_ctx(j, m):
                for c in range(2):
                    sp.wait_ge(ctx_wr[c], 16 * (2 * j + m + 1))
                at_least(sp, S["wo_ready"], j)
                src = ctx_dram[j, m].rearrange("s n -> (s n)").rearrange("(k p t) -> p k t", k=4, t=TOK)
                sp.dma_start(ctx_r[m][:, :, :], src).then_inc(ctx_ld[m], 16)

            def write_v(j):
                sp.wait_ge(S["v_stored"], j + 1)
                sp.dma_start(v_dram[j].rearrange("m o s -> o m s"), v_lin[:, :, :]).then_inc(S["v_written"], 16)

            def read_v(j, m):
                wait_apart(sp, S["sp_waits"], S["v_written"], 16 * (j + 1))
                at_least(sp, S["pv_ready"], 4 * j - 2 + 2 * m)
                src = v_dram[j, m].rearrange("o s -> (o s)").rearrange("(k p d) -> p k d", k=2, d=C)
                sp.dma_start(v_tok[:, m, :, :], src).then_inc(v_ld[m], 16)

            def body(i, live):
                if live(1):
                    read_v(i - 1, 0)
                if live(2):
                    write_ctx(i - 2, 3)
                    read_ctx(i - 2, 1)
                if live(1):
                    read_v(i - 1, 1)
                if live(-1):
                    load_x(i + 1)
                if live(1):
                    write_ctx(i - 1, 0)
                    write_ctx(i - 1, 1)
                if live(0):
                    write_v(i)
                if live(1):
                    write_ctx(i - 1, 2)
                    read_ctx(i - 1, 0)

            load_x(0)
            for i in range(3):
                body(i, lambda lag, i=i: i - lag >= 0)
            with sp.Fori(3, NP - 1) as i:
                body(i, lambda lag: True)
            for i in range(NP - 1, NP + 2):
                body(i, lambda lag, i=i: i - lag < NP)

            with sp.Fori(0, NP) as j:
                sp.wait_ge(S["l3_fin"], j + 1)
                for c in range(2):
                    dst = out.rearrange("(j m) (c p) d -> j c p m d", m=2, c=2)[j, c]
                    sp.dma_start(dst, o_sb[:, 2 * c:2 * c + 2, :]).then_inc(S["l3_stored"], 16)
            sp.wait_ge(S["l3_stored"], 32 * NP)

        @block.gpsimd
        def _(pool):
            k = 0
            for t, v in ((ident, 0.0), (ident2, 0.0), (tie_tok, 1.0), (tie_exp, 1.0), (half, -0.5), (pick, 0.0)):
                nc.gpsimd.memset(t[:], v).then_inc(S["consts_ready"], 1)
                k += 1
            pool.wait_ge(S["consts_ready"], k)
            nc.gpsimd.affine_select(out=ident[:], in_=ident[:], compare_op=ALU.not_equal, fill=1.0, base=0,
                                    pattern=[[-1, 128]], channel_multiplier=1).then_inc(S["consts_ready"], 1)
            nc.gpsimd.affine_select(out=tie_tok[:], in_=tie_tok[:], compare_op=ALU.is_gt, fill=0.0, base=0,
                                    pattern=[[CH, 2], [-1, TOK]], channel_multiplier=1).then_inc(S["consts_ready"], 1)
            nc.gpsimd.affine_select(out=tie_exp[:], in_=tie_exp[:], compare_op=ALU.is_gt, fill=0.0, base=0,
                                    pattern=[[1, 8], [-1, 8]], channel_multiplier=0).then_inc(S["consts_ready"], 1)
            for k, base in ((9, 0), (11, -C)):
                pool.wait_ge(S["consts_ready"], k)
                nc.gpsimd.affine_select(out=pick[:], in_=pick[:], compare_op=ALU.not_equal, fill=1.0,
                                        base=base // 2, pattern=[[-2, EP], [-1, 2], [0, C]],
                                        channel_multiplier=1).then_inc(S["consts_ready"], 1)
                nc.gpsimd.affine_select(out=ident2[:], in_=ident2[:], compare_op=ALU.not_equal, fill=1.0, base=base,
                                        pattern=[[-1, C]], channel_multiplier=1).then_inc(S["consts_ready"], 1)

            def rstd_pow(n, j):
                pool.wait_ge(S[f"ln_{n}"], 4 * j + 3)
                nc.gpsimd.tensor_tensor(rstd[n][:, :], ve[n][:, :], half[:, :], ALU.pow).then_inc(S[f"pow_{n}"], 1)

            pool.wait_ge(S["consts_ready"], 13)
            with pool.Fori(0, NP) as j:
                rstd_pow("a", j)

            def sum_experts(j):
                for ep in range(1, EP):
                    pool.wait_ge(S["prod_done"], EP * j + ep + 1)
                    if ep > 1:
                        pool.wait_ge(S["prod_sum"], 3 * j + ep - 1)
                    nc.gpsimd.tensor_tensor(prod[:, 0, :], prod[:, 0, :], prod[:, ep, :],
                                            ALU.add).then_inc(S["prod_sum"], 1)

            def base_mlp(j):
                pool.wait_ge(S["l1_fx"], j + 1)
                at_least(pool, S["l2_h4"], j)
                nc.gpsimd.tensor_tensor(base2[:, :, :], h[:, j], fx[:, :, :], ALU.add).then_inc(S["l2_base"], 1)
                pool.wait_ge(S["l2_base"], 2 * j + 1)
                nc.gpsimd.tensor_tensor(base2[:, :, :], base2[:, :, :],
                                        mb2_b[:, :].unsqueeze(1).to_broadcast([CH, G, C]),
                                        ALU.add).then_inc(S["l2_base"], 1)

            def base_ffn(j):
                pool.wait_ge(S["ln_6"], 4 * j + 4)
                at_least(pool, S["l3_fin"], j)
                nc.gpsimd.tensor_tensor(base3[:, :, :], x4[:, :, 0, :], h4[:, :, :], ALU.add).then_inc(S["l3_base"], 1)

            def base_attn(j):
                pool.wait_ge(S["ln_3"], 4 * j + 4)
                at_least(pool, S["l1_fx"], j)
                nc.gpsimd.tensor_tensor(x3b[:, :, :], x3[:, :, :],
                                        bo_b[:, :].unsqueeze(1).to_broadcast([CH, G, C]),
                                        ALU.add).then_inc(S["l1_x3b"], 1)

            def route(j):
                pool.wait_ge(S["l3_t"], j + 1)
                pool.wait_ge(S["l3_rank"], 9 * j + 9)
                nc.gpsimd.tensor_tensor(o_t[:, :, :], o_t[:, :, :],
                                        w_sel[:, :].unsqueeze(2).to_broadcast([CH, G, C]),
                                        ALU.mult).then_inc(S["l3_mul"], 1)

            def body(i, live):
                if live(0):
                    rstd_pow("m", i)
                if live(1):
                    sum_experts(i - 1)
                if live(3):
                    rstd_pow("6", i - 3)
                if live(4):
                    route(i - 4)
                if live(2):
                    rstd_pow("5", i - 2)
                if live(1):
                    rstd_pow("3", i - 1)
                if live(3):
                    base_ffn(i - 3)
                if live(2):
                    base_mlp(i - 2)
                if live(1):
                    rstd_pow("4", i - 1)
                    base_attn(i - 1)

            run_lagged(pool, NP, 4, body)

        @block.tensor
        def _(pe):
            pe.wait_ge(S["w_loaded"], 16 * N_LOADS)
            pe.wait_ge(S["consts_ready"], 13)

            def begin(name, *needs):
                at_least(pe, S["setup_done"], idx[name] - 7)
                for n in needs:
                    pe.wait_ge(S["setup_done"], idx[n] + 1)

            def done(ins):
                ins.then_inc(S["setup_mm"], 1)

            def mm(o, l, r, start=True, stop=True):
                return nc.tensor.matmul(o, l, r, start=start, stop=stop)

            def flat(t):
                return t[:, :, :, :].rearrange("p g k c -> p g (k c)")

            w_view = wtok_n.rearrange("e (k q) -> e q k", q=PATCH)
            for b in range(2):
                begin(f"tok{b}")
                o = sbank(f"tok{b}")[0:48, :].rearrange("p (q e) -> p q e", e=C)
                for q in range(8):
                    last = nc.tensor.transpose(o[:, q, :], w_view[:, 8 * b + q, :], ident[0:C, 0:C])
                done(last)
            for b in range(2):
                begin(f"a{b}")
                for k in range(4):
                    last = mm(sbank(f"a{b}")[:, k * 128:(k + 1) * 128], wq_n[:, 4 * b + k, :], wk_dup[:, :])
                done(last)
            begin("wv")
            done(nc.tensor.transpose(sbank("wv")[:, 0:C], wv_n[:, :], ident[0:C, 0:C]))
            begin("wo")
            for k in range(4):
                last = nc.tensor.transpose(sbank("wo")[:, k * C:(k + 1) * C], wo_n[:, k * 128:(k + 1) * 128],
                                           ident[0:C, 0:C])
            done(last)
            begin("wg")
            done(nc.tensor.transpose(sbank("wg")[:, 0:EXPERTS], wg_n[:, :], ident[0:EXPERTS, 0:EXPERTS]))
            for b in range(4):
                begin(f"w1_{b}")
                for k in range(4):
                    last = nc.tensor.transpose(sbank(f"w1_{b}")[:, k * 128:(k + 1) * 128],
                                               w1_n[:, 4 * b + k, :], ident[:, :])
                done(last)
            for b in range(2):
                begin(f"w2_{b}")
                for k in range(4):
                    ep, hc = 2 * b + k // 2, k % 2
                    last = nc.tensor.transpose(sbank(f"w2_{b}")[:, k * 128:(k + 1) * 128],
                                               w2_n[:, ep, hc * 128:(hc + 1) * 128], ident[:, :])
                done(last)
            begin("wx")
            for k in range(2):
                last = nc.tensor.transpose(sbank("wx")[:, k * C:(k + 1) * C], wx_n[:, k * 128:(k + 1) * 128],
                                           ident[0:C, 0:C])
            done(last)
            begin("bfull")
            for k in range(2):
                last = mm(sbank("bfull")[:, k:k + 1], wx_n[:, k * 128:(k + 1) * 128], ln1b[:, :])
            done(last)
            begin("wqk", "wx", "bfull")
            for t, bd in enumerate((bdq, bdk)):
                for k in range(2):
                    last = mm(sbank("wqk")[:, t * 32:(t + 1) * 32], wx_dup[:, k, :], bd[:, k, :],
                              start=(k == 0), stop=(k == 1))
            done(last)
            begin("qb")
            for k in range(2):
                last = mm(sbank("qb")[0:CH, 0:32], wxa[:, k, C:C + 1].to_broadcast([128, CH]), bdq[:, k, :],
                          start=(k == 0), stop=(k == 1))
            done(last)
            begin("kb")
            for k in range(2):
                last = mm(sbank("kb")[0:32, 0:1], bdk[:, k, :], wxa[:, k, C:C + 1], start=(k == 0), stop=(k == 1))
            done(last)
            begin("vt")
            for k in range(2):
                last = mm(sbank("vt")[:, k * (C + 1):(k + 1) * (C + 1)], bdv[:, :], wxa[:, k, :])
            done(last)
            for i in range(4):
                begin(f"u{i}", "vt")
                r = slice(LD * i, LD * (i + 1))
                for k in range(2):
                    last = mm(sbank(f"u{i}")[0:C + 1, k * C:(k + 1) * C], vt[r, k, :], wo1_n[r, k, :])
                done(last)
            begin("b1m")
            for k in range(2):
                last = mm(sbank("b1m")[:, k:k + 1], m1_n[0:C, k * 128:(k + 1) * 128], ln2b[:, :])
            done(last)
            pe.wait_ge(S["setup_done"], len(SETUP) + 1)

            def mm2(o, hi, lo, x):
                mm(o, hi, x, start=True, stop=False)
                return mm(o, lo, x, start=False, stop=True)

            def tok_part(j, q0, q1):
                if q0 == 0:
                    pe.wait_ge(S["x_loaded"], 96 * (j + 1))
                    at_least(pe, S["xt_split"], j)
                for q in range(q0, q1):
                    last = mm(bank[0][:, 0:TOK], w_tok[:, q, :], x_sb[:, :, q::PATCH],
                              start=(q == 0), stop=(q == PATCH - 1))
                if q1 == PATCH:
                    last.then_inc(S["tok_ready"], 1)

            def h0_turn(j):
                pe.wait_ge(S["tok_stored"], j + 1)
                for c in range(2):
                    last = nc.tensor.transpose(bank[0][0:CH, 256 + c * 128:256 + (c + 1) * 128],
                                               h_t[:, c * CH:(c + 1) * CH], ident[:, :])
                last.then_inc(S["h0_ready"], 1)

            def turn_norm(y, o, ln, j, ready):
                pe.wait_ge(S[ln], 4 * j + 4)
                for g in range(G):
                    last = nc.tensor.transpose(o[:, g_cols(g)], y[:, g, 0:2 * C], ident[0:CH, 0:CH])
                last.then_inc(S[ready], 1)

            def v_mm(j):
                pe.wait_ge(S["xt_split"], j + 1)
                at_least(pe, S["g_split"], 8 * j - 1)
                mm2(bank[2][0:C, 0:PAIR], wv_hi[:, :], wv_lo[:, :], x_a[:, :]).then_inc(S["v_ready"], 1)

            def g_mm(j, s):
                m, k = s // 4, s % 4
                if s == 0:
                    pe.wait_ge(S["v_stored"], j + 1)
                else:
                    at_least(pe, S["g_split"], 8 * j + s - 1)
                for n in (2 * k, 2 * k + 1):
                    w = slice(n * 128, (n + 1) * 128)
                    last = mm2(bank[2 + s % 2][:, (n % 2) * TOK:(n % 2 + 1) * TOK], a_hi[:, w], a_lo[:, w],
                               x_a[:, m * TOK:(m + 1) * TOK])
                last.then_inc(S["g_ready"], 1)

            def scores(j, u, k):
                m, c, s = u // 2, u % 2, 4 * u + k
                pe.wait_ge(S["g_split"], 8 * j + 4 * m + k + 1)
                at_least(pe, S["exp_done"], 16 * j + s - 1)
                if s == 0:
                    at_least(pe, S["wo_added"], j - 1)
                for n in (2 * k, 2 * k + 1):
                    r = slice(c * CH, (c + 1) * CH)
                    last = mm2(bank[4 + s % 2][0:CH, (n % 2) * TOK:(n % 2 + 1) * TOK], g_hi[m][:, n, r],
                               g_lo[m][:, n, r], x_a[:, m * TOK:(m + 1) * TOK])
                last.then_inc(S["scores_ready"], 1)

            PT_BANK = (1, 6)

            def turn_probs(j, u, k):
                c, tc, hh = u % 2, k % 2, k // 2
                t = 4 * u + k
                if k == 0:
                    pe.wait_ge(S["exp_done"], 16 * j + 4 * u + 4)
                at_least(pe, S["pt_act" if t % 2 else "pt_dve"], 8 * j + t // 2)
                p = prob[c][0:CH, :].rearrange("p (n t) -> p n t", n=HEADS)
                for q in range(4):
                    last = nc.tensor.transpose(bank[PT_BANK[t % 2]][0:CH, q * CH:(q + 1) * CH],
                                               p[:, 4 * hh + q, tc * CH:(tc + 1) * CH], ident[0:CH, 0:CH])
                last.then_inc(S["pt_ready"], 1)

            def weigh_v(j, u, k):
                m, c = u // 2, u % 2
                if k == 0:
                    pe.wait_ge(v_ld[m], 16 * (j + 1))
                    at_least(pe, S["ctx_norm"], 4 * j + u)
                if k % 2 == 0:
                    pe.wait_ge(S["pt_dve"], 8 * j + 2 * u + k // 2 + 1)
                    pe.wait_ge(S["pt_act"], 8 * j + 2 * u + k // 2 + 1)
                pt = prob_t[c][0:CH, :].rearrange("p (k n s) -> p k n s", k=2, n=HEADS)
                for n in (2 * k, 2 * k + 1):
                    for tc in range(2):
                        last = mm(bank[7][0:CH, n * C:(n + 1) * C], pt[:, tc, n, :], v_tok[:, m, tc, :],
                                  start=(tc == 0), stop=(tc == 1))
                if k == 3:
                    last.then_inc(S["pv_ready"], 1)

            def out_proj(j, g):
                c, m = g // 2, g % 2
                if g == 0:
                    for mm_ in range(2):
                        pe.wait_ge(ctx_ld[mm_], 16 * (j + 1))
                    pe.wait_ge(S["exp_done"], min(16 * j + 31, 16 * NP) if isinstance(j, int) else 16 * j + 31)
                for k in range(4):
                    last = mm(bank[4][0:CH, g * C:(g + 1) * C], ctx_r[m][:, k, c * CH:(c + 1) * CH], wo_t[:, k, :],
                              start=(k == 0), stop=(k == 3))
                if g == G - 1:
                    last.then_inc(S["wo_ready"], 1)

            def body1(i, live):
                a, o = i - 1, i - 2

                def steps(order, u):
                    for op, k in order:
                        if op == "S" and live(1):
                            scores(a, u, k)
                        elif op == "T" and live(1):
                            turn_probs(a, u - 1, k)
                        elif op == "W" and live(1):
                            weigh_v(a, u - 2, k)
                        elif op == "L" and live(2):
                            weigh_v(o, 3, k)
                        elif op == "P" and live(0):
                            tok_part(i, 2 * k, 2 * k + 2)
                        elif op == "H" and live(0):
                            h0_turn(i)
                        elif op == "N" and live(0):
                            turn_norm(flat(y_a), bank[0], "ln_a", i, "xt_ready")
                        elif op == "V" and live(0):
                            v_mm(i)
                        elif op == "G" and live(0):
                            g_mm(i, k)
                        elif op == "O" and live(2):
                            out_proj(o, k)

                steps([("S", 0), ("P", 0), ("L", 0), ("S", 1), ("P", 1), ("L", 1), ("S", 2), ("P", 2), ("L", 2),
                       ("S", 3), ("P", 3), ("L", 3)], 0)
                steps([("S", 0), ("P", 4), ("S", 1), ("P", 5), ("T", 0), ("S", 2), ("T", 1), ("P", 6), ("S", 3),
                       ("T", 2), ("P", 7), ("T", 3)], 1)
                steps([("S", 0), ("H", 0), ("W", 0), ("S", 1), ("W", 1), ("T", 0), ("S", 2), ("T", 1), ("W", 2),
                       ("S", 3), ("T", 2), ("W", 3), ("T", 3)], 2)
                steps([("S", 0), ("W", 0), ("S", 1), ("W", 1), ("T", 0), ("S", 2), ("T", 1), ("W", 2),
                       ("S", 3), ("T", 2), ("W", 3), ("T", 3)], 3)
                steps([("N", 0), ("W", 0), ("W", 1), ("T", 0), ("T", 1), ("V", 0), ("G", 0), ("W", 2), ("G", 1),
                       ("T", 2), ("W", 3), ("G", 2), ("O", 0), ("G", 3), ("T", 3), ("G", 4), ("O", 1), ("G", 5),
                       ("O", 2), ("G", 6), ("O", 3), ("G", 7)], 4)

            run_lagged(pe, NP, 2, body1)

            def gate_mm(j):
                pe.wait_ge(S["xm_split"], j + 1)
                at_least(pe, S["moe_added"], j)
                for g in range(G):
                    o = bank[4][0:CH, PAIR + g * EXPERTS:PAIR + (g + 1) * EXPERTS]
                    mm(o, x_m[:, g_cols(g)], wg_hi[:, :], start=True, stop=False)
                    last = mm(o, x_m[:, g_cols(g)], wg_lo[:, :], start=False, stop=True)
                last.then_inc(S["gate_ready"], 1)

            def turn_gate(j):
                at_least(pe, S["moe_added"], j)
                wait_apart(pe, S["pe_waits"], S["gate_link"], GATE_LINKS * (j + 1))
                for g in range(G):
                    last = nc.tensor.transpose(bank[4][0:C, g_cols(g)], comb2[:, g, :], ident[0:CH, 0:CH])
                last.then_inc(S["comb_ready"], 1)

            def spread_gate(j, ep):
                if ep == 0:
                    pe.wait_ge(S["comb_stored"], j + 1)
                else:
                    pe.wait_ge(S["cb_stored"], EP * j + ep)
                mm(bank[4][:, 0:PAIR], pick_r[:, ep, :], comb_t[:, :]).then_inc(S["cb_ready"], 1)

            def ff1(j, ep, r):
                for hc in range(2):
                    q = 4 * ep + 2 * r + hc
                    if ep == 0 and r == 0 and hc == 0:
                        pe.wait_ge(S["xm_split"], j + 1)
                    at_least(pe, S["relu_dve" if q % 2 else "relu_act"], 8 * j + q // 2)
                    mm2(bank[q % 2][:, 0:PAIR], w1_hi[:, q, :], w1_lo[:, q, :], x_m[:, :]).then_inc(S["ff1_ready"], 1)

            def ff2(j, ep):
                pe.wait_ge(S["relu_act"], 8 * j + 2 * ep + 2)
                pe.wait_ge(S["relu_dve"], 8 * j + 2 * ep + 2)
                at_least(pe, S["prod_done"], EP * j + ep - 1)
                for hc in range(2):
                    for r in range(2):
                        last = mm(bank[2 + ep % 2][r * C:(r + 1) * C, 0:PAIR], w2_t[:, ep, hc, r * C:(r + 1) * C],
                                  hid[:, ep % 2, 2 * r + hc, :], start=(hc == 0), stop=(hc == 1))
                last.then_inc(S["ff2_ready"], 1)

            def moe_out(j, more):
                if more:
                    pe.wait_ge(S["xm_split"], j + 2)
                pe.wait_ge(S["prod_sum"], 3 * j + 3)
                for g in range(G):
                    last = mm(bank[4][0:CH, g * C:(g + 1) * C], prod[:, 0, g_cols(g)], ident2[:, :])
                last.then_inc(S["moe_ready"], 1)

            def l1_k(j):
                pe.wait_ge(S["l1_split"], j + 1)
                mm2(bank[5][0:32, 0:PAIR], wqk_hi[:, 32:64], wqk_lo[:, 32:64], x_l1[:, :]).then_inc(S["l1_k"], 1)

            def l1_q(j):
                pe.wait_ge(S["l1_kb"], j + 1)
                for g in range(G):
                    o = bank[5][0:CH, g * 32:(g + 1) * 32]
                    mm(o, x_l1[:, g_cols(g)], wqk_hi[:, 0:32], start=True, stop=False)
                    last = mm(o, x_l1[:, g_cols(g)], wqk_lo[:, 0:32], start=False, stop=True)
                last.then_inc(S["l1_q"], 1)

            def l1_kt(j):
                wait_apart(pe, S["pe_waits"], S["l1_klink"], KLINKS * (j + 1))
                for g in range(G):
                    c, m = g // 2, g % 2
                    last = nc.tensor.transpose(bank[5][0:CH, 128 + g * 32:128 + (g + 1) * 32],
                                               kl[:, m, c * CH:(c + 1) * CH], ident[0:32, 0:32])
                last.then_inc(S["l1_kt"], 1)

            def l1_g(j):
                pe.wait_ge(S["l1_kts"], j + 1)
                for m in range(2):
                    for c in range(2):
                        last = mm(bank[5][0:C + 1, 256 + m * 32:256 + (m + 1) * 32], n3[:, 2 * c + m, C:2 * C + 1],
                                  k_t[:, 2 * c + m, :], start=(c == 0), stop=(c == 1))
                last.then_inc(S["l1_g"], 1)

            def l1_qt(j):
                pe.wait_ge(S["l1_gs"], j + 1)
                wait_apart(pe, S["pe_waits"], S["l1_qlink"], QLINKS * (j + 1))
                q = ql[:, :, :].rearrange("p (c n) r -> p c (n r)", c=2)
                for c in range(2):
                    last = nc.tensor.transpose(bank[5][0:C, c * CH:(c + 1) * CH], q[:, c, :], ident[0:CH, 0:CH])

            def l1_m(j):
                for n in range(LH):
                    last = mm(bank[5][0:C, 320 + n * 8:320 + (n + 1) * 8], u_w[:, n, :],
                              kx[:, :, n * LR:(n + 1) * LR])
                last.then_inc(S["l1_m"], 1)

            def l1_mt(j):
                wait_apart(pe, S["pe_waits"], S["l1_ms"], j + 1)
                nc.tensor.transpose(bank[5][0:C, 384:384 + C], m_t[:, :, :, :].rearrange("p m n r -> p (m n r)"),
                                    ident[0:C, 0:C]).then_inc(S["l1_mt"], 1)

            def l1_attn(j):
                pe.wait_ge(S["l1_mts"], 2 * (j + 1))
                pe.wait_ge(S["l1_qts"], j + 1)
                for c in range(2):
                    last = mm(bank[5][0:CH, c * 128:(c + 1) * 128], q_t[:, c, :],
                              m_bd[:, :, :].rearrange("p m o -> p (m o)"))
                last.then_inc(S["l1_attn"], 1)

            def mlp_in(j, k, b, start, ready, gelu, hi, lo, x):
                if k == 0:
                    pe.wait_ge(S[start], j + 1)
                else:
                    pe.wait_ge(S[gelu], 2 * j + 1)
                mm2(bank[b][:, 0:PAIR], hi[:, k * 128:(k + 1) * 128], lo[:, k * 128:(k + 1) * 128],
                    x[:, :]).then_inc(S[ready], 1)

            def mlp_out(j, b, gelu, hid_t, w, ready):
                pe.wait_ge(S[gelu], 2 * j + 2)
                for g in range(G):
                    for k in range(2):
                        last = mm(bank[b][0:CH, g * C:(g + 1) * C], hid_t[:, k, g_cols(g)], w[:, k, :],
                                  start=(k == 0), stop=(k == 1))
                last.then_inc(S[ready], 1)

            def l3_w(j):
                pe.wait_ge(S["l3_split"], j + 1)
                mm2(bank[7][0:CH, 0:PAIR], wr_hi[:, :], wr_lo[:, :], x_l3[:, :]).then_inc(S["l3_w"], 1)

            def l3_wi(j):
                wait_apart(pe, S["pe_waits"], S["l3_wb"], j + 1)
                for g in range(G):
                    last = nc.tensor.transpose(bank[7][0:CH, 400 + g:401 + g], w_b[0:1, g_cols(g)], ident[0:1, 0:1])
                last.then_inc(S["l3_wi"], 1)

            def turn(y, b, ln, j, ready, free, free_at):
                at_least(pe, S[free], free_at)
                turn_norm(y, bank[b], ln, j, ready)

            def body2(i, live):
                f, l1, l2, l3 = i - 1, i - 2, i - 3, i - 4
                if live(1):
                    ff1(f, 0, 0)
                    turn_gate(f)
                if live(2):
                    turn(n3, 5, "ln_4", l1, "l1_xt", "l1_fx", l1)
                if live(4):
                    turn(flat(x4), 7, "ln_6", l3, "l3_xt", "l3_t", l3)
                if live(1):
                    ff1(f, 0, 1)
                    spread_gate(f, 0)
                if live(3):
                    turn(flat(y_2), 6, "ln_5", l2, "l2_xt", "l2_h4", l2)
                if live(1):
                    ff1(f, 1, 0)
                if live(2):
                    l1_k(l1)
                if live(4):
                    l3_w(l3)
                if live(1):
                    ff1(f, 1, 1)
                    spread_gate(f, 1)
                if live(3):
                    mlp_in(l2, 0, 6, "l2_split", "l2_ff", "l2_gelu", m1_hi, m1_lo, x_l2)
                if live(1):
                    ff2(f, 0)
                if live(2):
                    l1_q(l1)
                if live(4):
                    l3_wi(l3)
                if live(1):
                    ff1(f, 2, 0)
                if live(3):
                    mlp_in(l2, 1, 6, "l2_split", "l2_ff", "l2_gelu", m1_hi, m1_lo, x_l2)
                if live(2):
                    l1_kt(l1)
                if live(4):
                    mlp_in(l3, 0, 7, "l3_wis", "l3_ff", "l3_gelu", f1_hi, f1_lo, x_l3)
                if live(1):
                    ff1(f, 2, 1)
                    spread_gate(f, 2)
                    ff2(f, 1)
                if live(3):
                    mlp_out(l2, 6, "l2_gelu", hid2, m2_w, "l2_out")
                if live(2):
                    l1_g(l1)
                if live(1):
                    ff1(f, 3, 0)
                if live(4):
                    mlp_in(l3, 1, 7, "l3_wis", "l3_ff", "l3_gelu", f1_hi, f1_lo, x_l3)
                if live(2):
                    l1_qt(l1)
                    l1_m(l1)
                if live(1):
                    ff1(f, 3, 1)
                    spread_gate(f, 3)
                    ff2(f, 2)
                if live(4):
                    mlp_out(l3, 7, "l3_gelu", hid3, f2_w, "l3_out")
                if live(2):
                    l1_mt(l1)
                if live(1):
                    ff2(f, 3)
                if live(2):
                    l1_attn(l1)
                if live(0):
                    turn(flat(y_m), 4, "ln_m", i, "xm_t", "cb_stored", EP * i)
                if live(1):
                    moe_out(f, live(0))
                if live(0):
                    gate_mm(i)

            pe.wait_ge(S["wo_added"], NP)
            run_lagged(pe, NP, 4, body2)

        @block.scalar
        def _(act):
            with nc.allow_non_contiguous_dma(reason="bias vectors, a few kB in all"):
                for dst, src in weight_loads()[1::2]:
                    act.dma_start(dst, src).then_inc(S["w_loaded"], 16)
            act.wait_ge(S["w_loaded"], 16 * N_LOADS)

            def hi_part(j, dst, b, ready, hi, free, free_at):
                act.wait_ge(S[ready], j + 1)
                at_least(act, S[free], free_at)
                nc.scalar.activation(dst[:, :], bank[b][:, 0:PAIR], ACT.Copy).then_inc(S[hi], 1)

            def exps(j, u, k):
                c, s = u % 2, 4 * u + k
                if k == 0:
                    at_least(act, S["pt_ready"], 16 * j + 4 * u - 4)
                    at_least(act, S["recip_done"], 4 * j + u - 1)
                act.wait_ge(S["max_ready"], 16 * j + s + 1)
                for n in (2 * k, 2 * k + 1):
                    last = nc.scalar.activation(prob[c][0:CH, n * TOK:(n + 1) * TOK],
                                                bank[4 + s % 2][0:CH, (n % 2) * TOK:(n % 2 + 1) * TOK], ACT.Exp,
                                                bias=nmax[c][:, n:n + 1], accum_out=psum_[c][:, n:n + 1])
                last.then_inc(S["exp_done"], 1)

            def store_probs(j, u, k):
                c, q = u % 2, 2 + k // 2
                if k == 1:
                    at_least(act, S["pv_ready"], 4 * j + u - 1)
                act.wait_ge(S["pt_ready"], 16 * j + 4 * u + k + 1)
                nc.scalar.activation(prob_t[c][0:CH, q * 4 * CH:(q + 1) * 4 * CH], bank[6][0:CH, 0:4 * CH],
                                     ACT.Copy).then_inc(S["pt_act"], 1)

            def store_g_hi(j, s):
                m, k = s // 4, s % 4
                act.wait_ge(S["g_ready"], 8 * j + s + 1)
                nc.scalar.activation(g_hi[m][:, 2 * k:2 * k + 2, :],
                                     bank[2 + s % 2][:, 0:PAIR].rearrange("p (n t) -> p n t", n=2),
                                     ACT.Copy).then_inc(S["g_hi_ready"], 1)

            def store_tok(j):
                act.wait_ge(S["tok_ready"], j + 1)
                at_least(act, S["h0_ready"], j)
                nc.scalar.activation(h_t[:, :], bank[0][:, 0:TOK], ACT.Identity,
                                     bias=tok_b[:, :]).then_inc(S["tok_stored"], 1)

            def body1(i, live):
                a = i - 1
                for u in range(4):
                    for k in range(4):
                        if live(1):
                            exps(a, u, k)
                            if u and k % 2:
                                store_probs(a, u - 1, k)
                    if live(0) and u == 1:
                        store_tok(i)
                if live(0):
                    hi_part(i, x_a, 0, "xt_ready", "xt_hi", "scores_ready", 16 * i)
                if live(1):
                    store_probs(a, 3, 1)
                for s in range(8):
                    if live(1) and s == 4:
                        store_probs(a, 3, 3)
                    if live(0):
                        store_g_hi(i, s)

            run_lagged(act, NP, 2, body1)

            def relu(j, q):
                ep = q // 4
                act.wait_ge(S["ff1_ready"], HCH * j + q + 1)
                if q % 4 == 0:
                    at_least(act, S["ff2_ready"], EP * j + ep - 1)
                nc.scalar.activation(hid[:, ep % 2, q % 4, :], bank[0][:, 0:PAIR], ACT.Relu,
                                     bias=b1_c[:, q:q + 1]).then_inc(S["relu_act"], 1)

            def store_comb(j):
                act.wait_ge(S["comb_ready"], j + 1)
                at_least(act, S["cb_ready"], EP * j)
                nc.scalar.activation(comb_t[:, :], bank[4][0:C, 0:PAIR], ACT.Copy).then_inc(S["comb_stored"], 1)

            def store_gate(j, ep):
                act.wait_ge(S["cb_ready"], EP * j + ep + 1)
                at_least(act, S["prod_done"], EP * (j - 1) + ep + 1)
                nc.scalar.activation(comb_b[:, ep, :], bank[4][:, 0:PAIR], ACT.Copy).then_inc(S["cb_stored"], 1)

            def k_bias_add(j):
                act.wait_ge(S["l1_k"], j + 1)
                at_least(act, S["l1_kt"], j)
                nc.scalar.activation(kl[:, :, :], bank[5][0:32, 0:PAIR].rearrange("p (m t) -> p m t", m=2),
                                     ACT.Identity, bias=k_bias[:, :]).then_inc(S["l1_kb"], 1)

            def k_exp(j):
                act.wait_ge(S["l1_klink"], KLINKS * j + 1)
                for m in range(2):
                    last = nc.scalar.activation(kl[:, m, :], kl[:, m, :], ACT.Exp, bias=kmax[:, m:m + 1],
                                                accum_out=ksum[:, m:m + 1])
                last.then_inc(S["l1_kexp"], 1)

            def q_exp(j):
                act.wait_ge(S["l1_qlink"], QLINKS * j + 3)
                nc.scalar.activation(ql[:, :, :], ql[:, :, :], ACT.Exp).then_inc(S["l1_qexp"], 1)

            def gate_exp(j):
                act.wait_ge(S["gate_link"], GATE_LINKS * j + 3)
                nc.scalar.activation(gexp[:, :, :], gexp[:, :, :], ACT.Exp).then_inc(S["gate_exp"], 1)

            def router_bias(j):
                act.wait_ge(S["l3_w"], j + 1)
                at_least(act, S["l3_rank"], 9 * j)
                nc.scalar.activation(w_b[:, :], bank[7][0:CH, 0:PAIR], ACT.Identity,
                                     bias=br_b[:, :]).then_inc(S["l3_wb"], 1)

            def gelu(j, k, b, ff, done, hid_t, bias, func, out_sem):
                act.wait_ge(S[ff], 2 * j + k + 1)
                if k == 0:
                    at_least(act, S[out_sem], j)
                nc.scalar.activation(hid_t[:, k, :], bank[b][:, 0:PAIR], func,
                                     bias=bias[:, k:k + 1]).then_inc(S[done], 1)

            def body2(i, live):
                f, l1, l2, l3 = i - 1, i - 2, i - 3, i - 4
                if live(1):
                    relu(f, 0)
                    store_comb(f)
                if live(2):
                    hi_part(l1, x_l1, 5, "l1_xt", "l1_hi", "l1_q", l1)
                if live(4):
                    hi_part(l3, x_l3, 7, "l3_xt", "l3_hi", "l3_ff", 2 * l3)
                if live(1):
                    relu(f, 2)
                    store_gate(f, 0)
                if live(3):
                    hi_part(l2, x_l2, 6, "l2_xt", "l2_hi", "l2_ff", 2 * l2)
                if live(1):
                    relu(f, 4)
                if live(2):
                    k_bias_add(l1)
                if live(4):
                    router_bias(l3)
                if live(1):
                    relu(f, 6)
                    store_gate(f, 1)
                if live(2):
                    k_exp(l1)
                if live(1):
                    relu(f, 8)
                if live(2):
                    q_exp(l1)
                if live(3):
                    gelu(l2, 0, 6, "l2_ff", "l2_gelu", hid2, m1_bias, ACT.Gelu, "l2_out")
                if live(1):
                    relu(f, 10)
                    store_gate(f, 2)
                if live(3):
                    gelu(l2, 1, 6, "l2_ff", "l2_gelu", hid2, m1_bias, ACT.Gelu, "l2_out")
                if live(4):
                    gelu(l3, 0, 7, "l3_ff", "l3_gelu", hid3, fb1_c, ACT.Gelu_apprx_tanh, "l3_out")
                if live(1):
                    relu(f, 12)
                if live(4):
                    gelu(l3, 1, 7, "l3_ff", "l3_gelu", hid3, fb1_c, ACT.Gelu_apprx_tanh, "l3_out")
                if live(1):
                    relu(f, 14)
                    store_gate(f, 3)
                if live(0):
                    hi_part(i, x_m, 4, "xm_t", "xm_hi", "ff1_ready", HCH * i)
                    gate_exp(i)

            run_lagged(act, NP, 4, body2)

        @block.vector
        def _(dve):
            V = nc.vector

            def tt(o, x, y, op):
                return V.tensor_tensor(o, x, y, op)

            V.memset(x_sb[32:IMG_ROW, :, :], 0.0).then_inc(S["zeroed"], 1)
            zero = Links(dve, S["setup_link"], 0, 0)
            for t in (w_tok[:], bdq[:], bdk[:], bdv[:], m_bd[:]):
                zero.mark(V.memset(t, 0.0))
            zero.mark(V.memset(comb2[:], 0.0))
            zero.mark(V.memset(n3[:, :, 2 * C:2 * C + 1], 1.0))
            zero.mark(V.memset(g1_aug[C:C + 1, :], 1.0))
            zero.wait()
            dve.wait_ge(S["consts_ready"], 13)
            zero.mark(V.tensor_copy(pick_r[:, :, :], pick[:, :, :, :].rearrange("p q r d -> p q (r d)")))
            dve.wait_ge(S["w_loaded"], 16 * N_LOADS)
            for i in range(4):
                r = slice(LD * i, LD * (i + 1))
                for k in range(2):
                    n = 4 * k + i
                    zero.mark(V.tensor_copy(bdq[r, k, n * LR:(n + 1) * LR], q1_n[r, :]))
                    zero.mark(V.tensor_copy(bdk[r, k, n * LR:(n + 1) * LR], k1_n[r, :]))
                zero.mark(V.tensor_copy(bdv[r, r], v1_n[r, :]))
            zero.wait()

            def start(name):
                dve.wait_ge(S["setup_mm"], idx[name] + 1)

            def finish(ins):
                ins.then_inc(S["setup_done"], 1)

            def split(hi, lo, src, scalar):
                zero.link(V.tensor_scalar(hi, src, scalar, None, ALU.mult))
                return V.scalar_tensor_tensor(out=lo, in0=src, scalar=scalar, in1=hi.bitcast(F32), op0=ALU.mult,
                                              op1=ALU.subtract)

            for b in range(2):
                start(f"tok{b}")
                o = sbank(f"tok{b}")[0:48, :].rearrange("p (q e) -> p q e", e=C)
                zero.mark(V.tensor_copy(w_tok[0:48, 8 * b:8 * b + 8, 0:C], o))
                finish(V.tensor_copy(w_tok[IMG_ROW:IMG_ROW + 48, 8 * b:8 * b + 8, C:2 * C], o))
            scale = float(np.float32(1.0) / np.sqrt(HEADS).astype(np.float32))
            for b in range(2):
                start(f"a{b}")
                w = slice(512 * b, 512 * (b + 1))
                finish(split(a_hi[:, w], a_lo[:, w], sbank(f"a{b}")[:, :], scale))
            start("wv")
            finish(split(wv_hi[:, :], wv_lo[:, :], sbank("wv")[:, 0:C], 1.0))
            start("wo")
            finish(V.tensor_copy(wo_t[:, :, :], sbank("wo")[:, 0:4 * C].rearrange("p (k o) -> p k o", k=4)))
            start("wg")
            finish(split(wg_hi[:, :], wg_lo[:, :], sbank("wg")[:, 0:EXPERTS], 1.0))
            for b in range(4):
                start(f"w1_{b}")
                w = slice(4 * b, 4 * b + 4)
                finish(split(w1_hi[:, w, :].rearrange("p q n -> p (q n)"), w1_lo[:, w, :].rearrange("p q n -> p (q n)"),
                             sbank(f"w1_{b}")[:, :], 1.0))
            for b in range(2):
                start(f"w2_{b}")
                finish(V.tensor_copy(w2_t[:, 2 * b:2 * b + 2, :, :].rearrange("p q k n -> p (q k n)"),
                                     sbank(f"w2_{b}")[:, :]))
            start("wx")
            wx_t = sbank("wx")[:, 0:2 * C].rearrange("p (k c) -> p k c", k=2)
            zero.mark(V.tensor_copy(wx_dup[:, :, 0:C], wx_t))
            zero.mark(V.tensor_copy(wx_dup[:, :, C:2 * C], wx_t))
            finish(V.tensor_copy(wxa[:, :, 0:C], wx_t))
            start("bfull")
            finish(tt(wxa[:, :, C], sbank("bfull")[:, 0:2], bx_c[:, :], ALU.add))
            start("wqk")
            finish(split(wqk_hi[:, :], wqk_lo[:, :], sbank("wqk")[:, 0:64], g1_dup[:, 0:1]))
            start("qb")
            finish(V.tensor_copy(q_bias[:, :], sbank("qb")[0:CH, 0:32]))
            start("kb")
            finish(V.tensor_copy(k_bias[:, :], sbank("kb")[0:32, 0:1]))
            start("vt")
            finish(V.tensor_copy(vt[:, :, :], sbank("vt")[:, 0:2 * (C + 1)].rearrange("p (k c) -> p k c", k=2)))
            for i in range(4):
                start(f"u{i}")
                finish(V.tensor_scalar(u_w[:, i::4, :],
                                       sbank(f"u{i}")[0:C + 1, 0:2 * C].rearrange("p (k o) -> p k o", k=2),
                                       g1_aug[:, 0:1], None, ALU.mult))
            start("b1m")
            zero.mark(tt(m1_bias[:, :], sbank("b1m")[:, 0:2], mb1_c[:, :], ALU.add))
            split_m = split(m1_hi[:, :], m1_lo[:, :], m1_n[:, :], g2_dup[:, 0:1])
            zero.mark(split_m)
            zero.mark(split(f1_hi[:, :], f1_lo[:, :], f1_n[:, :], 1.0))
            zero.link(V.tensor_copy(wr_hi[:, :], wr_n[:, 0:1].to_broadcast([128, CH])))
            finish(tt(wr_lo[:, :], wr_n[:, 0:1].to_broadcast([128, CH]), wr_hi[:, :].bitcast(F32), ALU.subtract))
            zero.wait()
            V.engine_nop().then_inc(S["setup_done"], 1)

            def ln_stats(n, j, src, ready, ready_at):
                wait_apart(dve, S["dve_waits"], S[ready], ready_at)
                L = Links(dve, S[f"ln_{n}"], j, 4)
                for g in range(G):
                    last = V.bn_stats(st[n][:, g, :], src(g))
                L.mark(last)
                wait_apart(dve, S["dve_waits"], L.sem, L.base + L.k)
                for g in range(G):
                    last = V.bn_aggr(mv[n][:, g, :], st[n][:, g, :])
                L.link(last)
                L.mark(V.tensor_scalar(ve[n][:, :], mv[n][:, :, 1], EPS, None, ALU.add))

            def ln_apply(n, j, src, dst, free=None, free_at=0):
                dve.wait_ge(S[f"pow_{n}"], j + 1)
                if free:
                    at_least(dve, S[free], free_at)
                for g in range(G):
                    o, x = dst(g), src(g)
                    if len(o.shape) == 3:
                        x = x.unsqueeze(1).to_broadcast([CH, 2, C])
                    last = V.tensor_scalar(o, x, mv[n][:, g, 0:1], rstd[n][:, g:g + 1], ALU.subtract, ALU.mult)
                last.then_inc(S[f"ln_{n}"], 1)

            def lo_part(j, dst, b, hi, split_sem):
                dve.wait_ge(S[hi], j + 1)
                tt(dst[C:128, :], bank[b][C:128, 0:PAIR], dst[C:128, :].bitcast(F32),
                   ALU.subtract).then_inc(S[split_sem], 1)

            def neg_max(j, u, k):
                c, s = u % 2, 4 * u + k
                if k == 0:
                    at_least(dve, S["exp_done"], 16 * j + 4 * u - 4)
                dve.wait_ge(S["scores_ready"], 16 * j + s + 1)
                V.tensor_reduce(nmax[c][:, 2 * k:2 * k + 2],
                                bank[4 + s % 2][0:CH, 0:PAIR].rearrange("p (n t) -> p n t", n=2), AX_X, ALU.max,
                                negate=True).then_inc(S["max_ready"], 1)

            def store_probs(j, u, k):
                c, q = u % 2, k // 2
                if k == 0:
                    at_least(dve, S["pv_ready"], 4 * j + u - 1)
                dve.wait_ge(S["pt_ready"], 16 * j + 4 * u + k + 1)
                V.tensor_copy(prob_t[c][0:CH, q * 4 * CH:(q + 1) * 4 * CH],
                              bank[1][0:CH, 0:4 * CH]).then_inc(S["pt_dve"], 1)

            def invert_sums(j, u):
                c = u % 2
                dve.wait_ge(S["exp_done"], 16 * j + 4 * u + 4)
                at_least(dve, S["ctx_norm"], 4 * j + u - 1)
                V.reciprocal(rsum[c][:, :], psum_[c][:, :]).then_inc(S["recip_done"], 1)

            def normalise(j, u):
                m, c = u // 2, u % 2
                dve.wait_ge(S["recip_done"], 4 * j + u + 1)
                dve.wait_ge(S["pv_ready"], 4 * j + u + 1)
                at_least(dve, ctx_wr[c], 16 * (2 * j + m))
                tt(ctx_sb[c][:, :].rearrange("p (n d) -> p n d", n=HEADS),
                   bank[7][0:CH, :].rearrange("p (n d) -> p n d", n=HEADS),
                   rsum[c][:, :].unsqueeze(2).to_broadcast([CH, HEADS, C]), ALU.mult).then_inc(S["ctx_norm"], 1)

            def store_v(j):
                dve.wait_ge(S["v_ready"], j + 1)
                at_least(dve, S["v_written"], 16 * j)
                V.tensor_copy(v_lin[:, :, :], bank[2][0:C, 0:PAIR].rearrange("p (m t) -> p m t", m=2))\
                    .then_inc(S["v_stored"], 1)

            def store_g_lo(j, s):
                m, k = s // 4, s % 4
                dve.wait_ge(S["g_hi_ready"], 8 * j + s + 1)
                tt(g_lo[m][:, 2 * k:2 * k + 2, :], bank[2 + s % 2][:, 0:PAIR].rearrange("p (n t) -> p n t", n=2),
                   g_hi[m][:, 2 * k:2 * k + 2, :].bitcast(F32), ALU.subtract).then_inc(S["g_split"], 1)

            def add_attention(j):
                dve.wait_ge(S["wo_ready"], j + 1)
                dve.wait_ge(S["h0_stored"], j + 1)
                tt(h[:, j], bank[4][0:CH, 0:256].rearrange("p (g c) -> p g c", g=G), h[:, j],
                   ALU.add).then_inc(S["wo_added"], 1)

            def store_h0(j):
                dve.wait_ge(S["h0_ready"], j + 1)
                V.tensor_copy(h[:, j], bank[0][0:CH, 256:512].rearrange("p (g c) -> p g c", g=G))\
                    .then_inc(S["h0_stored"], 1)

            def body1(i, live):
                a, o = i - 1, i - 2
                for u in range(4):
                    if u == 1 and live(2):
                        normalise(o, 3)
                    if u == 3 and live(1):
                        normalise(a, 0)
                    if live(1):
                        neg_max(a, u, 0)
                    if u == 2 and live(0):
                        store_h0(i)
                    if live(1):
                        neg_max(a, u, 1)
                    if u == 0 and live(2):
                        invert_sums(o, 3)
                    if u > 0 and live(1):
                        invert_sums(a, u - 1)
                        store_probs(a, u - 1, 0)
                    if live(1):
                        neg_max(a, u, 2)
                    if live(0):
                        if u == 2:
                            ln_stats("a", i, lambda g: h[:, i, g, :], "h0_stored", i + 1)
                        if u == 3:
                            ln_apply("a", i, lambda g: h[:, i, g, :], lambda g: y_a[:, g, :, :], "xt_ready", i)
                    if live(1):
                        neg_max(a, u, 3)
                    if u > 0 and live(1):
                        store_probs(a, u - 1, 2)
                if live(1):
                    normalise(a, 1)
                if live(0):
                    lo_part(i, x_a, 0, "xt_hi", "xt_split")
                if live(1):
                    store_probs(a, 3, 0)
                if live(0):
                    store_v(i)
                for s in range(8):
                    if live(1) and s == 2:
                        store_probs(a, 3, 2)
                    if live(1) and s == 3:
                        normalise(a, 2)
                    if live(2) and s == 7:
                        add_attention(o)
                    if live(0):
                        store_g_lo(i, s)

            run_lagged(dve, NP, 2, body1)

            def relu(j, q):
                ep = q // 4
                dve.wait_ge(S["ff1_ready"], HCH * j + q + 1)
                if q % 4 == 1:
                    at_least(dve, S["ff2_ready"], EP * j + ep - 1)
                V.tensor_scalar(hid[:, ep % 2, q % 4, :], bank[1][:, 0:PAIR], b1_c[:, q:q + 1], 0.0, ALU.add,
                                ALU.max).then_inc(S["relu_dve"], 1)

            def weigh(j, ep):
                dve.wait_ge(S["ff2_ready"], EP * j + ep + 1)
                dve.wait_ge(S["cb_stored"], EP * j + ep + 1)
                if ep == 0:
                    at_least(dve, S["moe_ready"], j)
                V.scalar_tensor_tensor(out=prod[:, ep, :], in0=bank[2 + ep % 2][:, 0:PAIR], scalar=b2_c[:, ep:ep + 1],
                                       in1=comb_b[:, ep, :], op0=ALU.add, op1=ALU.mult).then_inc(S["prod_done"], 1)

            def gate_scores(j):
                L = Links(dve, S["gate_link"], j, GATE_LINKS)
                dve.wait_ge(S["gate_ready"], j + 1)
                L.link(tt(gs[:, :, :], bank[4][0:CH, PAIR:PAIR + 32].rearrange("p (g e) -> p g e", g=G),
                          bg_b[:, :].unsqueeze(1).to_broadcast([CH, G, EXPERTS]), ALU.add))
                L.link(V.tensor_reduce(gmax[:, :], gs[:, :, :], AX_X, ALU.max, negate=True))
                L.mark(tt(gexp[:, :, :], gs[:, :, :], gmax[:, :].unsqueeze(2).to_broadcast([CH, G, EXPERTS]), ALU.add))
                return L

            def gate_weights(j, L):
                other = gs[:, :, :].unsqueeze(2).to_broadcast([CH, G, EXPERTS, EXPERTS])
                own = gs[:, :, :].unsqueeze(3).to_broadcast([CH, G, EXPERTS, EXPERTS])
                L.mark(tt(above[:, :, :, :], other, own, ALU.is_gt))
                L.link(tt(tied[:, :, :, :], other, own, ALU.is_equal))
                L.link(tt(tied[:, :, :, :], tied[:, :, :, :],
                          tie_exp[:, :, :].unsqueeze(1).to_broadcast([CH, G, EXPERTS, EXPERTS]), ALU.mult))
                L.link(tt(above[:, :, :, :], above[:, :, :, :], tied[:, :, :, :], ALU.add))
                L.link(V.tensor_reduce(rank_e[:, :, :], above[:, :, :, :], AX_X, ALU.add))
                dve.wait_ge(S["gate_exp"], j + 1)
                L.link(V.scalar_tensor_tensor(out=gexp[:, :, :], in0=rank_e[:, :, :], scalar=1.5, in1=gexp[:, :, :],
                                              op0=ALU.is_lt, op1=ALU.mult))
                L.link(V.tensor_reduce(gsum[:, :], gexp[:, :, :], AX_X, ALU.add))
                L.link(V.reciprocal(gmax[:, :], gsum[:, :]))
                L.link(tt(comb[:, :, :], gexp[:, :, :], gmax[:, :].unsqueeze(2).to_broadcast([CH, G, EXPERTS]),
                          ALU.mult))
                at_least(dve, S["comb_ready"], j)
                L.link(V.tensor_copy(comb2[:, :, 0:EXPERTS].bitcast(F32R), comb[:, :, :]))
                L.mark(tt(comb2[:, :, 32:32 + EXPERTS], comb[:, :, :], comb2[:, :, 0:EXPERTS], ALU.subtract))
                L.end()

            def add_experts(j):
                dve.wait_ge(S["moe_ready"], j + 1)
                tt(h[:, j], bank[4][0:CH, 0:256].rearrange("p (g c) -> p g c", g=G), h[:, j],
                   ALU.add).then_inc(S["moe_added"], 1)

            def k_max(j):
                dve.wait_ge(S["l1_kb"], j + 1)
                V.tensor_reduce(kmax[:, :], kl[:, :, :], AX_X, ALU.max, negate=True).then_inc(S["l1_klink"], 1)

            def k_norm(j):
                dve.wait_ge(S["l1_kexp"], j + 1)
                V.reciprocal(krec[:, :], ksum[:, :]).then_inc(S["l1_klink"], 1)
                dve.wait_ge(S["l1_klink"], KLINKS * j + 2)
                tt(kl[:, :, :], kl[:, :, :], krec[:, :].unsqueeze(2).to_broadcast([32, 2, TOK]),
                   ALU.mult).then_inc(S["l1_klink"], 1)

            qv = ql[:, :, :].rearrange("p (g n) r -> p g (n r)", g=G)

            def q_shift(j):
                L = Links(dve, S["l1_qlink"], j, QLINKS)
                dve.wait_ge(S["l1_q"], j + 1)
                at_least(dve, S["l1_m"], j)
                L.link(tt(qv, bank[5][0:CH, 0:128].rearrange("p (g n) -> p g n", g=G),
                          q_bias[:, :].unsqueeze(1).to_broadcast([CH, G, 32]), ALU.add))
                L.link(V.tensor_reduce(qmax[:, :], ql[:, :, :], AX_X, ALU.max, negate=True))
                L.link(tt(ql[:, :, :], ql[:, :, :], qmax[:, :].unsqueeze(2).to_broadcast([CH, G * LH, LR]), ALU.add))
                return L

            def q_norm(j, L):
                dve.wait_ge(S["l1_qexp"], j + 1)
                L.link(V.tensor_reduce(qmax[:, :], ql[:, :, :], AX_X, ALU.add))
                L.link(V.reciprocal(qmax[:, :], qmax[:, :]))
                L.mark(tt(ql[:, :, :], ql[:, :, :], qmax[:, :].unsqueeze(2).to_broadcast([CH, G * LH, LR]), ALU.mult))
                L.end()

            def store(j, dst, src, ready, done, free=None):
                dve.wait_ge(S[ready], j + 1)
                if free:
                    at_least(dve, S[free], j)
                V.tensor_copy(dst, src).then_inc(S[done], 1)

            def store_m(j):
                dve.wait_ge(S["l1_mt"], j + 1)
                at_least(dve, S["l1_attn"], j)
                for m in range(2):
                    V.tensor_copy(m_bd[32 * m:32 * m + 32, m, :],
                                  bank[5][32 * m:32 * m + 32, 384:384 + C]).then_inc(S["l1_mts"], 1)

            def rank_tokens(j):
                for g in range(G):
                    c, m = g // 2, g % 2
                    V.scalar_tensor_tensor(out=tie_w[:, g, :], in0=w_b[:, m * TOK:(m + 1) * TOK], scalar=w_i[:, g:g + 1],
                                           in1=tie_tok[:, c, :], op0=ALU.is_equal, op1=ALU.mult)\
                        .then_inc(S["l3_rank"], 1)
                for g in range(G):
                    c, m = g // 2, g % 2
                    dve.wait_ge(S["l3_rank"], 9 * j + g + 1)
                    V.scalar_tensor_tensor(out=tie_w[:, g, :], in0=w_b[:, m * TOK:(m + 1) * TOK], scalar=w_i[:, g:g + 1],
                                           in1=tie_w[:, g, :], op0=ALU.is_gt, op1=ALU.add,
                                           accum_out=rank_w[:, g:g + 1]).then_inc(S["l3_rank"], 1)
                dve.wait_ge(S["l3_rank"], 9 * j + 8)
                at_least(dve, S["l3_mul"], j)
                V.scalar_tensor_tensor(out=w_sel[:, :], in0=rank_w[:, :], scalar=KEEP - 0.5, in1=w_i[:, :],
                                       op0=ALU.is_lt, op1=ALU.mult).then_inc(S["l3_rank"], 1)

            def tokens(b):
                return bank[b][0:CH, 0:256].rearrange("p (g c) -> p g c", g=G)

            def body2(i, live):
                f, l1, l2, l3 = i - 1, i - 2, i - 3, i - 4
                if live(1):
                    relu(f, 1)
                if live(2):
                    lo_part(l1, x_l1, 5, "l1_hi", "l1_split")
                if live(4):
                    lo_part(l3, x_l3, 7, "l3_hi", "l3_split")
                if live(1):
                    relu(f, 3)
                if live(3):
                    lo_part(l2, x_l2, 6, "l2_hi", "l2_split")
                if live(0):
                    ln_stats("m", i, lambda g: h[:, i, g, :], "wo_added", i + 1)
                if live(1):
                    relu(f, 5)
                if live(2):
                    k_max(l1)
                if live(1):
                    relu(f, 7)
                    weigh(f, 0)
                if live(2):
                    Lq = q_shift(l1)
                    k_norm(l1)
                if live(4):
                    store(l3, w_i[:, :], bank[7][0:CH, 400:404], "l3_wi", "l3_wis")
                if live(1):
                    relu(f, 9)
                if live(2):
                    q_norm(l1, Lq)
                    store(l1, k_t[:, :, :], bank[5][0:CH, 128:256].rearrange("p (g n) -> p g n", g=G), "l1_kt",
                          "l1_kts", "l1_g")
                if live(1):
                    relu(f, 11)
                    weigh(f, 1)
                if live(4):
                    dve.wait_ge(S["l3_wis"], l3 + 1)
                    rank_tokens(l3)
                if live(2):
                    store(l1, kx[:, :, :], bank[5][0:C + 1, 256:320].rearrange("p (m n) -> p m n", m=2), "l1_g",
                          "l1_gs", "l1_m")
                if live(1):
                    relu(f, 13)
                if live(2):
                    store(l1, q_t[:, :, :], bank[5][0:C, 0:TOK].rearrange("p (c t) -> p c t", c=2), "l1_m",
                          "l1_qts", "l1_attn")
                    store(l1, m_t[:, :, :, :].rearrange("p m n r -> p n m r"),
                          bank[5][0:C, 320:384].rearrange("p (n m r) -> p n m r", n=LH, m=2), "l1_m", "l1_ms", "l1_mt")
                if live(1):
                    relu(f, 15)
                    weigh(f, 2)
                if live(0):
                    ln_apply("m", i, lambda g: h[:, i, g, :], lambda g: y_m[:, g, :, :], "xm_t", i)
                if live(3):
                    dve.wait_ge(S["l2_out"], l2 + 1)
                    dve.wait_ge(S["l2_base"], 2 * l2 + 2)
                    at_least(dve, S["l3_base"], l2)
                    tt(h4[:, :, :], tokens(6), base2[:, :, :], ALU.add).then_inc(S["l2_h4"], 1)
                    ln_stats("6", l2, lambda g: h4[:, g, :], "l2_h4", l2 + 1)
                if live(2):
                    store_m(l1)
                if live(4):
                    dve.wait_ge(S["l3_out"], l3 + 1)
                    at_least(dve, S["l3_fin"], l3)
                    tt(o_t[:, :, :], tokens(7), fb2_b[:, :].unsqueeze(1).to_broadcast([CH, G, C]),
                       ALU.add).then_inc(S["l3_t"], 1)
                if live(1):
                    weigh(f, 3)
                if live(2):
                    dve.wait_ge(S["l1_attn"], l1 + 1)
                    dve.wait_ge(S["l1_x3b"], l1 + 1)
                    at_least(dve, S["l2_base"], 2 * l1)
                    at_least(dve, S["ln_5"], 4 * l1)
                    tt(fx[:, :, :], tokens(5), x3b[:, :, :], ALU.add).then_inc(S["l1_fx"], 1)
                    ln_stats("5", l1, lambda g: fx[:, g, :], "l1_fx", l1 + 1)
                if live(3):
                    ln_apply("6", l2, lambda g: h4[:, g, :], lambda g: x4[:, g, :, :], "l3_xt", l2)
                if live(0):
                    lo_part(i, x_m, 4, "xm_hi", "xm_split")
                if live(1):
                    add_experts(f)
                    ln_stats("3", f, lambda g: h[:, f, g, :], "moe_added", f + 1)
                if live(2):
                    ln_apply("5", l1, lambda g: fx[:, g, :], lambda g: y_2[:, g, :, :], "l2_xt", l1)
                if live(4):
                    dve.wait_ge(S["l3_mul"], l3 + 1)
                    dve.wait_ge(S["l3_base"], l3 + 1)
                    at_least(dve, S["l3_stored"], 32 * l3)
                    tt(o_sb[:, :, :], o_t[:, :, :], base3[:, :, :], ALU.add).then_inc(S["l3_fin"], 1)
                if live(0):
                    Lg = gate_scores(i)
                if live(1):
                    ln_apply("3", f, lambda g: h[:, f, g, :], lambda g: x3[:, g, :], "l1_x3b", f)
                    ln_stats("4", f, lambda g: x3[:, g, :], "ln_3", 4 * f + 4)
                if live(0):
                    gate_weights(i, Lg)
                if live(1):
                    ln_apply("4", f, lambda g: x3[:, g, :], lambda g: n3[:, g, 0:2 * C].rearrange("p (k c) -> p k c", k=2), "l1_g", f)

            run_lagged(dve, NP, 4, body2)


_INS = ["x", "L0_tok_W", "L0_tok_b", "L0_attn_Wq", "L0_attn_Wk", "L0_attn_Wv", "L0_attn_Wo", "L0_ffn_Wg", "L0_ffn_bg",
        "L0_ffn_W1", "L0_ffn_b1", "L0_ffn_W2", "L0_ffn_b2", "L1_attn_ln1_g", "L1_attn_ln1_b", "L1_attn_Wx",
        "L1_attn_bx", "L1_attn_Wq", "L1_attn_Wk", "L1_attn_Wv", "L1_attn_Wo", "L1_attn_bo", "L1_attn_ln2_g",
        "L1_attn_ln2_b", "L1_attn_W1", "L1_attn_b1", "L1_attn_W2", "L1_attn_b2", "L1_ffn_attention_mask", "L1_ffn_wr",
        "L1_ffn_br", "L1_ffn_w1", "L1_ffn_b1", "L1_ffn_w2", "L1_ffn_b2"]
_UNUSED = {"L1_ffn_attention_mask"}


def kernel(**inputs):
    import numpy as _np
    import concourse.bacc as _bacc
    from concourse import mybir as _mybir
    from concourse.bass_utils import run_bass_kernel_spmd as _run

    nc = _bacc.Bacc("TRN2", target_bir_lowering=False, num_devices=1)
    arrays, args = {}, {}
    for name in _INS:
        if name in _UNUSED:
            continue
        v = _np.ascontiguousarray(inputs[name])
        arrays[f"in_{name}_dram"] = v
        args[name] = nc.dram_tensor(f"in_{name}_dram", v.shape, _mybir.dt.from_np(v.dtype), kind="ExternalInput").ap()
    shape = (inputs["x"].shape[0], TOK, C)
    out = nc.dram_tensor("out_0_dram", shape, F32, kind="ExternalOutput").ap()
    vit_tower(nc, args, out)
    r = _run(nc, [arrays], core_ids=[0])
    return r.results[0]["out_0_dram"]
```

```python
from contextlib import ExitStack

import numpy as np

import concourse.bass as bass
from concourse import mybir

F32 = mybir.dt.float32
F32R = mybir.dt.float32r
ALU = mybir.AluOpType
ACT = mybir.ActivationFunctionType
AX_X = mybir.AxisListType.X

C = 64
PATCH = 16
SIDE = 14
TOK = SIDE * SIDE
CH = TOK // 2
G = 4
PAIR = 2 * TOK
IMG_ROW = 64
XROWS = IMG_ROW + 48
HEADS = 8
EXPERTS = 8
EP = EXPERTS // 2
HCH = 2 * EXPERTS
LH, LR, LD = 8, 4, 32
KEEP = TOK // 2 - 1
EPS = 1e-5
LN_LINKS = 3
DEPTH = 5


def at_least(eng, sem, value):
    if isinstance(value, int) and value <= 0:
        return
    eng.wait_ge(sem, value)


def wait_apart(eng, waits, sem, value):
    eng.wait_ge(sem, value)
    if not isinstance(value, int):
        eng.sem_inc(waits, 1)


class Links:

    def __init__(self, eng, sem, j, n):
        self.eng, self.sem, self.base, self.n, self.k = eng, sem, j * n, n, 0

    def mark(self, ins):
        self.k += 1
        ins.then_inc(self.sem, 1)

    def wait(self):
        self.eng.wait_ge(self.sem, self.base + self.k)

    def link(self, ins):
        self.mark(ins)
        self.wait()

    def end(self):
        assert self.k == self.n, (self.k, self.n)


def run_lagged(eng, pairs, depth, body):
    for i in range(depth + 1):
        body(i, lambda lag, i=i: i - lag >= 0)
    with eng.Fori(depth + 1, pairs) as i:
        body(i, lambda lag: True)
    for i in range(pairs, pairs + depth):
        body(i, lambda lag, i=i: i - lag < pairs)


def vit_tower(nc, a, out):
    B = a["x"].shape[0]
    NP = B // 2
    with ExitStack() as ctx:
        def sb(name, shape, dt=F32):
            return ctx.enter_context(nc.sbuf_tensor(name, shape, dt))

        def sem(name):
            return ctx.enter_context(nc.semaphore(name))

        bank = [ctx.enter_context(nc.psum_tensor(f"bank{i}", [128, 512], F32)) for i in range(8)]

        v_dram = nc.dram_tensor("v_scratch", (NP, 2, C, TOK), F32, kind="Internal").ap()
        ctx_dram = nc.dram_tensor("ctx_scratch", (NP, 2, TOK, HEADS * C), F32, kind="Internal").ap()

        ident = sb("ident", [128, 128])
        ident2 = sb("ident2", [128, C])
        pick = sb("pick", [C, EP, 2, C])
        pick_r = sb("pick_r", [C, EP, 2 * C], F32R)
        tie_tok = sb("tie_tok", [CH, 2, TOK])
        tie_exp = sb("tie_exp", [CH, EXPERTS, EXPERTS])
        eps = sb("eps", [CH, G])
        half = sb("half", [CH, G])
        w_tok = sb("w_tok", [XROWS, PATCH, 2 * C])
        a_hi = sb("a_hi", [128, HEADS * 128], F32R)
        a_lo = sb("a_lo", [128, HEADS * 128], F32R)
        wv_hi, wv_lo = sb("wv_hi", [128, C], F32R), sb("wv_lo", [128, C], F32R)
        wo_t = sb("wo_t", [128, 4, C])
        wg_hi, wg_lo = sb("wg_hi", [128, EXPERTS], F32R), sb("wg_lo", [128, EXPERTS], F32R)
        w1_hi = sb("w1_hi", [128, HCH, 128], F32R)
        w1_lo = sb("w1_lo", [128, HCH, 128], F32R)
        w2_t = sb("w2_t", [128, EP, 2, 128])
        wqk_hi, wqk_lo = sb("wqk_hi", [128, 64], F32R), sb("wqk_lo", [128, 64], F32R)
        wxa = sb("wxa", [128, 2, C + 1])
        wx_dup = sb("wx_dup", [128, 2, 2 * C])
        bdq, bdk = sb("bdq", [128, 2, 32]), sb("bdk", [128, 2, 32])
        bdv = sb("bdv", [128, 128])
        vt = sb("vt", [128, 2, C + 1])
        u_w = sb("u_w", [C + 1, LH, C])
        q_bias = sb("q_bias", [CH, 32])
        k_bias = sb("k_bias", [32, 1])
        m1_hi, m1_lo = sb("m1_hi", [128, 256], F32R), sb("m1_lo", [128, 256], F32R)
        f1_hi, f1_lo = sb("f1_hi", [128, 256], F32R), sb("f1_lo", [128, 256], F32R)
        m1_s = sb("m1_s", [128, 256])
        m1_bias = sb("m1_bias", [128, 2])
        wr_hi, wr_lo = sb("wr_hi", [128, CH], F32R), sb("wr_lo", [128, CH], F32R)
        m2_w, f2_w = sb("m2_w", [128, 2, C]), sb("f2_w", [128, 2, C])
        tok_b = sb("tok_b", [128, 1])
        g1_dup, g2_dup = sb("g1_dup", [128, 1]), sb("g2_dup", [128, 1])
        g1_aug = sb("g1_aug", [C + 1, 1])
        ln1b, ln2b = sb("ln1b", [C, 1]), sb("ln2b", [C, 1])
        bx_c = sb("bx_c", [128, 2])
        mb1_c, fb1_c = sb("mb1_c", [128, 2]), sb("fb1_c", [128, 2])
        b1_c = sb("b1_c", [128, HCH])
        b2_c = sb("b2_c", [128, EP])
        bg_b = sb("bg_b", [CH, EXPERTS])
        bo_b, mb2_b, fb2_b = sb("bo_b", [CH, C]), sb("mb2_b", [CH, C]), sb("fb2_b", [CH, C])
        br_b = sb("br_b", [CH, 1])
        wk_dup = sb("wk_dup", [C, 128])
        wv_n, wg_n = sb("wv_n", [C, 2 * C]), sb("wg_n", [EXPERTS, 2 * C])
        wx_n = sb("wx_n", [C, 256])
        wo1_n = sb("wo1_n", [128, 2, C])
        q1_n, k1_n, v1_n = sb("q1_n", [128, LR]), sb("k1_n", [128, LR]), sb("v1_n", [128, LD])
        m1_n, f1_n = sb("m1_n", [128, 256]), sb("f1_n", [128, 256])
        wr_n = sb("wr_n", [128, 1])

        h = sb("h", [CH, NP, G, C])

        x_sb = sb("x_sb", [XROWS, SIDE, SIDE * PATCH])
        h_t = sb("h_t", [128, TOK])
        NORMS = "am3456"
        st = {n: sb(f"st_{n}", [CH, G, 6]) for n in NORMS}
        mv = {n: sb(f"mv_{n}", [CH, G, 2]) for n in NORMS}
        ve = {n: sb(f"ve_{n}", [CH, G]) for n in NORMS}
        rstd = {n: sb(f"rstd_{n}", [CH, G]) for n in NORMS}
        y_a = sb("y_a", [CH, G, 2, C])
        x_a = sb("x_a", [128, PAIR], F32R)
        v_lin = sb("v_lin", [C, 2, TOK])
        v_tok = sb("v_tok", [CH, 2, 2, C])
        g_hi = [sb(f"g_hi{m}", [128, HEADS, TOK], F32R) for m in range(2)]
        g_lo = [sb(f"g_lo{m}", [128, HEADS, TOK], F32R) for m in range(2)]
        nmax = [sb(f"nmax{c}", [CH, HEADS]) for c in range(2)]
        psum_ = [sb(f"psums{c}", [CH, HEADS]) for c in range(2)]
        rsum = [sb(f"rsum{c}", [CH, HEADS]) for c in range(2)]
        prob = [sb(f"prob{c}", [128, HEADS * TOK]) for c in range(2)]
        prob_t = [sb(f"prob_t{c}", [128, 2 * HEADS * CH]) for c in range(2)]
        ctx_sb = [sb(f"ctx_sb{c}", [CH, HEADS * C]) for c in range(2)]
        ctx_r = [sb(f"ctx_r{m}", [128, 4, TOK]) for m in range(2)]
        hid = sb("hid", [128, 2, 4, PAIR])
        w1_n = hid[:, :, :, :].rearrange("p a b t -> p (a b t)")[:, 0:HCH * 2 * C].rearrange("p (q c) -> p q c", q=HCH)
        w2_n = prob_t[1][:, 0:EP * 256].rearrange("p (q n) -> p q n", q=EP)
        wtok_n = prob[0][0:C, 0:3 * PATCH * PATCH]
        wq_n = prob[1][0:C, 0:2 * HEADS * C].rearrange("p (n c) -> p n c", n=HEADS)
        wo_n = prob_t[0][0:C, 0:512]

        gs = sb("gs", [CH, G, EXPERTS])
        above = sb("above", [CH, G, EXPERTS, EXPERTS])
        tied = sb("tied", [CH, G, EXPERTS, EXPERTS])
        rank_e = sb("rank_e", [CH, G, EXPERTS])
        gmax = sb("gmax", [CH, G])
        gexp = sb("gexp", [CH, G, EXPERTS])
        gsum = sb("gsum", [CH, G])
        comb = sb("comb", [CH, G, EXPERTS])
        comb2 = sb("comb2", [CH, G, C])
        comb_t = sb("comb_t", [C, PAIR], F32R)
        comb_b = prob[0][:, :].rearrange("p (q t) -> p q t", q=EP)
        prod = prob[1][:, :].rearrange("p (q t) -> p q t", q=EP)
        x_parts = g_lo[1][:, :, :].rearrange("p n t -> p (n t)")
        x_m, x_l1, x_l2, x_l3 = (x_parts[:, k * PAIR:(k + 1) * PAIR] for k in range(4))
        turned = prob_t[0][0:CH, 0:3 * G * 2 * C].rearrange("p (k g d c) -> p k g d c", k=3, g=G, d=2)
        y_m, y_2, x4 = (turned[:, k] for k in range(3))
        tie_w = prob_t[1][0:CH, 0:G * TOK].rearrange("p (g t) -> p g t", g=G)
        w_b = prob_t[1][0:CH, G * TOK:G * TOK + PAIR]
        base3 = prob_t[1][0:CH, G * TOK + PAIR:G * TOK + PAIR + G * C].rearrange("p (g c) -> p g c", g=G)
        fx, h4, o_t, o_sb = (ctx_sb[k // 2][:, :].rearrange("p (k g c) -> p k g c", k=2, g=G)[:, k % 2] for k in range(4))
        hid2, hid3 = (ctx_r[m][:, :, :].rearrange("p (k m) t -> p k (m t)", k=2) for m in range(2))
        x3 = sb("x3", [CH, G, C])
        x3b = sb("x3b", [CH, G, C])
        n3 = sb("n3", [CH, G, 2 * C + 1])
        kl = sb("kl", [32, 2, TOK])
        kmax, ksum, krec = sb("kmax", [32, 2]), sb("ksum", [32, 2]), sb("krec", [32, 2])
        k_t = sb("k_t", [CH, G, 32])
        ql = sb("ql", [CH, G * LH, LR])
        qmax = sb("qmax", [CH, G * LH])
        q_t = sb("q_t", [C, 2, CH])
        kx = sb("kx", [C + 1, 2, 32])
        m_t = sb("m_t", [C, 2, LH, LR])
        m_bd = sb("m_bd", [C, 2, C])
        base2 = sb("base2", [CH, G, C])
        w_i = sb("w_i", [CH, G])
        rank_w = sb("rank_w", [CH, G])
        w_sel = sb("w_sel", [CH, G])

        S = {}

        def sems(names):
            for n in names.split():
                S[n] = sem(n)

        sems("w_loaded consts_ready zeroed setup_mm setup_done setup_link")
        for n in NORMS:
            sems(f"ln_{n} pow_{n}")
        sems("x_loaded tok_ready tok_stored h0_ready h0_stored xt_ready xt_hi xt_split v_ready v_stored "
             "v_written v_ld0 v_ld1 g_ready g_hi_ready g_split scores_ready max_ready exp_done pt_ready pt_dve pt_act "
             "pv_ready ctx_norm ctx_wr0 ctx_wr1 ctx_ld0 ctx_ld1 wo_ready wo_added recip_done")
        sems("sp_waits pe_waits dve_waits")
        sems("xm_t xm_hi xm_split gate_ready gate_link gate_rank gate_exp comb_ready comb_stored cb_ready cb_stored ff1_ready "
             "relu_done ff2_ready prod_done prod_sum moe_ready moe_added")
        sems("l1_xt l1_hi l1_split l1_k l1_kb l1_klink l1_kexp l1_kt l1_kts l1_q l1_qlink l1_qexp "
             "l1_qts l1_g l1_gs l1_m l1_ms l1_mt l1_mts l1_attn l1_fx l1_x3b l1_zero")
        sems("l2_xt l2_hi l2_split l2_ff l2_gelu l2_out l2_h4 l2_base")
        sems("l3_xt l3_hi l3_split l3_w l3_wb l3_wi l3_wis l3_rank l3_ff l3_gelu l3_out l3_t l3_mul l3_fin l3_base "
             "l3_stored")
        v_ld = (S["v_ld0"], S["v_ld1"])
        ctx_wr, ctx_ld = (S["ctx_wr0"], S["ctx_wr1"]), (S["ctx_ld0"], S["ctx_ld1"])

        GATE_LINKS, KLINKS, QLINKS = 12, 3, 6

        SETUP = ["tok0", "tok1", "a0", "a1", "wv", "wo", "wg", "w1_0", "w1_1", "w1_2", "w1_3", "w2_0", "w2_1",
                 "wx", "bfull", "wqk", "qb", "kb", "vt", "u0", "u1", "u2", "u3", "b1m"]
        idx = {n: k for k, n in enumerate(SETUP)}

        def sbank(name):
            return bank[idx[name] % 8]

        def g_cols(g):
            c, m = g // 2, g % 2
            return slice(m * TOK + c * CH, m * TOK + (c + 1) * CH)

        def weight_loads():
            col = lambda v: v.rearrange("(p a) -> p a", a=1)
            L = []
            L.append((wtok_n, a["L0_tok_W"]))
            for k in range(2):
                w = slice(k * C, (k + 1) * C)
                L.append((wq_n[:, :, w], a["L0_attn_Wq"].rearrange("(n o) c -> o n c", n=HEADS)))
                L.append((wv_n[:, w], a["L0_attn_Wv"]))
                L.append((wg_n[:, w], a["L0_ffn_Wg"]))
                L.append((w1_n[:, :, w], a["L0_ffn_W1"].rearrange("e (k p) c -> p (e k) c", k=2)))
                L.append((wk_dup[:, k * C:(k + 1) * C], a["L0_attn_Wk"]))
                L.append((tok_b[k * C:(k + 1) * C, :], col(a["L0_tok_b"])))
                L.append((g1_dup[k * C:(k + 1) * C, :], col(a["L1_attn_ln1_g"])))
                L.append((g2_dup[k * C:(k + 1) * C, :], col(a["L1_attn_ln2_g"])))
                L.append((m1_n[k * C:(k + 1) * C, :], a["L1_attn_W1"]))
                L.append((f1_n[k * C:(k + 1) * C, :], a["L1_ffn_w1"]))
                L.append((wr_n[k * C:(k + 1) * C, :], a["L1_ffn_wr"]))
            L.append((wo_n, a["L0_attn_Wo"]))
            L.append((w2_n, a["L0_ffn_W2"].rearrange("(q r) d n -> (r d) q n", r=2)))
            L.append((b1_c[:, :], a["L0_ffn_b1"].rearrange("e (k p) -> p (e k)", k=2)))
            L.append((b2_c[:, :], a["L0_ffn_b2"].rearrange("(q r) d -> (r d) q", r=2)))
            L.append((bg_b[:, :], a["L0_ffn_bg"].partition_broadcast(CH)))
            L.append((wx_n[:, :], a["L1_attn_Wx"]))
            L.append((bx_c[:, :], a["L1_attn_bx"].rearrange("(k p) -> p k", k=2)))
            L.append((g1_aug[0:C, :], col(a["L1_attn_ln1_g"])))
            L.append((ln1b[:, :], col(a["L1_attn_ln1_b"])))
            L.append((ln2b[:, :], col(a["L1_attn_ln2_b"])))
            for i in range(4):
                r = slice(LD * i, LD * (i + 1))
                L.append((q1_n[r, :], a["L1_attn_Wq"]))
                L.append((k1_n[r, :], a["L1_attn_Wk"]))
                L.append((v1_n[r, :], a["L1_attn_Wv"]))
            L.append((wo1_n[:, :, :], a["L1_attn_Wo"].rearrange("(k p) o -> p k o", k=2)))
            L.append((bo_b[:, :], a["L1_attn_bo"].partition_broadcast(CH)))
            L.append((mb1_c[:, :], a["L1_attn_b1"].rearrange("(k p) -> p k", k=2)))
            L.append((m2_w[:, :, :], a["L1_attn_W2"].rearrange("(k p) o -> p k o", k=2)))
            L.append((mb2_b[:, :], a["L1_attn_b2"].partition_broadcast(CH)))
            L.append((fb1_c[:, :], a["L1_ffn_b1"].rearrange("(k p) -> p k", k=2)))
            L.append((f2_w[:, :, :], a["L1_ffn_w2"].rearrange("(k p) o -> p k o", k=2)))
            L.append((fb2_b[:, :], a["L1_ffn_b2"].partition_broadcast(CH)))
            L.append((br_b[:, :], a["L1_ffn_br"].partition_broadcast(CH)))
            return L

        N_LOADS = len(weight_loads())
        block = ctx.enter_context(nc.Block())

        @block.sync
        def _(sp):
            with nc.allow_non_contiguous_dma(reason="bias vectors, a few kB in all"):
                for dst, src in weight_loads()[0::2]:
                    sp.dma_start(dst, src).then_inc(S["w_loaded"], 16)
            sp.wait_ge(S["zeroed"], 1)

            def load_x(j):
                at_least(sp, S["tok_ready"], j)
                for m in range(2):
                    for ch in range(3):
                        p = IMG_ROW * m + PATCH * ch
                        src = a["x"].rearrange("(j m) c (r q) w -> j m c q r w", m=2, q=PATCH)[j, m, ch]
                        sp.dma_start(x_sb[p:p + PATCH, :, :], src).then_inc(S["x_loaded"], 16)

            def write_ctx(j, u):
                m, c = u // 2, u % 2
                at_least(sp, S["ctx_norm"], 4 * j + u + 1)
                sp.dma_start(ctx_dram[j, m, c * CH:(c + 1) * CH, :], ctx_sb[c][:, :]).then_inc(ctx_wr[c], 16)

            def read_ctx(j, m):
                for c in range(2):
                    sp.wait_ge(ctx_wr[c], 16 * (2 * j + m + 1))
                at_least(sp, S["wo_ready"], j)
                src = ctx_dram[j, m].rearrange("s n -> (s n)").rearrange("(k p t) -> p k t", k=4, t=TOK)
                sp.dma_start(ctx_r[m][:, :, :], src).then_inc(ctx_ld[m], 16)

            def write_v(j):
                sp.wait_ge(S["v_stored"], j + 1)
                sp.dma_start(v_dram[j].rearrange("m o s -> o m s"), v_lin[:, :, :]).then_inc(S["v_written"], 16)

            def read_v(j, m):
                wait_apart(sp, S["sp_waits"], S["v_written"], 16 * (j + 1))
                at_least(sp, S["pv_ready"], 4 * j - 2 + 2 * m)
                src = v_dram[j, m].rearrange("o s -> (o s)").rearrange("(k p d) -> p k d", k=2, d=C)
                sp.dma_start(v_tok[:, m, :, :], src).then_inc(v_ld[m], 16)

            def body(i, live):
                if live(1):
                    read_v(i - 1, 0)
                if live(2):
                    write_ctx(i - 2, 3)
                    read_ctx(i - 2, 1)
                if live(1):
                    read_v(i - 1, 1)
                if live(-1):
                    load_x(i + 1)
                if live(1):
                    write_ctx(i - 1, 0)
                    write_ctx(i - 1, 1)
                if live(0):
                    write_v(i)
                if live(1):
                    write_ctx(i - 1, 2)
                    read_ctx(i - 1, 0)

            load_x(0)
            for i in range(3):
                body(i, lambda lag, i=i: i - lag >= 0)
            with sp.Fori(3, NP - 1) as i:
                body(i, lambda lag: True)
            for i in range(NP - 1, NP + 2):
                body(i, lambda lag, i=i: i - lag < NP)

            with sp.Fori(0, NP) as j:
                sp.wait_ge(S["l3_fin"], j + 1)
                for c in range(2):
                    dst = out.rearrange("(j m) (c p) d -> j c p m d", m=2, c=2)[j, c]
                    sp.dma_start(dst, o_sb[:, 2 * c:2 * c + 2, :]).then_inc(S["l3_stored"], 16)
            sp.wait_ge(S["l3_stored"], 32 * NP)

        @block.gpsimd
        def _(pool):
            k = 0
            for t, v in ((ident, 0.0), (ident2, 0.0), (tie_tok, 1.0), (tie_exp, 1.0), (half, -0.5), (eps, EPS), (pick, 0.0)):
                nc.gpsimd.memset(t[:], v).then_inc(S["consts_ready"], 1)
                k += 1
            pool.wait_ge(S["consts_ready"], k)
            nc.gpsimd.affine_select(out=ident[:], in_=ident[:], compare_op=ALU.not_equal, fill=1.0, base=0,
                                    pattern=[[-1, 128]], channel_multiplier=1).then_inc(S["consts_ready"], 1)
            nc.gpsimd.affine_select(out=tie_tok[:], in_=tie_tok[:], compare_op=ALU.is_gt, fill=0.0, base=0,
                                    pattern=[[CH, 2], [-1, TOK]], channel_multiplier=1).then_inc(S["consts_ready"], 1)
            nc.gpsimd.affine_select(out=tie_exp[:], in_=tie_exp[:], compare_op=ALU.is_gt, fill=0.0, base=0,
                                    pattern=[[1, 8], [-1, 8]], channel_multiplier=0).then_inc(S["consts_ready"], 1)
            for k, base in ((10, 0), (12, -C)):
                pool.wait_ge(S["consts_ready"], k)
                nc.gpsimd.affine_select(out=pick[:], in_=pick[:], compare_op=ALU.not_equal, fill=1.0,
                                        base=base // 2, pattern=[[-2, EP], [-1, 2], [0, C]],
                                        channel_multiplier=1).then_inc(S["consts_ready"], 1)
                nc.gpsimd.affine_select(out=ident2[:], in_=ident2[:], compare_op=ALU.not_equal, fill=1.0, base=base,
                                        pattern=[[-1, C]], channel_multiplier=1).then_inc(S["consts_ready"], 1)

            def rstd_pow(j, n):
                pool.wait_ge(S[f"ln_{n}"], LN_LINKS * j + 2)
                at_least(pool, S[f"pow_{n}"], 2 * j)
                nc.gpsimd.tensor_tensor(ve[n][:, :], mv[n][:, :, 1], eps[:, :], ALU.add).then_inc(S[f"pow_{n}"], 1)
                pool.wait_ge(S[f"pow_{n}"], 2 * j + 1)
                nc.gpsimd.tensor_tensor(rstd[n][:, :], ve[n][:, :], half[:, :], ALU.pow).then_inc(S[f"pow_{n}"], 1)

            pool.wait_ge(S["consts_ready"], 14)
            with pool.Fori(0, NP) as j:
                rstd_pow(j, "a")

            def gate_ranks(j):
                pool.wait_ge(S["gate_link"], GATE_LINKS * j + 5)
                nc.gpsimd.tensor_tensor(tied[:, :, :, :], tied[:, :, :, :],
                                        tie_exp[:, :, :].unsqueeze(1).to_broadcast([CH, G, EXPERTS, EXPERTS]),
                                        ALU.mult).then_inc(S["gate_rank"], 1)
                pool.wait_ge(S["gate_rank"], 2 * j + 1)
                nc.gpsimd.tensor_tensor(above[:, :, :, :], above[:, :, :, :], tied[:, :, :, :],
                                        ALU.add).then_inc(S["gate_rank"], 1)

            def sum_experts(j, ep):
                pool.wait_ge(S["prod_done"], EP * j + ep + 1)
                if ep > 1:
                    pool.wait_ge(S["prod_sum"], 3 * j + ep - 1)
                nc.gpsimd.tensor_tensor(prod[:, 0, :], prod[:, 0, :], prod[:, ep, :],
                                        ALU.add).then_inc(S["prod_sum"], 1)

            def base_mlp(j):
                pool.wait_ge(S["l1_fx"], j + 1)
                at_least(pool, S["l2_h4"], j)
                nc.gpsimd.tensor_tensor(base2[:, :, :], h[:, j], fx[:, :, :], ALU.add).then_inc(S["l2_base"], 1)
                pool.wait_ge(S["l2_base"], 2 * j + 1)
                nc.gpsimd.tensor_tensor(base2[:, :, :], base2[:, :, :],
                                        mb2_b[:, :].unsqueeze(1).to_broadcast([CH, G, C]),
                                        ALU.add).then_inc(S["l2_base"], 1)

            def base_ffn(j):
                pool.wait_ge(S["ln_6"], LN_LINKS * (j + 1))
                at_least(pool, S["l3_fin"], j)
                nc.gpsimd.tensor_tensor(base3[:, :, :], x4[:, :, 0, :], h4[:, :, :], ALU.add).then_inc(S["l3_base"], 1)

            def base_attn(j):
                pool.wait_ge(S["ln_3"], LN_LINKS * (j + 1))
                at_least(pool, S["l1_fx"], j)
                nc.gpsimd.tensor_tensor(x3b[:, :, :], x3[:, :, :],
                                        bo_b[:, :].unsqueeze(1).to_broadcast([CH, G, C]),
                                        ALU.add).then_inc(S["l1_x3b"], 1)

            def route(j):
                pool.wait_ge(S["l3_t"], j + 1)
                pool.wait_ge(S["l3_rank"], 9 * j + 9)
                nc.gpsimd.tensor_tensor(o_t[:, :, :], o_t[:, :, :],
                                        w_sel[:, :].unsqueeze(2).to_broadcast([CH, G, C]),
                                        ALU.mult).then_inc(S["l3_mul"], 1)

            def body(i, live):
                def at(lag, step, *args):
                    if live(lag):
                        step(i - lag, *args)

                at(1, sum_experts, 1)
                at(0, rstd_pow, "m")
                at(1, sum_experts, 2)
                at(4, base_ffn)
                at(1, sum_experts, 3)
                at(0, gate_ranks)
                at(1, rstd_pow, "3")
                at(2, base_mlp)
                at(2, rstd_pow, "5")
                at(1, rstd_pow, "4")
                at(1, base_attn)
                at(3, rstd_pow, "6")
                at(4, route)

            run_lagged(pool, NP, DEPTH, body)

        @block.tensor
        def _(pe):
            pe.wait_ge(S["w_loaded"], 16 * N_LOADS)
            pe.wait_ge(S["consts_ready"], 14)

            def begin(name, *needs):
                at_least(pe, S["setup_done"], idx[name] - 7)
                for n in needs:
                    pe.wait_ge(S["setup_done"], idx[n] + 1)

            def done(ins):
                ins.then_inc(S["setup_mm"], 1)

            def mm(o, l, r, start=True, stop=True):
                return nc.tensor.matmul(o, l, r, start=start, stop=stop)

            def flat(t):
                return t[:, :, :, :].rearrange("p g k c -> p g (k c)")

            w_view = wtok_n.rearrange("e (k q) -> e q k", q=PATCH)
            for b in range(2):
                begin(f"tok{b}")
                o = sbank(f"tok{b}")[0:48, :].rearrange("p (q e) -> p q e", e=C)
                for q in range(8):
                    last = nc.tensor.transpose(o[:, q, :], w_view[:, 8 * b + q, :], ident[0:C, 0:C])
                done(last)
            for b in range(2):
                begin(f"a{b}")
                for k in range(4):
                    last = mm(sbank(f"a{b}")[:, k * 128:(k + 1) * 128], wq_n[:, 4 * b + k, :], wk_dup[:, :])
                done(last)
            begin("wv")
            done(nc.tensor.transpose(sbank("wv")[:, 0:C], wv_n[:, :], ident[0:C, 0:C]))
            begin("wo")
            for k in range(4):
                last = nc.tensor.transpose(sbank("wo")[:, k * C:(k + 1) * C], wo_n[:, k * 128:(k + 1) * 128],
                                           ident[0:C, 0:C])
            done(last)
            begin("wg")
            done(nc.tensor.transpose(sbank("wg")[:, 0:EXPERTS], wg_n[:, :], ident[0:EXPERTS, 0:EXPERTS]))
            for b in range(4):
                begin(f"w1_{b}")
                for k in range(4):
                    last = nc.tensor.transpose(sbank(f"w1_{b}")[:, k * 128:(k + 1) * 128],
                                               w1_n[:, 4 * b + k, :], ident[:, :])
                done(last)
            for b in range(2):
                begin(f"w2_{b}")
                for k in range(4):
                    ep, hc = 2 * b + k // 2, k % 2
                    last = nc.tensor.transpose(sbank(f"w2_{b}")[:, k * 128:(k + 1) * 128],
                                               w2_n[:, ep, hc * 128:(hc + 1) * 128], ident[:, :])
                done(last)
            begin("wx")
            for k in range(2):
                last = nc.tensor.transpose(sbank("wx")[:, k * C:(k + 1) * C], wx_n[:, k * 128:(k + 1) * 128],
                                           ident[0:C, 0:C])
            done(last)
            begin("bfull")
            for k in range(2):
                last = mm(sbank("bfull")[:, k:k + 1], wx_n[:, k * 128:(k + 1) * 128], ln1b[:, :])
            done(last)
            begin("wqk", "wx", "bfull")
            for t, bd in enumerate((bdq, bdk)):
                for k in range(2):
                    last = mm(sbank("wqk")[:, t * 32:(t + 1) * 32], wx_dup[:, k, :], bd[:, k, :],
                              start=(k == 0), stop=(k == 1))
            done(last)
            begin("qb")
            for k in range(2):
                last = mm(sbank("qb")[0:CH, 0:32], wxa[:, k, C:C + 1].to_broadcast([128, CH]), bdq[:, k, :],
                          start=(k == 0), stop=(k == 1))
            done(last)
            begin("kb")
            for k in range(2):
                last = mm(sbank("kb")[0:32, 0:1], bdk[:, k, :], wxa[:, k, C:C + 1], start=(k == 0), stop=(k == 1))
            done(last)
            begin("vt")
            for k in range(2):
                last = mm(sbank("vt")[:, k * (C + 1):(k + 1) * (C + 1)], bdv[:, :], wxa[:, k, :])
            done(last)
            for i in range(4):
                begin(f"u{i}", "vt")
                r = slice(LD * i, LD * (i + 1))
                for k in range(2):
                    last = mm(sbank(f"u{i}")[0:C + 1, k * C:(k + 1) * C], vt[r, k, :], wo1_n[r, k, :])
                done(last)
            begin("b1m")
            for k in range(2):
                last = mm(sbank("b1m")[:, k:k + 1], m1_n[0:C, k * 128:(k + 1) * 128], ln2b[:, :])
            done(last)
            pe.wait_ge(S["setup_done"], len(SETUP) + 1)

            def mm2(o, hi, lo, x):
                mm(o, hi, x, start=True, stop=False)
                return mm(o, lo, x, start=False, stop=True)

            def tok_part(j, q0, q1):
                if q0 == 0:
                    pe.wait_ge(S["x_loaded"], 96 * (j + 1))
                    at_least(pe, S["xt_split"], j)
                for q in range(q0, q1):
                    last = mm(bank[0][:, 0:TOK], w_tok[:, q, :], x_sb[:, :, q::PATCH],
                              start=(q == 0), stop=(q == PATCH - 1))
                if q1 == PATCH:
                    last.then_inc(S["tok_ready"], 1)

            def h0_turn(j):
                pe.wait_ge(S["tok_stored"], j + 1)
                for c in range(2):
                    last = nc.tensor.transpose(bank[0][0:CH, 256 + c * 128:256 + (c + 1) * 128],
                                               h_t[:, c * CH:(c + 1) * CH], ident[:, :])
                last.then_inc(S["h0_ready"], 1)

            def turn_norm(y, o, ln, j, ready):
                pe.wait_ge(S[ln], LN_LINKS * (j + 1))
                for g in range(G):
                    last = nc.tensor.transpose(o[:, g_cols(g)], y[:, g, 0:2 * C], ident[0:CH, 0:CH])
                last.then_inc(S[ready], 1)

            def v_mm(j):
                pe.wait_ge(S["xt_split"], j + 1)
                at_least(pe, S["g_split"], 8 * j - 1)
                mm2(bank[2][0:C, 0:PAIR], wv_hi[:, :], wv_lo[:, :], x_a[:, :]).then_inc(S["v_ready"], 1)

            def g_mm(j, s):
                m, k = s // 4, s % 4
                if s == 0:
                    pe.wait_ge(S["v_stored"], j + 1)
                else:
                    at_least(pe, S["g_split"], 8 * j + s - 1)
                for n in (2 * k, 2 * k + 1):
                    w = slice(n * 128, (n + 1) * 128)
                    last = mm2(bank[2 + s % 2][:, (n % 2) * TOK:(n % 2 + 1) * TOK], a_hi[:, w], a_lo[:, w],
                               x_a[:, m * TOK:(m + 1) * TOK])
                last.then_inc(S["g_ready"], 1)

            def scores(j, u, k):
                m, c, s = u // 2, u % 2, 4 * u + k
                pe.wait_ge(S["g_split"], 8 * j + 4 * m + k + 1)
                at_least(pe, S["exp_done"], 16 * j + s - 1)
                if s == 0:
                    at_least(pe, S["wo_added"], j - 1)
                for n in (2 * k, 2 * k + 1):
                    r = slice(c * CH, (c + 1) * CH)
                    last = mm2(bank[4 + s % 2][0:CH, (n % 2) * TOK:(n % 2 + 1) * TOK], g_hi[m][:, n, r],
                               g_lo[m][:, n, r], x_a[:, m * TOK:(m + 1) * TOK])
                last.then_inc(S["scores_ready"], 1)

            PT_BANK = (1, 6)

            def turn_probs(j, u, k):
                c, tc, hh = u % 2, k % 2, k // 2
                t = 4 * u + k
                if k == 0:
                    pe.wait_ge(S["exp_done"], 16 * j + 4 * u + 4)
                at_least(pe, S["pt_act" if t % 2 else "pt_dve"], 8 * j + t // 2)
                p = prob[c][0:CH, :].rearrange("p (n t) -> p n t", n=HEADS)
                for q in range(4):
                    last = nc.tensor.transpose(bank[PT_BANK[t % 2]][0:CH, q * CH:(q + 1) * CH],
                                               p[:, 4 * hh + q, tc * CH:(tc + 1) * CH], ident[0:CH, 0:CH])
                last.then_inc(S["pt_ready"], 1)

            def weigh_v(j, u, k):
                m, c = u // 2, u % 2
                if k == 0:
                    pe.wait_ge(v_ld[m], 16 * (j + 1))
                    at_least(pe, S["ctx_norm"], 4 * j + u)
                if k % 2 == 0:
                    pe.wait_ge(S["pt_dve"], 8 * j + 2 * u + k // 2 + 1)
                    pe.wait_ge(S["pt_act"], 8 * j + 2 * u + k // 2 + 1)
                pt = prob_t[c][0:CH, :].rearrange("p (k n s) -> p k n s", k=2, n=HEADS)
                for n in (2 * k, 2 * k + 1):
                    for tc in range(2):
                        last = mm(bank[7][0:CH, n * C:(n + 1) * C], pt[:, tc, n, :], v_tok[:, m, tc, :],
                                  start=(tc == 0), stop=(tc == 1))
                if k == 3:
                    last.then_inc(S["pv_ready"], 1)

            def out_proj(j, g):
                c, m = g // 2, g % 2
                if g == 0:
                    for mm_ in range(2):
                        pe.wait_ge(ctx_ld[mm_], 16 * (j + 1))
                    pe.wait_ge(S["exp_done"], min(16 * j + 31, 16 * NP) if isinstance(j, int) else 16 * j + 31)
                for k in range(4):
                    last = mm(bank[4][0:CH, g * C:(g + 1) * C], ctx_r[m][:, k, c * CH:(c + 1) * CH], wo_t[:, k, :],
                              start=(k == 0), stop=(k == 3))
                if g == G - 1:
                    last.then_inc(S["wo_ready"], 1)

            def body1(i, live):
                a, o = i - 1, i - 2

                def steps(order, u):
                    for op, k in order:
                        if op == "S" and live(1):
                            scores(a, u, k)
                        elif op == "T" and live(1):
                            turn_probs(a, u - 1, k)
                        elif op == "W" and live(1):
                            weigh_v(a, u - 2, k)
                        elif op == "L" and live(2):
                            weigh_v(o, 3, k)
                        elif op == "P" and live(0):
                            tok_part(i, 2 * k, 2 * k + 2)
                        elif op == "H" and live(0):
                            h0_turn(i)
                        elif op == "N" and live(0):
                            turn_norm(flat(y_a), bank[0], "ln_a", i, "xt_ready")
                        elif op == "V" and live(0):
                            v_mm(i)
                        elif op == "G" and live(0):
                            g_mm(i, k)
                        elif op == "O" and live(2):
                            out_proj(o, k)

                steps([("S", 0), ("P", 0), ("L", 0), ("S", 1), ("P", 1), ("L", 1), ("S", 2), ("P", 2), ("L", 2),
                       ("S", 3), ("P", 3), ("L", 3)], 0)
                steps([("S", 0), ("P", 4), ("S", 1), ("P", 5), ("T", 0), ("S", 2), ("T", 1), ("P", 6), ("S", 3),
                       ("T", 2), ("P", 7), ("T", 3)], 1)
                steps([("S", 0), ("H", 0), ("W", 0), ("S", 1), ("W", 1), ("T", 0), ("S", 2), ("T", 1), ("W", 2),
                       ("S", 3), ("T", 2), ("W", 3), ("T", 3)], 2)
                steps([("S", 0), ("W", 0), ("S", 1), ("W", 1), ("T", 0), ("S", 2), ("T", 1), ("W", 2),
                       ("S", 3), ("T", 2), ("W", 3), ("T", 3)], 3)
                steps([("N", 0), ("W", 0), ("W", 1), ("T", 0), ("T", 1), ("V", 0), ("G", 0), ("W", 2), ("G", 1),
                       ("T", 2), ("W", 3), ("G", 2), ("O", 0), ("G", 3), ("T", 3), ("G", 4), ("O", 1), ("G", 5),
                       ("O", 2), ("G", 6), ("O", 3), ("G", 7)], 4)

            run_lagged(pe, NP, 2, body1)

            def gate_mm(j):
                pe.wait_ge(S["xm_split"], j + 1)
                for g in range(G):
                    o = bank[4][0:CH, PAIR + g * EXPERTS:PAIR + (g + 1) * EXPERTS]
                    mm(o, x_m[:, g_cols(g)], wg_hi[:, :], start=True, stop=False)
                    last = mm(o, x_m[:, g_cols(g)], wg_lo[:, :], start=False, stop=True)
                last.then_inc(S["gate_ready"], 1)

            def turn_gate(j):
                wait_apart(pe, S["pe_waits"], S["gate_link"], GATE_LINKS * (j + 1))
                for g in range(G):
                    last = nc.tensor.transpose(bank[4][0:C, g_cols(g)], comb2[:, g, :], ident[0:CH, 0:CH])
                last.then_inc(S["comb_ready"], 1)

            def spread_gate(j, ep):
                if ep == 0:
                    pe.wait_ge(S["comb_stored"], j + 1)
                else:
                    pe.wait_ge(S["cb_stored"], EP * j + ep)
                mm(bank[4][:, 0:PAIR], pick_r[:, ep, :], comb_t[:, :]).then_inc(S["cb_ready"], 1)

            def ff1(j, u):
                for q in (2 * u, 2 * u + 1):
                    if q == 0:
                        pe.wait_ge(S["xm_split"], j + 1)
                    at_least(pe, S["relu_done"], HCH * j + q - 1)
                    mm2(bank[q % 2][:, 0:PAIR], w1_hi[:, q, :], w1_lo[:, q, :], x_m[:, :]).then_inc(S["ff1_ready"], 1)

            def ff2(j, ep):
                pe.wait_ge(S["relu_done"], HCH * j + 4 * ep + 4)
                if ep == 0:
                    at_least(pe, S["moe_added"], j)
                at_least(pe, S["prod_done"], EP * j + ep - 1)
                for hc in range(2):
                    for r in range(2):
                        last = mm(bank[2 + ep % 2][r * C:(r + 1) * C, 0:PAIR], w2_t[:, ep, hc, r * C:(r + 1) * C],
                                  hid[:, ep % 2, 2 * r + hc, :], start=(hc == 0), stop=(hc == 1))
                last.then_inc(S["ff2_ready"], 1)

            def moe_out(j):
                pe.wait_ge(S["prod_sum"], 3 * j + 3)
                for g in range(G):
                    last = mm(bank[2][0:CH, g * C:(g + 1) * C], prod[:, 0, g_cols(g)], ident2[:, :])
                last.then_inc(S["moe_ready"], 1)

            def l1_k(j):
                pe.wait_ge(S["l1_split"], j + 1)
                mm2(bank[5][0:32, 0:PAIR], wqk_hi[:, 32:64], wqk_lo[:, 32:64], x_l1[:, :]).then_inc(S["l1_k"], 1)

            def l1_q(j):
                pe.wait_ge(S["l1_kb"], j + 1)
                for g in range(G):
                    o = bank[5][0:CH, g * 32:(g + 1) * 32]
                    mm(o, x_l1[:, g_cols(g)], wqk_hi[:, 0:32], start=True, stop=False)
                    last = mm(o, x_l1[:, g_cols(g)], wqk_lo[:, 0:32], start=False, stop=True)
                last.then_inc(S["l1_q"], 1)

            def l1_kt(j):
                wait_apart(pe, S["pe_waits"], S["l1_klink"], KLINKS * (j + 1))
                for g in range(G):
                    c, m = g // 2, g % 2
                    last = nc.tensor.transpose(bank[5][0:CH, 128 + g * 32:128 + (g + 1) * 32],
                                               kl[:, m, c * CH:(c + 1) * CH], ident[0:32, 0:32])
                last.then_inc(S["l1_kt"], 1)

            def l1_g(j):
                pe.wait_ge(S["l1_kts"], j + 1)
                for m in range(2):
                    for c in range(2):
                        last = mm(bank[5][0:C + 1, 256 + m * 32:256 + (m + 1) * 32], n3[:, 2 * c + m, C:2 * C + 1],
                                  k_t[:, 2 * c + m, :], start=(c == 0), stop=(c == 1))
                last.then_inc(S["l1_g"], 1)

            def l1_qt(j):
                pe.wait_ge(S["l1_gs"], j + 1)
                wait_apart(pe, S["pe_waits"], S["l1_qlink"], QLINKS * (j + 1))
                q = ql[:, :, :].rearrange("p (c n) r -> p c (n r)", c=2)
                for c in range(2):
                    last = nc.tensor.transpose(bank[5][0:C, c * CH:(c + 1) * CH], q[:, c, :], ident[0:CH, 0:CH])

            def l1_m(j):
                for n in range(LH):
                    last = mm(bank[5][0:C, 320 + n * 8:320 + (n + 1) * 8], u_w[:, n, :],
                              kx[:, :, n * LR:(n + 1) * LR])
                last.then_inc(S["l1_m"], 1)

            def l1_mt(j):
                wait_apart(pe, S["pe_waits"], S["l1_ms"], j + 1)
                nc.tensor.transpose(bank[5][0:C, 384:384 + C], m_t[:, :, :, :].rearrange("p m n r -> p (m n r)"),
                                    ident[0:C, 0:C]).then_inc(S["l1_mt"], 1)

            def l1_attn(j):
                pe.wait_ge(S["l1_mts"], 2 * (j + 1))
                pe.wait_ge(S["l1_qts"], j + 1)
                for c in range(2):
                    last = mm(bank[5][0:CH, c * 128:(c + 1) * 128], q_t[:, c, :],
                              m_bd[:, :, :].rearrange("p m o -> p (m o)"))
                last.then_inc(S["l1_attn"], 1)

            def mlp_in(j, k, b, start, ready, gelu, hi, lo, x):
                if k == 0:
                    pe.wait_ge(S[start], j + 1)
                else:
                    pe.wait_ge(S[gelu], 2 * j + 1)
                mm2(bank[b][:, 0:PAIR], hi[:, k * 128:(k + 1) * 128], lo[:, k * 128:(k + 1) * 128],
                    x[:, :]).then_inc(S[ready], 1)

            def mlp_out(j, b, gelu, hid_t, w, ready):
                pe.wait_ge(S[gelu], 2 * j + 2)
                for g in range(G):
                    for k in range(2):
                        last = mm(bank[b][0:CH, g * C:(g + 1) * C], hid_t[:, k, g_cols(g)], w[:, k, :],
                                  start=(k == 0), stop=(k == 1))
                last.then_inc(S[ready], 1)

            def l3_w(j):
                pe.wait_ge(S["l3_split"], j + 1)
                mm2(bank[7][0:CH, 0:PAIR], wr_hi[:, :], wr_lo[:, :], x_l3[:, :]).then_inc(S["l3_w"], 1)

            def l3_wi(j):
                wait_apart(pe, S["pe_waits"], S["l3_wb"], j + 1)
                for g in range(G):
                    last = nc.tensor.transpose(bank[7][0:CH, 400 + g:401 + g], w_b[0:1, g_cols(g)], ident[0:1, 0:1])
                last.then_inc(S["l3_wi"], 1)

            def turn_xm(j):
                at_least(pe, S["cb_stored"], EP * j)
                turn_norm(flat(y_m), bank[4], "ln_m", j, "xm_t")

            def turn_l1(j):
                at_least(pe, S["l1_fx"], j)
                turn_norm(n3, bank[5], "ln_4", j, "l1_xt")

            def turn_l2(j):
                at_least(pe, S["l2_h4"], j)
                turn_norm(flat(y_2), bank[6], "ln_5", j, "l2_xt")

            def turn_l3(j):
                at_least(pe, S["l3_t"], j)
                turn_norm(flat(x4), bank[7], "ln_6", j, "l3_xt")

            def l1_qm(j):
                l1_qt(j)
                l1_m(j)

            def l2_in(j, k):
                mlp_in(j, k, 6, "l2_split", "l2_ff", "l2_gelu", m1_hi, m1_lo, x_l2)

            def l2_out(j):
                mlp_out(j, 6, "l2_gelu", hid2, m2_w, "l2_out")

            def l3_in(j, k):
                mlp_in(j, k, 7, "l3_wis", "l3_ff", "l3_gelu", f1_hi, f1_lo, x_l3)

            def l3_out(j):
                mlp_out(j, 7, "l3_gelu", hid3, f2_w, "l3_out")

            def body2(i, live):
                def at(lag, step, *args):
                    if live(lag):
                        step(i - lag, *args)

                at(1, spread_gate, 2)
                at(2, l1_k)
                at(1, ff1, 5)
                at(2, l1_q)
                at(3, l2_in, 0)
                at(1, ff1, 6)
                at(1, ff2, 2)
                at(4, turn_l3)
                at(1, spread_gate, 3)
                at(1, ff1, 7)
                at(2, l1_kt)
                at(0, turn_xm)
                at(1, ff2, 3)
                at(2, l1_g)
                at(3, l2_in, 1)
                at(2, l1_qm)
                at(4, l3_w)
                at(1, moe_out)
                at(2, l1_mt)
                at(4, l3_wi)
                at(0, gate_mm)
                at(0, ff1, 0)
                at(2, l1_attn)
                at(3, l2_out)
                at(0, ff1, 1)
                at(4, l3_in, 0)
                at(0, ff2, 0)
                at(4, l3_in, 1)
                at(0, turn_gate)
                at(0, ff1, 2)
                at(4, l3_out)
                at(0, ff1, 3)
                at(2, turn_l2)
                at(0, spread_gate, 0)
                at(0, ff1, 4)
                at(0, ff2, 1)
                at(1, turn_l1)
                at(0, spread_gate, 1)

            pe.wait_ge(S["wo_added"], NP)
            run_lagged(pe, NP, DEPTH, body2)

        @block.scalar
        def _(act):
            with nc.allow_non_contiguous_dma(reason="bias vectors, a few kB in all"):
                for dst, src in weight_loads()[1::2]:
                    act.dma_start(dst, src).then_inc(S["w_loaded"], 16)
            act.wait_ge(S["w_loaded"], 16 * N_LOADS)

            def hi_part(j, dst, b, ready, hi, free, free_at):
                act.wait_ge(S[ready], j + 1)
                at_least(act, S[free], free_at)
                nc.scalar.activation(dst[:, :], bank[b][:, 0:PAIR], ACT.Copy).then_inc(S[hi], 1)

            def exps(j, u, k):
                c, s = u % 2, 4 * u + k
                if k == 0:
                    at_least(act, S["pt_ready"], 16 * j + 4 * u - 4)
                    at_least(act, S["recip_done"], 4 * j + u - 1)
                act.wait_ge(S["max_ready"], 16 * j + s + 1)
                for n in (2 * k, 2 * k + 1):
                    last = nc.scalar.activation(prob[c][0:CH, n * TOK:(n + 1) * TOK],
                                                bank[4 + s % 2][0:CH, (n % 2) * TOK:(n % 2 + 1) * TOK], ACT.Exp,
                                                bias=nmax[c][:, n:n + 1], accum_out=psum_[c][:, n:n + 1])
                last.then_inc(S["exp_done"], 1)

            def store_probs(j, u, k):
                c, q = u % 2, 2 + k // 2
                if k == 1:
                    at_least(act, S["pv_ready"], 4 * j + u - 1)
                act.wait_ge(S["pt_ready"], 16 * j + 4 * u + k + 1)
                nc.scalar.activation(prob_t[c][0:CH, q * 4 * CH:(q + 1) * 4 * CH], bank[6][0:CH, 0:4 * CH],
                                     ACT.Copy).then_inc(S["pt_act"], 1)

            def store_g_hi(j, s):
                m, k = s // 4, s % 4
                act.wait_ge(S["g_ready"], 8 * j + s + 1)
                nc.scalar.activation(g_hi[m][:, 2 * k:2 * k + 2, :],
                                     bank[2 + s % 2][:, 0:PAIR].rearrange("p (n t) -> p n t", n=2),
                                     ACT.Copy).then_inc(S["g_hi_ready"], 1)

            def store_tok(j):
                act.wait_ge(S["tok_ready"], j + 1)
                at_least(act, S["h0_ready"], j)
                nc.scalar.activation(h_t[:, :], bank[0][:, 0:TOK], ACT.Identity,
                                     bias=tok_b[:, :]).then_inc(S["tok_stored"], 1)

            def body1(i, live):
                a = i - 1
                for u in range(4):
                    for k in range(4):
                        if live(1):
                            exps(a, u, k)
                            if u and k % 2:
                                store_probs(a, u - 1, k)
                    if live(0) and u == 1:
                        store_tok(i)
                if live(0):
                    hi_part(i, x_a, 0, "xt_ready", "xt_hi", "scores_ready", 16 * i)
                if live(1):
                    store_probs(a, 3, 1)
                for s in range(8):
                    if live(1) and s == 4:
                        store_probs(a, 3, 3)
                    if live(0):
                        store_g_hi(i, s)

            run_lagged(act, NP, 2, body1)

            def relu(j, q):
                ep = q // 4
                act.wait_ge(S["ff1_ready"], HCH * j + q + 1)
                if q % 4 == 0:
                    at_least(act, S["ff2_ready"], EP * j + ep - 1)
                nc.scalar.activation(hid[:, ep % 2, q % 4, :], bank[q % 2][:, 0:PAIR], ACT.Relu,
                                     bias=b1_c[:, q:q + 1]).then_inc(S["relu_done"], 1)

            def store_comb(j):
                act.wait_ge(S["comb_ready"], j + 1)
                at_least(act, S["cb_ready"], EP * j)
                nc.scalar.activation(comb_t[:, :], bank[4][0:C, 0:PAIR], ACT.Copy).then_inc(S["comb_stored"], 1)

            def store_gate(j, ep):
                act.wait_ge(S["cb_ready"], EP * j + ep + 1)
                at_least(act, S["prod_done"], EP * (j - 1) + ep + 1)
                nc.scalar.activation(comb_b[:, ep, :], bank[4][:, 0:PAIR], ACT.Copy).then_inc(S["cb_stored"], 1)

            def k_bias_add(j):
                act.wait_ge(S["l1_k"], j + 1)
                at_least(act, S["l1_kt"], j)
                nc.scalar.activation(kl[:, :, :], bank[5][0:32, 0:PAIR].rearrange("p (m t) -> p m t", m=2),
                                     ACT.Identity, bias=k_bias[:, :]).then_inc(S["l1_kb"], 1)

            def k_exp(j):
                act.wait_ge(S["l1_klink"], KLINKS * j + 1)
                for m in range(2):
                    last = nc.scalar.activation(kl[:, m, :], kl[:, m, :], ACT.Exp, bias=kmax[:, m:m + 1],
                                                accum_out=ksum[:, m:m + 1])
                last.then_inc(S["l1_kexp"], 1)

            def q_exp(j):
                act.wait_ge(S["l1_qlink"], QLINKS * j + 3)
                nc.scalar.activation(ql[:, :, :], ql[:, :, :], ACT.Exp).then_inc(S["l1_qexp"], 1)

            def gate_exp(j):
                act.wait_ge(S["gate_link"], GATE_LINKS * j + 3)
                nc.scalar.activation(gexp[:, :, :], gexp[:, :, :], ACT.Exp).then_inc(S["gate_exp"], 1)

            def router_bias(j):
                act.wait_ge(S["l3_w"], j + 1)
                at_least(act, S["l3_rank"], 9 * j)
                nc.scalar.activation(w_b[:, :], bank[7][0:CH, 0:PAIR], ACT.Identity,
                                     bias=br_b[:, :]).then_inc(S["l3_wb"], 1)

            def gelu(j, k, b, ff, done, hid_t, bias, func, out_sem):
                act.wait_ge(S[ff], 2 * j + k + 1)
                if k == 0:
                    at_least(act, S[out_sem], j)
                nc.scalar.activation(hid_t[:, k, :], bank[b][:, 0:PAIR], func,
                                     bias=bias[:, k:k + 1]).then_inc(S[done], 1)

            def l2_gelu(j, k):
                gelu(j, k, 6, "l2_ff", "l2_gelu", hid2, m1_bias, ACT.Gelu, "l2_out")

            def l3_gelu(j, k):
                gelu(j, k, 7, "l3_ff", "l3_gelu", hid3, fb1_c, ACT.Gelu_apprx_tanh, "l3_out")

            def hi_xm(j):
                hi_part(j, x_m, 4, "xm_t", "xm_hi", "ff1_ready", HCH * j)

            def hi_l1(j):
                hi_part(j, x_l1, 5, "l1_xt", "l1_hi", "l1_q", j)

            def hi_l2(j):
                hi_part(j, x_l2, 6, "l2_xt", "l2_hi", "l2_ff", 2 * j)

            def hi_l3(j):
                hi_part(j, x_l3, 7, "l3_xt", "l3_hi", "l3_ff", 2 * j)

            def body2(i, live):
                def at(lag, step, *args):
                    if live(lag):
                        step(i - lag, *args)

                at(2, k_bias_add)
                at(1, relu, 10)
                at(1, relu, 11)
                at(2, k_exp)
                at(1, relu, 12)
                at(1, store_gate, 2)
                at(1, relu, 13)
                at(2, q_exp)
                at(1, store_gate, 3)
                at(4, hi_l3)
                at(1, relu, 14)
                at(1, relu, 15)
                at(3, l2_gelu, 0)
                at(0, hi_xm)
                at(4, router_bias)
                at(3, l2_gelu, 1)
                at(0, relu, 0)
                at(0, relu, 1)
                at(0, gate_exp)
                at(0, relu, 2)
                at(0, relu, 3)
                at(4, l3_gelu, 0)
                at(4, l3_gelu, 1)
                at(0, relu, 4)
                at(0, relu, 5)
                at(0, relu, 6)
                at(0, store_comb)
                at(0, relu, 7)
                at(0, relu, 8)
                at(0, relu, 9)
                at(1, hi_l1)
                at(0, store_gate, 0)
                at(2, hi_l2)
                at(0, store_gate, 1)

            run_lagged(act, NP, DEPTH, body2)

        @block.vector
        def _(dve):
            V = nc.vector

            def tt(o, x, y, op):
                return V.tensor_tensor(o, x, y, op)

            V.memset(x_sb[32:IMG_ROW, :, :], 0.0).then_inc(S["zeroed"], 1)
            zero = Links(dve, S["setup_link"], 0, 0)
            for t in (w_tok[:], bdq[:], bdk[:], bdv[:], m_bd[:]):
                zero.mark(V.memset(t, 0.0))
            zero.mark(V.memset(comb2[:], 0.0))
            zero.mark(V.memset(n3[:, :, 2 * C:2 * C + 1], 1.0))
            zero.mark(V.memset(g1_aug[C:C + 1, :], 1.0))
            zero.wait()
            dve.wait_ge(S["consts_ready"], 14)
            zero.mark(V.tensor_copy(pick_r[:, :, :], pick[:, :, :, :].rearrange("p q r d -> p q (r d)")))
            dve.wait_ge(S["w_loaded"], 16 * N_LOADS)
            for i in range(4):
                r = slice(LD * i, LD * (i + 1))
                for k in range(2):
                    n = 4 * k + i
                    zero.mark(V.tensor_copy(bdq[r, k, n * LR:(n + 1) * LR], q1_n[r, :]))
                    zero.mark(V.tensor_copy(bdk[r, k, n * LR:(n + 1) * LR], k1_n[r, :]))
                zero.mark(V.tensor_copy(bdv[r, r], v1_n[r, :]))
            zero.wait()

            def start(name):
                dve.wait_ge(S["setup_mm"], idx[name] + 1)

            def finish(ins):
                ins.then_inc(S["setup_done"], 1)

            def split(hi, lo, src, scalar):
                zero.link(V.tensor_scalar(hi, src, scalar, None, ALU.mult))
                return V.scalar_tensor_tensor(out=lo, in0=src, scalar=scalar, in1=hi.bitcast(F32), op0=ALU.mult,
                                              op1=ALU.subtract)

            for b in range(2):
                start(f"tok{b}")
                o = sbank(f"tok{b}")[0:48, :].rearrange("p (q e) -> p q e", e=C)
                zero.mark(V.tensor_copy(w_tok[0:48, 8 * b:8 * b + 8, 0:C], o))
                finish(V.tensor_copy(w_tok[IMG_ROW:IMG_ROW + 48, 8 * b:8 * b + 8, C:2 * C], o))
            scale = float(np.float32(1.0) / np.sqrt(HEADS).astype(np.float32))
            for b in range(2):
                start(f"a{b}")
                w = slice(512 * b, 512 * (b + 1))
                finish(split(a_hi[:, w], a_lo[:, w], sbank(f"a{b}")[:, :], scale))
            start("wv")
            finish(split(wv_hi[:, :], wv_lo[:, :], sbank("wv")[:, 0:C], 1.0))
            start("wo")
            finish(V.tensor_copy(wo_t[:, :, :], sbank("wo")[:, 0:4 * C].rearrange("p (k o) -> p k o", k=4)))
            start("wg")
            finish(split(wg_hi[:, :], wg_lo[:, :], sbank("wg")[:, 0:EXPERTS], 1.0))
            for b in range(4):
                start(f"w1_{b}")
                w = slice(4 * b, 4 * b + 4)
                finish(split(w1_hi[:, w, :].rearrange("p q n -> p (q n)"), w1_lo[:, w, :].rearrange("p q n -> p (q n)"),
                             sbank(f"w1_{b}")[:, :], 1.0))
            for b in range(2):
                start(f"w2_{b}")
                finish(V.tensor_copy(w2_t[:, 2 * b:2 * b + 2, :, :].rearrange("p q k n -> p (q k n)"),
                                     sbank(f"w2_{b}")[:, :]))
            start("wx")
            wx_t = sbank("wx")[:, 0:2 * C].rearrange("p (k c) -> p k c", k=2)
            zero.mark(V.tensor_copy(wx_dup[:, :, 0:C], wx_t))
            zero.mark(V.tensor_copy(wx_dup[:, :, C:2 * C], wx_t))
            finish(V.tensor_copy(wxa[:, :, 0:C], wx_t))
            start("bfull")
            finish(tt(wxa[:, :, C], sbank("bfull")[:, 0:2], bx_c[:, :], ALU.add))
            start("wqk")
            finish(split(wqk_hi[:, :], wqk_lo[:, :], sbank("wqk")[:, 0:64], g1_dup[:, 0:1]))
            start("qb")
            finish(V.tensor_copy(q_bias[:, :], sbank("qb")[0:CH, 0:32]))
            start("kb")
            finish(V.tensor_copy(k_bias[:, :], sbank("kb")[0:32, 0:1]))
            start("vt")
            finish(V.tensor_copy(vt[:, :, :], sbank("vt")[:, 0:2 * (C + 1)].rearrange("p (k c) -> p k c", k=2)))
            for i in range(4):
                start(f"u{i}")
                finish(V.tensor_scalar(u_w[:, i::4, :],
                                       sbank(f"u{i}")[0:C + 1, 0:2 * C].rearrange("p (k o) -> p k o", k=2),
                                       g1_aug[:, 0:1], None, ALU.mult))
            start("b1m")
            zero.mark(tt(m1_bias[:, :], sbank("b1m")[:, 0:2], mb1_c[:, :], ALU.add))
            split_m = split(m1_hi[:, :], m1_lo[:, :], m1_n[:, :], g2_dup[:, 0:1])
            zero.mark(split_m)
            zero.mark(split(f1_hi[:, :], f1_lo[:, :], f1_n[:, :], 1.0))
            zero.link(V.tensor_copy(wr_hi[:, :], wr_n[:, 0:1].to_broadcast([128, CH])))
            finish(tt(wr_lo[:, :], wr_n[:, 0:1].to_broadcast([128, CH]), wr_hi[:, :].bitcast(F32), ALU.subtract))
            zero.wait()
            V.engine_nop().then_inc(S["setup_done"], 1)

            def ln_stats(n, j, src, ready, ready_at):
                wait_apart(dve, S["dve_waits"], S[ready], ready_at)
                L = Links(dve, S[f"ln_{n}"], j, LN_LINKS)
                for g in range(G):
                    last = V.bn_stats(st[n][:, g, :], src(g))
                L.mark(last)
                wait_apart(dve, S["dve_waits"], L.sem, L.base + L.k)
                for g in range(G):
                    last = V.bn_aggr(mv[n][:, g, :], st[n][:, g, :])
                L.mark(last)

            def ln_apply(n, j, src, dst, free=None, free_at=0):
                dve.wait_ge(S[f"pow_{n}"], 2 * (j + 1))
                if free:
                    at_least(dve, S[free], free_at)
                for g in range(G):
                    o, x = dst(g), src(g)
                    if len(o.shape) == 3:
                        x = x.unsqueeze(1).to_broadcast([CH, 2, C])
                    last = V.tensor_scalar(o, x, mv[n][:, g, 0:1], rstd[n][:, g:g + 1], ALU.subtract, ALU.mult)
                last.then_inc(S[f"ln_{n}"], 1)

            def lo_part(j, dst, b, hi, split_sem):
                dve.wait_ge(S[hi], j + 1)
                tt(dst[C:128, :], bank[b][C:128, 0:PAIR], dst[C:128, :].bitcast(F32),
                   ALU.subtract).then_inc(S[split_sem], 1)

            def neg_max(j, u, k):
                c, s = u % 2, 4 * u + k
                if k == 0:
                    at_least(dve, S["exp_done"], 16 * j + 4 * u - 4)
                dve.wait_ge(S["scores_ready"], 16 * j + s + 1)
                V.tensor_reduce(nmax[c][:, 2 * k:2 * k + 2],
                                bank[4 + s % 2][0:CH, 0:PAIR].rearrange("p (n t) -> p n t", n=2), AX_X, ALU.max,
                                negate=True).then_inc(S["max_ready"], 1)

            def store_probs(j, u, k):
                c, q = u % 2, k // 2
                if k == 0:
                    at_least(dve, S["pv_ready"], 4 * j + u - 1)
                dve.wait_ge(S["pt_ready"], 16 * j + 4 * u + k + 1)
                V.tensor_copy(prob_t[c][0:CH, q * 4 * CH:(q + 1) * 4 * CH],
                              bank[1][0:CH, 0:4 * CH]).then_inc(S["pt_dve"], 1)

            def invert_sums(j, u):
                c = u % 2
                dve.wait_ge(S["exp_done"], 16 * j + 4 * u + 4)
                at_least(dve, S["ctx_norm"], 4 * j + u - 1)
                V.reciprocal(rsum[c][:, :], psum_[c][:, :]).then_inc(S["recip_done"], 1)

            def normalise(j, u):
                m, c = u // 2, u % 2
                dve.wait_ge(S["recip_done"], 4 * j + u + 1)
                dve.wait_ge(S["pv_ready"], 4 * j + u + 1)
                at_least(dve, ctx_wr[c], 16 * (2 * j + m))
                tt(ctx_sb[c][:, :].rearrange("p (n d) -> p n d", n=HEADS),
                   bank[7][0:CH, :].rearrange("p (n d) -> p n d", n=HEADS),
                   rsum[c][:, :].unsqueeze(2).to_broadcast([CH, HEADS, C]), ALU.mult).then_inc(S["ctx_norm"], 1)

            def store_v(j):
                dve.wait_ge(S["v_ready"], j + 1)
                at_least(dve, S["v_written"], 16 * j)
                V.tensor_copy(v_lin[:, :, :], bank[2][0:C, 0:PAIR].rearrange("p (m t) -> p m t", m=2))\
                    .then_inc(S["v_stored"], 1)

            def store_g_lo(j, s):
                m, k = s // 4, s % 4
                dve.wait_ge(S["g_hi_ready"], 8 * j + s + 1)
                tt(g_lo[m][:, 2 * k:2 * k + 2, :], bank[2 + s % 2][:, 0:PAIR].rearrange("p (n t) -> p n t", n=2),
                   g_hi[m][:, 2 * k:2 * k + 2, :].bitcast(F32), ALU.subtract).then_inc(S["g_split"], 1)

            def add_attention(j):
                dve.wait_ge(S["wo_ready"], j + 1)
                dve.wait_ge(S["h0_stored"], j + 1)
                tt(h[:, j], bank[4][0:CH, 0:256].rearrange("p (g c) -> p g c", g=G), h[:, j],
                   ALU.add).then_inc(S["wo_added"], 1)

            def store_h0(j):
                dve.wait_ge(S["h0_ready"], j + 1)
                V.tensor_copy(h[:, j], bank[0][0:CH, 256:512].rearrange("p (g c) -> p g c", g=G))\
                    .then_inc(S["h0_stored"], 1)

            def body1(i, live):
                a, o = i - 1, i - 2
                for u in range(4):
                    if u == 1 and live(2):
                        normalise(o, 3)
                    if u == 3 and live(1):
                        normalise(a, 0)
                    if live(1):
                        neg_max(a, u, 0)
                    if u == 2 and live(0):
                        store_h0(i)
                    if live(1):
                        neg_max(a, u, 1)
                    if u == 0 and live(2):
                        invert_sums(o, 3)
                    if u > 0 and live(1):
                        invert_sums(a, u - 1)
                        store_probs(a, u - 1, 0)
                    if live(1):
                        neg_max(a, u, 2)
                    if live(0):
                        if u == 2:
                            ln_stats("a", i, lambda g: h[:, i, g, :], "h0_stored", i + 1)
                        if u == 3:
                            ln_apply("a", i, lambda g: h[:, i, g, :], lambda g: y_a[:, g, :, :], "xt_ready", i)
                    if live(1):
                        neg_max(a, u, 3)
                    if u > 0 and live(1):
                        store_probs(a, u - 1, 2)
                if live(1):
                    normalise(a, 1)
                if live(0):
                    lo_part(i, x_a, 0, "xt_hi", "xt_split")
                if live(1):
                    store_probs(a, 3, 0)
                if live(0):
                    store_v(i)
                for s in range(8):
                    if live(1) and s == 2:
                        store_probs(a, 3, 2)
                    if live(1) and s == 3:
                        normalise(a, 2)
                    if live(2) and s == 7:
                        add_attention(o)
                    if live(0):
                        store_g_lo(i, s)

            run_lagged(dve, NP, 2, body1)

            def weigh(j, ep):
                dve.wait_ge(S["ff2_ready"], EP * j + ep + 1)
                dve.wait_ge(S["cb_stored"], EP * j + ep + 1)
                if ep == 0:
                    at_least(dve, S["moe_ready"], j)
                V.scalar_tensor_tensor(out=prod[:, ep, :], in0=bank[2 + ep % 2][:, 0:PAIR], scalar=b2_c[:, ep:ep + 1],
                                       in1=comb_b[:, ep, :], op0=ALU.add, op1=ALU.mult).then_inc(S["prod_done"], 1)

            def gate_scores(j):
                L = Links(dve, S["gate_link"], j, GATE_LINKS)
                dve.wait_ge(S["gate_ready"], j + 1)
                L.link(tt(gs[:, :, :], bank[4][0:CH, PAIR:PAIR + 32].rearrange("p (g e) -> p g e", g=G),
                          bg_b[:, :].unsqueeze(1).to_broadcast([CH, G, EXPERTS]), ALU.add))
                L.link(V.tensor_reduce(gmax[:, :], gs[:, :, :], AX_X, ALU.max, negate=True))
                L.mark(tt(gexp[:, :, :], gs[:, :, :], gmax[:, :].unsqueeze(2).to_broadcast([CH, G, EXPERTS]), ALU.add))
                other = gs[:, :, :].unsqueeze(2).to_broadcast([CH, G, EXPERTS, EXPERTS])
                own = gs[:, :, :].unsqueeze(3).to_broadcast([CH, G, EXPERTS, EXPERTS])
                L.mark(tt(above[:, :, :, :], other, own, ALU.is_gt))
                L.mark(tt(tied[:, :, :, :], other, own, ALU.is_equal))

            def gate_weights(j):
                L = Links(dve, S["gate_link"], j, GATE_LINKS)
                L.k = 5
                dve.wait_ge(S["gate_rank"], 2 * j + 2)
                L.link(V.tensor_reduce(rank_e[:, :, :], above[:, :, :, :], AX_X, ALU.add))
                dve.wait_ge(S["gate_exp"], j + 1)
                L.link(V.scalar_tensor_tensor(out=gexp[:, :, :], in0=rank_e[:, :, :], scalar=1.5, in1=gexp[:, :, :],
                                              op0=ALU.is_lt, op1=ALU.mult))
                L.link(V.tensor_reduce(gsum[:, :], gexp[:, :, :], AX_X, ALU.add))
                L.link(V.reciprocal(gmax[:, :], gsum[:, :]))
                L.link(tt(comb[:, :, :], gexp[:, :, :], gmax[:, :].unsqueeze(2).to_broadcast([CH, G, EXPERTS]),
                          ALU.mult))
                at_least(dve, S["comb_ready"], j)
                L.link(V.tensor_copy(comb2[:, :, 0:EXPERTS].bitcast(F32R), comb[:, :, :]))
                L.mark(tt(comb2[:, :, 32:32 + EXPERTS], comb[:, :, :], comb2[:, :, 0:EXPERTS], ALU.subtract))
                L.end()

            def add_experts(j):
                dve.wait_ge(S["moe_ready"], j + 1)
                tt(h[:, j], bank[2][0:CH, 0:256].rearrange("p (g c) -> p g c", g=G), h[:, j],
                   ALU.add).then_inc(S["moe_added"], 1)

            def k_max(j):
                dve.wait_ge(S["l1_kb"], j + 1)
                V.tensor_reduce(kmax[:, :], kl[:, :, :], AX_X, ALU.max, negate=True).then_inc(S["l1_klink"], 1)

            def k_norm(j):
                dve.wait_ge(S["l1_kexp"], j + 1)
                V.reciprocal(krec[:, :], ksum[:, :]).then_inc(S["l1_klink"], 1)
                dve.wait_ge(S["l1_klink"], KLINKS * j + 2)
                tt(kl[:, :, :], kl[:, :, :], krec[:, :].unsqueeze(2).to_broadcast([32, 2, TOK]),
                   ALU.mult).then_inc(S["l1_klink"], 1)

            qv = ql[:, :, :].rearrange("p (g n) r -> p g (n r)", g=G)

            def q_shift(j):
                L = Links(dve, S["l1_qlink"], j, QLINKS)
                dve.wait_ge(S["l1_q"], j + 1)
                at_least(dve, S["l1_m"], j)
                L.link(tt(qv, bank[5][0:CH, 0:128].rearrange("p (g n) -> p g n", g=G),
                          q_bias[:, :].unsqueeze(1).to_broadcast([CH, G, 32]), ALU.add))
                L.link(V.tensor_reduce(qmax[:, :], ql[:, :, :], AX_X, ALU.max, negate=True))
                L.link(tt(ql[:, :, :], ql[:, :, :], qmax[:, :].unsqueeze(2).to_broadcast([CH, G * LH, LR]), ALU.add))

            def q_norm(j):
                L = Links(dve, S["l1_qlink"], j, QLINKS)
                L.k = 3
                dve.wait_ge(S["l1_qexp"], j + 1)
                L.link(V.tensor_reduce(qmax[:, :], ql[:, :, :], AX_X, ALU.add))
                L.link(V.reciprocal(qmax[:, :], qmax[:, :]))
                L.mark(tt(ql[:, :, :], ql[:, :, :], qmax[:, :].unsqueeze(2).to_broadcast([CH, G * LH, LR]), ALU.mult))
                L.end()

            def store(j, dst, src, ready, done, free=None):
                dve.wait_ge(S[ready], j + 1)
                if free:
                    at_least(dve, S[free], j)
                V.tensor_copy(dst, src).then_inc(S[done], 1)

            def store_m(j):
                dve.wait_ge(S["l1_mt"], j + 1)
                at_least(dve, S["l1_attn"], j)
                for m in range(2):
                    V.tensor_copy(m_bd[32 * m:32 * m + 32, m, :],
                                  bank[5][32 * m:32 * m + 32, 384:384 + C]).then_inc(S["l1_mts"], 1)

            def rank_tokens(j):
                for g in range(G):
                    c, m = g // 2, g % 2
                    V.scalar_tensor_tensor(out=tie_w[:, g, :], in0=w_b[:, m * TOK:(m + 1) * TOK], scalar=w_i[:, g:g + 1],
                                           in1=tie_tok[:, c, :], op0=ALU.is_equal, op1=ALU.mult)\
                        .then_inc(S["l3_rank"], 1)
                for g in range(G):
                    c, m = g // 2, g % 2
                    dve.wait_ge(S["l3_rank"], 9 * j + g + 1)
                    V.scalar_tensor_tensor(out=tie_w[:, g, :], in0=w_b[:, m * TOK:(m + 1) * TOK], scalar=w_i[:, g:g + 1],
                                           in1=tie_w[:, g, :], op0=ALU.is_gt, op1=ALU.add,
                                           accum_out=rank_w[:, g:g + 1]).then_inc(S["l3_rank"], 1)
                dve.wait_ge(S["l3_rank"], 9 * j + 8)
                at_least(dve, S["l3_mul"], j)
                V.scalar_tensor_tensor(out=w_sel[:, :], in0=rank_w[:, :], scalar=KEEP - 0.5, in1=w_i[:, :],
                                       op0=ALU.is_lt, op1=ALU.mult).then_inc(S["l3_rank"], 1)

            def tokens(b):
                return bank[b][0:CH, 0:256].rearrange("p (g c) -> p g c", g=G)

            def store_k_t(j):
                store(j, k_t[:, :, :], bank[5][0:CH, 128:256].rearrange("p (g n) -> p g n", g=G), "l1_kt", "l1_kts",
                      "l1_g")

            def store_kx(j):
                store(j, kx[:, :, :], bank[5][0:C + 1, 256:320].rearrange("p (m n) -> p m n", m=2), "l1_g", "l1_gs",
                      "l1_m")

            def store_qm(j):
                store(j, q_t[:, :, :], bank[5][0:C, 0:TOK].rearrange("p (c t) -> p c t", c=2), "l1_m", "l1_qts",
                      "l1_attn")
                store(j, m_t[:, :, :, :].rearrange("p m n r -> p n m r"),
                      bank[5][0:C, 320:384].rearrange("p (n m r) -> p n m r", n=LH, m=2), "l1_m", "l1_ms", "l1_mt")

            def store_w_i(j):
                store(j, w_i[:, :], bank[7][0:CH, 400:404], "l3_wi", "l3_wis")

            def add_fx(j):
                dve.wait_ge(S["l1_attn"], j + 1)
                dve.wait_ge(S["l1_x3b"], j + 1)
                at_least(dve, S["l2_base"], 2 * j)
                at_least(dve, S["ln_5"], LN_LINKS * j)
                tt(fx[:, :, :], tokens(5), x3b[:, :, :], ALU.add).then_inc(S["l1_fx"], 1)

            def add_h4(j):
                dve.wait_ge(S["l2_out"], j + 1)
                dve.wait_ge(S["l2_base"], 2 * j + 2)
                at_least(dve, S["l3_base"], j)
                tt(h4[:, :, :], tokens(6), base2[:, :, :], ALU.add).then_inc(S["l2_h4"], 1)

            def add_b2(j):
                dve.wait_ge(S["l3_out"], j + 1)
                at_least(dve, S["l3_fin"], j)
                tt(o_t[:, :, :], tokens(7), fb2_b[:, :].unsqueeze(1).to_broadcast([CH, G, C]),
                   ALU.add).then_inc(S["l3_t"], 1)

            def finish_pair(j):
                dve.wait_ge(S["l3_mul"], j + 1)
                dve.wait_ge(S["l3_base"], j + 1)
                at_least(dve, S["l3_stored"], 32 * j)
                tt(o_sb[:, :, :], o_t[:, :, :], base3[:, :, :], ALU.add).then_inc(S["l3_fin"], 1)

            def norm_stats(j, n):
                if n == "m":
                    ln_stats(n, j, lambda g: h[:, j, g, :], "wo_added", j + 1)
                elif n == "3":
                    ln_stats(n, j, lambda g: h[:, j, g, :], "moe_added", j + 1)
                elif n == "4":
                    ln_stats(n, j, lambda g: x3[:, g, :], "ln_3", LN_LINKS * (j + 1))
                elif n == "5":
                    ln_stats(n, j, lambda g: fx[:, g, :], "l1_fx", j + 1)
                else:
                    ln_stats(n, j, lambda g: h4[:, g, :], "l2_h4", j + 1)

            def norm_apply(j, n):
                if n == "m":
                    ln_apply(n, j, lambda g: h[:, j, g, :], lambda g: y_m[:, g, :, :], "xm_t", j)
                elif n == "3":
                    ln_apply(n, j, lambda g: h[:, j, g, :], lambda g: x3[:, g, :], "l1_x3b", j)
                elif n == "4":
                    ln_apply(n, j, lambda g: x3[:, g, :],
                             lambda g: n3[:, g, 0:2 * C].rearrange("p (k c) -> p k c", k=2), "l1_g", j)
                elif n == "5":
                    ln_apply(n, j, lambda g: fx[:, g, :], lambda g: y_2[:, g, :, :], "l2_xt", j)
                else:
                    ln_apply(n, j, lambda g: h4[:, g, :], lambda g: x4[:, g, :, :], "l3_xt", j)

            def lo_xm(j):
                lo_part(j, x_m, 4, "xm_hi", "xm_split")

            def lo_l1(j):
                lo_part(j, x_l1, 5, "l1_hi", "l1_split")

            def lo_l2(j):
                lo_part(j, x_l2, 6, "l2_hi", "l2_split")

            def lo_l3(j):
                lo_part(j, x_l3, 7, "l3_hi", "l3_split")

            def body2(i, live):
                def at(lag, step, *args):
                    if live(lag):
                        step(i - lag, *args)

                at(1, weigh, 1)
                at(2, lo_l1)
                at(3, lo_l2)
                at(0, norm_stats, "m")
                at(2, k_max)
                at(2, q_shift)
                at(4, norm_apply, "6")
                at(2, k_norm)
                at(1, weigh, 2)
                at(0, norm_apply, "m")
                at(2, q_norm)
                at(2, store_k_t)
                at(5, finish_pair)
                at(1, weigh, 3)
                at(2, store_kx)
                at(4, lo_l3)
                at(2, store_qm)
                at(0, lo_xm)
                at(1, add_experts)
                at(2, store_m)
                at(0, gate_scores)
                at(1, norm_stats, "3")
                at(2, add_fx)
                at(4, store_w_i)
                at(2, norm_stats, "5")
                at(3, add_h4)
                at(0, gate_weights)
                at(1, norm_apply, "3")
                at(1, norm_stats, "4")
                at(2, norm_apply, "5")
                at(4, add_b2)
                at(1, norm_apply, "4")
                at(3, norm_stats, "6")
                at(4, rank_tokens)
                at(0, weigh, 0)

            run_lagged(dve, NP, DEPTH, body2)


_INS = ["x", "L0_tok_W", "L0_tok_b", "L0_attn_Wq", "L0_attn_Wk", "L0_attn_Wv", "L0_attn_Wo", "L0_ffn_Wg", "L0_ffn_bg",
        "L0_ffn_W1", "L0_ffn_b1", "L0_ffn_W2", "L0_ffn_b2", "L1_attn_ln1_g", "L1_attn_ln1_b", "L1_attn_Wx",
        "L1_attn_bx", "L1_attn_Wq", "L1_attn_Wk", "L1_attn_Wv", "L1_attn_Wo", "L1_attn_bo", "L1_attn_ln2_g",
        "L1_attn_ln2_b", "L1_attn_W1", "L1_attn_b1", "L1_attn_W2", "L1_attn_b2", "L1_ffn_attention_mask", "L1_ffn_wr",
        "L1_ffn_br", "L1_ffn_w1", "L1_ffn_b1", "L1_ffn_w2", "L1_ffn_b2"]
_UNUSED = {"L1_ffn_attention_mask"}


def kernel(**inputs):
    import numpy as _np
    import concourse.bacc as _bacc
    from concourse import mybir as _mybir
    from concourse.bass_utils import run_bass_kernel_spmd as _run

    nc = _bacc.Bacc("TRN2", target_bir_lowering=False, num_devices=1)
    arrays, args = {}, {}
    for name in _INS:
        if name in _UNUSED:
            continue
        v = _np.ascontiguousarray(inputs[name])
        arrays[f"in_{name}_dram"] = v
        args[name] = nc.dram_tensor(f"in_{name}_dram", v.shape, _mybir.dt.from_np(v.dtype), kind="ExternalInput").ap()
    shape = (inputs["x"].shape[0], TOK, C)
    out = nc.dram_tensor("out_0_dram", shape, F32, kind="ExternalOutput").ap()
    vit_tower(nc, args, out)
    r = _run(nc, [arrays], core_ids=[0])
    return r.results[0]["out_0_dram"]
```

```python
from contextlib import ExitStack

import numpy as np

import concourse.bass as bass
from concourse import mybir

F32 = mybir.dt.float32
F32R = mybir.dt.float32r
ALU = mybir.AluOpType
ACT = mybir.ActivationFunctionType
AX_X = mybir.AxisListType.X

C = 64
PATCH = 16
SIDE = 14
TOK = SIDE * SIDE
CH = TOK // 2
G = 4
PAIR = 2 * TOK
IMG_ROW = 64
XROWS = IMG_ROW + 48
HEADS = 8
EXPERTS = 8
EP = EXPERTS // 2
HCH = 2 * EXPERTS
LH, LR, LD = 8, 4, 32
KEEP = TOK // 2 - 1
EPS = 1e-5
POOL_NORMS = "m3"
LN = {"a": 3, "m": 4, "3": 3, "4": 3, "5": 3, "6": 3}
POW = {n: 3 if n in POOL_NORMS else 2 for n in LN}
DEPTH1 = 3
DEPTH = 5


def at_least(eng, sem, value):
    if isinstance(value, int) and value <= 0:
        return
    eng.wait_ge(sem, value)


def wait_apart(eng, waits, sem, value):
    at_least(eng, sem, value)
    if not isinstance(value, int):
        eng.sem_inc(waits, 1)


class Links:

    def __init__(self, eng, sem, j, n):
        self.eng, self.sem, self.base, self.n, self.k = eng, sem, j * n, n, 0

    def mark(self, ins):
        self.k += 1
        ins.then_inc(self.sem, 1)

    def wait(self):
        self.eng.wait_ge(self.sem, self.base + self.k)

    def link(self, ins):
        self.mark(ins)
        self.wait()

    def end(self):
        assert self.k == self.n, (self.k, self.n)


def run_lagged(eng, pairs, depth, body):
    for i in range(depth + 2):
        body(i, lambda lag, i=i: i - lag >= 0)
    with eng.Fori(depth + 2, pairs) as i:
        body(i, lambda lag: True)
    for i in range(pairs, pairs + depth):
        body(i, lambda lag, i=i: i - lag < pairs)


def vit_tower(nc, a, out):
    B = a["x"].shape[0]
    NP = B // 2
    with ExitStack() as ctx:
        def sb(name, shape, dt=F32):
            return ctx.enter_context(nc.sbuf_tensor(name, shape, dt))

        def sem(name):
            return ctx.enter_context(nc.semaphore(name))

        bank = [ctx.enter_context(nc.psum_tensor(f"bank{i}", [128, 512], F32)) for i in range(8)]

        v_dram = nc.dram_tensor("v_scratch", (NP, 2, C, TOK), F32, kind="Internal").ap()
        ctx_dram = nc.dram_tensor("ctx_scratch", (NP, 2, TOK, HEADS * C), F32, kind="Internal").ap()

        ident = sb("ident", [128, 128])
        ident2 = sb("ident2", [128, C])
        pick = sb("pick", [C, EP, 2, C])
        pick_r = sb("pick_r", [C, EP, 2 * C], F32R)
        tie_tok = sb("tie_tok", [CH, 2, TOK])
        tie_exp = sb("tie_exp", [CH, EXPERTS, EXPERTS])
        eps = sb("eps", [CH, G])
        half = sb("half", [CH, G])
        w_tok = sb("w_tok", [XROWS, PATCH, 2 * C])
        a_hi = sb("a_hi", [128, HEADS * 128], F32R)
        a_lo = sb("a_lo", [128, HEADS * 128], F32R)
        wv_hi, wv_lo = sb("wv_hi", [128, C], F32R), sb("wv_lo", [128, C], F32R)
        wo_t = sb("wo_t", [128, 4, C])
        wg_hi, wg_lo = sb("wg_hi", [128, EXPERTS], F32R), sb("wg_lo", [128, EXPERTS], F32R)
        w1_hi = sb("w1_hi", [128, HCH, 128], F32R)
        w1_lo = sb("w1_lo", [128, HCH, 128], F32R)
        w2_t = sb("w2_t", [128, EP, 2, 128])
        wqk_hi, wqk_lo = sb("wqk_hi", [128, 64], F32R), sb("wqk_lo", [128, 64], F32R)
        wxa = sb("wxa", [128, 2, C + 1])
        wx_dup = sb("wx_dup", [128, 2, 2 * C])
        bdq, bdk = sb("bdq", [128, 2, 32]), sb("bdk", [128, 2, 32])
        bdv = sb("bdv", [128, 128])
        vt = sb("vt", [128, 2, C + 1])
        u_w = sb("u_w", [C + 1, LH, C])
        q_bias = sb("q_bias", [CH, 32])
        k_bias = sb("k_bias", [32, 1])
        m1_hi, m1_lo = sb("m1_hi", [128, 256], F32R), sb("m1_lo", [128, 256], F32R)
        f1_hi, f1_lo = sb("f1_hi", [128, 256], F32R), sb("f1_lo", [128, 256], F32R)
        m1_s = sb("m1_s", [128, 256])
        m1_bias = sb("m1_bias", [128, 2])
        wr_hi, wr_lo = sb("wr_hi", [128, CH], F32R), sb("wr_lo", [128, CH], F32R)
        m2_w, f2_w = sb("m2_w", [128, 2, C]), sb("f2_w", [128, 2, C])
        tok_b = sb("tok_b", [128, 1])
        g1_dup, g2_dup = sb("g1_dup", [128, 1]), sb("g2_dup", [128, 1])
        g1_aug = sb("g1_aug", [C + 1, 1])
        ln1b, ln2b = sb("ln1b", [C, 1]), sb("ln2b", [C, 1])
        bx_c = sb("bx_c", [128, 2])
        mb1_c, fb1_c = sb("mb1_c", [128, 2]), sb("fb1_c", [128, 2])
        b1_c = sb("b1_c", [128, HCH])
        b2_c = sb("b2_c", [128, EP])
        bg_b = sb("bg_b", [CH, EXPERTS])
        bo_b, mb2_b, fb2_b = sb("bo_b", [CH, C]), sb("mb2_b", [CH, C]), sb("fb2_b", [CH, C])
        br_b = sb("br_b", [CH, 1])
        wk_dup = sb("wk_dup", [C, 128])
        wv_n, wg_n = sb("wv_n", [C, 2 * C]), sb("wg_n", [EXPERTS, 2 * C])
        wx_n = sb("wx_n", [C, 256])
        wo1_n = sb("wo1_n", [128, 2, C])
        q1_n, k1_n, v1_n = sb("q1_n", [128, LR]), sb("k1_n", [128, LR]), sb("v1_n", [128, LD])
        m1_n, f1_n = sb("m1_n", [128, 256]), sb("f1_n", [128, 256])
        wr_n = sb("wr_n", [128, 1])

        h = sb("h", [CH, NP, G, C])

        x_sb = sb("x_sb", [XROWS, SIDE, SIDE * PATCH])
        h_t = sb("h_t", [128, TOK])
        NORMS = "am3456"
        st = {n: sb(f"st_{n}", [CH, G, 6]) for n in NORMS}
        mv = {n: sb(f"mv_{n}", [CH, G, 2]) for n in NORMS}
        ve = {n: sb(f"ve_{n}", [CH, G]) for n in NORMS}
        rstd = {n: sb(f"rstd_{n}", [CH, G]) for n in NORMS}
        y_a = sb("y_a", [CH, G, 2, C])
        x_a = sb("x_a", [128, PAIR], F32R)
        v_lin = sb("v_lin", [C, 2, TOK])
        v_tok = sb("v_tok", [CH, 2, 2, C])
        g_hi = [sb(f"g_hi{m}", [128, HEADS, TOK], F32R) for m in range(2)]
        g_lo = [sb(f"g_lo{m}", [128, HEADS, TOK], F32R) for m in range(2)]
        nmax = [sb(f"nmax{c}", [CH, HEADS]) for c in range(2)]
        psum_ = [sb(f"psums{c}", [CH, HEADS]) for c in range(2)]
        rsum = [sb(f"rsum{c}", [CH, HEADS]) for c in range(2)]
        prob = [sb(f"prob{c}", [128, HEADS * TOK]) for c in range(2)]
        prob_t = [sb(f"prob_t{c}", [128, 2 * HEADS * CH]) for c in range(2)]
        ctx_sb = [sb(f"ctx_sb{c}", [CH, HEADS * C]) for c in range(2)]
        ctx_r = [sb(f"ctx_r{m}", [128, 4, TOK]) for m in range(2)]
        hid = sb("hid", [128, 2, 4, PAIR])
        w1_n = hid[:, :, :, :].rearrange("p a b t -> p (a b t)")[:, 0:HCH * 2 * C].rearrange("p (q c) -> p q c", q=HCH)
        w2_n = prob_t[1][:, 0:EP * 256].rearrange("p (q n) -> p q n", q=EP)
        wtok_n = prob[0][0:C, 0:3 * PATCH * PATCH]
        wq_n = prob[1][0:C, 0:2 * HEADS * C].rearrange("p (n c) -> p n c", n=HEADS)
        wo_n = prob_t[0][0:C, 0:512]

        gs = sb("gs", [CH, G, EXPERTS])
        above = sb("above", [CH, G, EXPERTS, EXPERTS])
        tied = sb("tied", [CH, G, EXPERTS, EXPERTS])
        rank_e = sb("rank_e", [CH, G, EXPERTS])
        gmax = sb("gmax", [CH, G])
        gexp = sb("gexp", [CH, G, EXPERTS])
        gsum = sb("gsum", [CH, G])
        comb = sb("comb", [CH, G, EXPERTS])
        comb2 = sb("comb2", [CH, G, C])
        comb_t = sb("comb_t", [C, PAIR], F32R)
        comb_b = prob[0][:, :].rearrange("p (q t) -> p q t", q=EP)
        prod = prob[1][:, :].rearrange("p (q t) -> p q t", q=EP)
        x_parts = g_lo[1][:, :, :].rearrange("p n t -> p (n t)")
        x_m, x_l1, x_l2, x_l3 = (x_parts[:, k * PAIR:(k + 1) * PAIR] for k in range(4))
        turned = prob_t[0][0:CH, 0:3 * G * 2 * C].rearrange("p (k g d c) -> p k g d c", k=3, g=G, d=2)
        y_m, y_2, x4 = (turned[:, k] for k in range(3))
        tie_w = prob_t[1][0:CH, 0:G * TOK].rearrange("p (g t) -> p g t", g=G)
        w_b = prob_t[1][0:CH, G * TOK:G * TOK + PAIR]
        base3 = prob_t[1][0:CH, G * TOK + PAIR:G * TOK + PAIR + G * C].rearrange("p (g c) -> p g c", g=G)
        fx, h4, o_t, o_sb = (ctx_sb[k // 2][:, :].rearrange("p (k g c) -> p k g c", k=2, g=G)[:, k % 2] for k in range(4))
        hid2, hid3 = (ctx_r[m][:, :, :].rearrange("p (k m) t -> p k (m t)", k=2) for m in range(2))
        x3 = sb("x3", [CH, G, C])
        x3b = sb("x3b", [CH, G, C])
        centred = sb("centred", [CH, G, C])
        n3 = sb("n3", [CH, G, 2 * C + 1])
        kl = sb("kl", [32, 2, TOK])
        kmax, ksum, krec = sb("kmax", [32, 2]), sb("ksum", [32, 2]), sb("krec", [32, 2])
        k_t = sb("k_t", [CH, G, 32])
        ql = sb("ql", [CH, G * LH, LR])
        qmax = sb("qmax", [CH, G * LH])
        q_t = sb("q_t", [C, 2, CH])
        kx = sb("kx", [C + 1, 2, 32])
        m_t = sb("m_t", [C, 2, LH, LR])
        m_bd = sb("m_bd", [C, 2, C])
        base2 = sb("base2", [CH, G, C])
        w_i = sb("w_i", [CH, G])
        rank_w = sb("rank_w", [CH, G])
        w_sel = sb("w_sel", [CH, G])

        S = {}

        def sems(names):
            for n in names.split():
                S[n] = sem(n)

        sems("w_first w_loaded consts_ready zeroed setup_mm setup_done setup_link")
        for n in NORMS:
            sems(f"ln_{n} pow_{n}")
        sems("x_loaded tok_ready tok_stored h0_ready h0_stored xt_ready xt_hi xt_split v_ready v_stored "
             "v_written v_ld0 v_ld1 g_ready g_hi_ready g_split scores_ready max_ready exp_done pt_ready pt_dve pt_act "
             "pv_ready ctx_norm ctx_wr0 ctx_wr1 ctx_ld0 ctx_ld1 wo_ready wo_added recip_done")
        sems("sp_waits pe_waits dve_waits")
        sems("xm_t xm_hi xm_split gate_ready gate_link gate_rank gate_exp comb_ready comb_stored cb_ready cb_stored ff1_ready "
             "relu_done ff2_ready prod_done prod_sum moe_ready moe_added")
        sems("l1_xt l1_hi l1_split l1_k l1_kb l1_klink l1_kexp l1_kt l1_kts l1_q l1_qlink l1_qexp "
             "l1_qts l1_g l1_gs l1_m l1_ms l1_mt l1_mts l1_attn l1_fx l1_x3b l1_zero")
        sems("l2_xt l2_hi l2_split l2_ff l2_gelu l2_out l2_h4 l2_base")
        sems("l3_xt l3_hi l3_split l3_w l3_wb l3_wi l3_wis l3_rank l3_ff l3_gelu l3_out l3_t l3_mul l3_fin l3_base "
             "l3_stored")
        v_ld = (S["v_ld0"], S["v_ld1"])
        ctx_wr, ctx_ld = (S["ctx_wr0"], S["ctx_wr1"]), (S["ctx_ld0"], S["ctx_ld1"])

        GATE_LINKS, KLINKS, QLINKS = 12, 3, 6

        SETUP = ["tok0", "tok1", "a0", "a1", "wv", "wo", "wg", "w1_0", "w1_1", "w1_2", "w1_3", "w2_0", "w2_1",
                 "wx", "bfull", "wqk", "qb", "kb", "vt", "u0", "u1", "u2", "u3", "b1m"]
        idx = {n: k for k, n in enumerate(SETUP)}

        def sbank(name):
            return bank[idx[name] % 8]

        def g_cols(g):
            c, m = g // 2, g % 2
            return slice(m * TOK + c * CH, m * TOK + (c + 1) * CH)

        N_FIRST = 13

        def weight_loads():
            col = lambda v: v.rearrange("(p a) -> p a", a=1)
            L = []
            L.append((wtok_n, a["L0_tok_W"]))
            for k in range(2):
                w = slice(k * C, (k + 1) * C)
                L.append((wq_n[:, :, w], a["L0_attn_Wq"].rearrange("(n o) c -> o n c", n=HEADS)))
                L.append((wv_n[:, w], a["L0_attn_Wv"]))
                L.append((wg_n[:, w], a["L0_ffn_Wg"]))
                L.append((w1_n[:, :, w], a["L0_ffn_W1"].rearrange("e (k p) c -> p (e k) c", k=2)))
                L.append((wk_dup[:, k * C:(k + 1) * C], a["L0_attn_Wk"]))
            L.append((wo_n, a["L0_attn_Wo"]))
            L.append((w2_n, a["L0_ffn_W2"].rearrange("(q r) d n -> (r d) q n", r=2)))
            assert len(L) == N_FIRST
            for k in range(2):
                L.append((tok_b[k * C:(k + 1) * C, :], col(a["L0_tok_b"])))
                L.append((g1_dup[k * C:(k + 1) * C, :], col(a["L1_attn_ln1_g"])))
                L.append((g2_dup[k * C:(k + 1) * C, :], col(a["L1_attn_ln2_g"])))
                L.append((m1_n[k * C:(k + 1) * C, :], a["L1_attn_W1"]))
                L.append((f1_n[k * C:(k + 1) * C, :], a["L1_ffn_w1"]))
                L.append((wr_n[k * C:(k + 1) * C, :], a["L1_ffn_wr"]))
            L.append((b1_c[:, :], a["L0_ffn_b1"].rearrange("e (k p) -> p (e k)", k=2)))
            L.append((b2_c[:, :], a["L0_ffn_b2"].rearrange("(q r) d -> (r d) q", r=2)))
            L.append((bg_b[:, :], a["L0_ffn_bg"].partition_broadcast(CH)))
            L.append((wx_n[:, :], a["L1_attn_Wx"]))
            L.append((bx_c[:, :], a["L1_attn_bx"].rearrange("(k p) -> p k", k=2)))
            L.append((g1_aug[0:C, :], col(a["L1_attn_ln1_g"])))
            L.append((ln1b[:, :], col(a["L1_attn_ln1_b"])))
            L.append((ln2b[:, :], col(a["L1_attn_ln2_b"])))
            for i in range(4):
                r = slice(LD * i, LD * (i + 1))
                L.append((q1_n[r, :], a["L1_attn_Wq"]))
                L.append((k1_n[r, :], a["L1_attn_Wk"]))
                L.append((v1_n[r, :], a["L1_attn_Wv"]))
            L.append((wo1_n[:, :, :], a["L1_attn_Wo"].rearrange("(k p) o -> p k o", k=2)))
            L.append((bo_b[:, :], a["L1_attn_bo"].partition_broadcast(CH)))
            L.append((mb1_c[:, :], a["L1_attn_b1"].rearrange("(k p) -> p k", k=2)))
            L.append((m2_w[:, :, :], a["L1_attn_W2"].rearrange("(k p) o -> p k o", k=2)))
            L.append((mb2_b[:, :], a["L1_attn_b2"].partition_broadcast(CH)))
            L.append((fb1_c[:, :], a["L1_ffn_b1"].rearrange("(k p) -> p k", k=2)))
            L.append((f2_w[:, :, :], a["L1_ffn_w2"].rearrange("(k p) o -> p k o", k=2)))
            L.append((fb2_b[:, :], a["L1_ffn_b2"].partition_broadcast(CH)))
            L.append((br_b[:, :], a["L1_ffn_br"].partition_broadcast(CH)))
            return L

        N_LOADS = len(weight_loads())
        block = ctx.enter_context(nc.Block())

        @block.sync
        def _(sp):
            with nc.allow_non_contiguous_dma(reason="bias vectors, a few kB in all"):
                for k, (dst, src) in enumerate(weight_loads()):
                    if k % 2 == 0:
                        sp.dma_start(dst, src).then_inc(S["w_first" if k < N_FIRST else "w_loaded"], 16)
            sp.wait_ge(S["zeroed"], 1)

            def load_x(j):
                wait_apart(sp, S["sp_waits"], S["tok_ready"], j)
                for m in range(2):
                    for ch in range(3):
                        p = IMG_ROW * m + PATCH * ch
                        src = a["x"].rearrange("(j m) c (r q) w -> j m c q r w", m=2, q=PATCH)[j, m, ch]
                        sp.dma_start(x_sb[p:p + PATCH, :, :], src).then_inc(S["x_loaded"], 16)

            def write_ctx(j, u):
                m, c = u // 2, u % 2
                wait_apart(sp, S["sp_waits"], S["ctx_norm"], 4 * j + u + 1)
                sp.dma_start(ctx_dram[j, m, c * CH:(c + 1) * CH, :], ctx_sb[c][:, :]).then_inc(ctx_wr[c], 16)

            def read_ctx(j, m):
                for c in range(2):
                    wait_apart(sp, S["sp_waits"], ctx_wr[c], 16 * (2 * j + m + 1))
                wait_apart(sp, S["sp_waits"], S["wo_ready"], j)
                src = ctx_dram[j, m].rearrange("s n -> (s n)").rearrange("(k p t) -> p k t", k=4, t=TOK)
                sp.dma_start(ctx_r[m][:, :, :], src).then_inc(ctx_ld[m], 16)

            def write_v(j):
                wait_apart(sp, S["sp_waits"], S["v_stored"], j + 1)
                sp.dma_start(v_dram[j].rearrange("m o s -> o m s"), v_lin[:, :, :]).then_inc(S["v_written"], 16)

            def read_v(j, m):
                wait_apart(sp, S["sp_waits"], S["v_written"], 16 * (j + 1))
                wait_apart(sp, S["sp_waits"], S["pv_ready"], 4 * j - 2 + 2 * m)
                src = v_dram[j, m].rearrange("o s -> (o s)").rearrange("(k p d) -> p k d", k=2, d=C)
                sp.dma_start(v_tok[:, m, :, :], src).then_inc(v_ld[m], 16)

            def body1(i, live):
                def at(lag, step, *args):
                    if live(lag):
                        step(i - lag, *args)

                at(3, write_ctx, 1)
                at(2, write_v)
                at(3, read_ctx, 0)
                at(2, read_v, 0)
                at(3, write_ctx, 2)
                at(3, write_ctx, 3)
                at(2, read_v, 1)
                at(3, read_ctx, 1)
                at(0, load_x)
                at(2, write_ctx, 0)

            run_lagged(sp, NP, DEPTH1, body1)

            with sp.Fori(0, NP) as j:
                sp.wait_ge(S["l3_fin"], j + 1)
                for c in range(2):
                    dst = out.rearrange("(j m) (c p) d -> j c p m d", m=2, c=2)[j, c]
                    sp.dma_start(dst, o_sb[:, 2 * c:2 * c + 2, :]).then_inc(S["l3_stored"], 16)
            sp.wait_ge(S["l3_stored"], 32 * NP)

        @block.gpsimd
        def _(pool):
            k = 0
            for t, v in ((ident, 0.0), (ident2, 0.0), (tie_tok, 1.0), (tie_exp, 1.0), (half, -0.5), (eps, EPS), (pick, 0.0)):
                nc.gpsimd.memset(t[:], v).then_inc(S["consts_ready"], 1)
                k += 1
            pool.wait_ge(S["consts_ready"], k)
            nc.gpsimd.affine_select(out=ident[:], in_=ident[:], compare_op=ALU.not_equal, fill=1.0, base=0,
                                    pattern=[[-1, 128]], channel_multiplier=1).then_inc(S["consts_ready"], 1)
            nc.gpsimd.affine_select(out=tie_tok[:], in_=tie_tok[:], compare_op=ALU.is_gt, fill=0.0, base=0,
                                    pattern=[[CH, 2], [-1, TOK]], channel_multiplier=1).then_inc(S["consts_ready"], 1)
            nc.gpsimd.affine_select(out=tie_exp[:], in_=tie_exp[:], compare_op=ALU.is_gt, fill=0.0, base=0,
                                    pattern=[[1, 8], [-1, 8]], channel_multiplier=0).then_inc(S["consts_ready"], 1)
            for k, base in ((10, 0), (12, -C)):
                pool.wait_ge(S["consts_ready"], k)
                nc.gpsimd.affine_select(out=pick[:], in_=pick[:], compare_op=ALU.not_equal, fill=1.0,
                                        base=base // 2, pattern=[[-2, EP], [-1, 2], [0, C]],
                                        channel_multiplier=1).then_inc(S["consts_ready"], 1)
                nc.gpsimd.affine_select(out=ident2[:], in_=ident2[:], compare_op=ALU.not_equal, fill=1.0, base=base,
                                        pattern=[[-1, C]], channel_multiplier=1).then_inc(S["consts_ready"], 1)

            def rstd_pow(j, n):
                pool.wait_ge(S[f"ln_{n}"], LN[n] * j + 2)
                at_least(pool, S[f"pow_{n}"], POW[n] * j)
                nc.gpsimd.tensor_tensor(ve[n][:, :], mv[n][:, :, 1], eps[:, :], ALU.add).then_inc(S[f"pow_{n}"], 1)
                pool.wait_ge(S[f"pow_{n}"], POW[n] * j + 1)
                nc.gpsimd.tensor_tensor(rstd[n][:, :], ve[n][:, :], half[:, :], ALU.pow).then_inc(S[f"pow_{n}"], 1)

            def norm_apply(j, n):
                tt = nc.gpsimd.tensor_tensor
                scale = rstd[n][:, :].unsqueeze(2).to_broadcast([CH, G, C])
                pool.wait_ge(S[f"pow_{n}"], POW[n] * j + 2)
                if n == "3":
                    at_least(pool, S["l1_x3b"], j)
                    at_least(pool, S["ln_4"], LN["4"] * j)
                    dst = x3
                else:
                    at_least(pool, S["ln_m"], LN["m"] * j)
                    dst = centred
                tt(dst[:, :, :], h[:, j], mv[n][:, :, 0:1].to_broadcast([CH, G, C]),
                   ALU.subtract).then_inc(S[f"pow_{n}"], 1)
                pool.wait_ge(S[f"pow_{n}"], POW[n] * j + 3)
                if n == "3":
                    tt(x3[:, :, :], x3[:, :, :], scale, ALU.mult).then_inc(S["ln_3"], 1)
                else:
                    at_least(pool, S["xm_t"], j)
                    for k in range(2):
                        tt(y_m[:, :, k, :], centred[:, :, :], scale, ALU.mult).then_inc(S["ln_m"], 1)

            def finish_pair(j):
                pool.wait_ge(S["l3_mul"], j + 1)
                pool.wait_ge(S["l3_base"], j + 1)
                at_least(pool, S["l3_stored"], 32 * j)
                nc.gpsimd.tensor_tensor(o_sb[:, :, :], o_t[:, :, :], base3[:, :, :], ALU.add).then_inc(S["l3_fin"], 1)

            pool.wait_ge(S["consts_ready"], 14)
            with pool.Fori(0, NP) as j:
                rstd_pow(j, "a")

            def gate_ranks(j):
                pool.wait_ge(S["gate_link"], GATE_LINKS * j + 5)
                nc.gpsimd.tensor_tensor(tied[:, :, :, :], tied[:, :, :, :],
                                        tie_exp[:, :, :].unsqueeze(1).to_broadcast([CH, G, EXPERTS, EXPERTS]),
                                        ALU.mult).then_inc(S["gate_rank"], 1)
                pool.wait_ge(S["gate_rank"], 2 * j + 1)
                nc.gpsimd.tensor_tensor(above[:, :, :, :], above[:, :, :, :], tied[:, :, :, :],
                                        ALU.add).then_inc(S["gate_rank"], 1)

            def sum_experts(j, ep):
                pool.wait_ge(S["prod_done"], EP * j + ep + 1)
                if ep > 1:
                    pool.wait_ge(S["prod_sum"], 3 * j + ep - 1)
                nc.gpsimd.tensor_tensor(prod[:, 0, :], prod[:, 0, :], prod[:, ep, :],
                                        ALU.add).then_inc(S["prod_sum"], 1)

            def base_mlp(j):
                pool.wait_ge(S["l1_fx"], j + 1)
                at_least(pool, S["l2_h4"], j)
                nc.gpsimd.tensor_tensor(base2[:, :, :], h[:, j], fx[:, :, :], ALU.add).then_inc(S["l2_base"], 1)
                pool.wait_ge(S["l2_base"], 2 * j + 1)
                nc.gpsimd.tensor_tensor(base2[:, :, :], base2[:, :, :],
                                        mb2_b[:, :].unsqueeze(1).to_broadcast([CH, G, C]),
                                        ALU.add).then_inc(S["l2_base"], 1)

            def base_ffn(j):
                pool.wait_ge(S["ln_6"], LN["6"] * (j + 1))
                at_least(pool, S["l3_fin"], j)
                nc.gpsimd.tensor_tensor(base3[:, :, :], x4[:, :, 0, :], h4[:, :, :], ALU.add).then_inc(S["l3_base"], 1)

            def base_attn(j):
                pool.wait_ge(S["ln_3"], LN["3"] * (j + 1))
                at_least(pool, S["l1_fx"], j)
                nc.gpsimd.tensor_tensor(x3b[:, :, :], x3[:, :, :],
                                        bo_b[:, :].unsqueeze(1).to_broadcast([CH, G, C]),
                                        ALU.add).then_inc(S["l1_x3b"], 1)

            def route(j):
                pool.wait_ge(S["l3_t"], j + 1)
                pool.wait_ge(S["l3_rank"], 9 * j + 9)
                nc.gpsimd.tensor_tensor(o_t[:, :, :], o_t[:, :, :],
                                        w_sel[:, :].unsqueeze(2).to_broadcast([CH, G, C]),
                                        ALU.mult).then_inc(S["l3_mul"], 1)

            def body(i, live):
                def at(lag, step, *args):
                    if live(lag):
                        step(i - lag, *args)

                at(5, base_ffn)
                at(2, rstd_pow, "3")
                at(2, norm_apply, "3")
                at(4, rstd_pow, "6")
                at(2, rstd_pow, "4")
                at(3, rstd_pow, "5")
                at(0, rstd_pow, "m")
                at(3, base_mlp)
                at(0, norm_apply, "m")
                at(1, sum_experts, 1)
                at(2, base_attn)
                at(5, route)
                at(5, finish_pair)
                at(1, sum_experts, 2)
                at(1, sum_experts, 3)
                at(0, gate_ranks)

            run_lagged(pool, NP, DEPTH, body)

        @block.tensor
        def _(pe):
            pe.wait_ge(S["w_first"], 16 * N_FIRST)
            pe.wait_ge(S["consts_ready"], 14)

            def begin(name, *needs):
                at_least(pe, S["setup_done"], idx[name] - 7)
                for n in needs:
                    pe.wait_ge(S["setup_done"], idx[n] + 1)

            def done(ins):
                ins.then_inc(S["setup_mm"], 1)

            def mm(o, l, r, start=True, stop=True):
                return nc.tensor.matmul(o, l, r, start=start, stop=stop)

            def flat(t):
                return t[:, :, :, :].rearrange("p g k c -> p g (k c)")

            w_view = wtok_n.rearrange("e (k q) -> e q k", q=PATCH)
            for b in range(2):
                begin(f"tok{b}")
                o = sbank(f"tok{b}")[0:48, :].rearrange("p (q e) -> p q e", e=C)
                for q in range(8):
                    last = nc.tensor.transpose(o[:, q, :], w_view[:, 8 * b + q, :], ident[0:C, 0:C])
                done(last)
            for b in range(2):
                begin(f"a{b}")
                for k in range(4):
                    last = mm(sbank(f"a{b}")[:, k * 128:(k + 1) * 128], wq_n[:, 4 * b + k, :], wk_dup[:, :])
                done(last)
            begin("wv")
            done(nc.tensor.transpose(sbank("wv")[:, 0:C], wv_n[:, :], ident[0:C, 0:C]))
            begin("wo")
            for k in range(4):
                last = nc.tensor.transpose(sbank("wo")[:, k * C:(k + 1) * C], wo_n[:, k * 128:(k + 1) * 128],
                                           ident[0:C, 0:C])
            done(last)
            begin("wg")
            done(nc.tensor.transpose(sbank("wg")[:, 0:EXPERTS], wg_n[:, :], ident[0:EXPERTS, 0:EXPERTS]))
            for b in range(4):
                begin(f"w1_{b}")
                for k in range(4):
                    last = nc.tensor.transpose(sbank(f"w1_{b}")[:, k * 128:(k + 1) * 128],
                                               w1_n[:, 4 * b + k, :], ident[:, :])
                done(last)
            for b in range(2):
                begin(f"w2_{b}")
                for k in range(4):
                    ep, hc = 2 * b + k // 2, k % 2
                    last = nc.tensor.transpose(sbank(f"w2_{b}")[:, k * 128:(k + 1) * 128],
                                               w2_n[:, ep, hc * 128:(hc + 1) * 128], ident[:, :])
                done(last)
            pe.wait_ge(S["w_loaded"], 16 * (N_LOADS - N_FIRST))
            begin("wx")
            for k in range(2):
                last = nc.tensor.transpose(sbank("wx")[:, k * C:(k + 1) * C], wx_n[:, k * 128:(k + 1) * 128],
                                           ident[0:C, 0:C])
            done(last)
            begin("bfull")
            for k in range(2):
                last = mm(sbank("bfull")[:, k:k + 1], wx_n[:, k * 128:(k + 1) * 128], ln1b[:, :])
            done(last)
            begin("wqk", "wx", "bfull")
            for t, bd in enumerate((bdq, bdk)):
                for k in range(2):
                    last = mm(sbank("wqk")[:, t * 32:(t + 1) * 32], wx_dup[:, k, :], bd[:, k, :],
                              start=(k == 0), stop=(k == 1))
            done(last)
            begin("qb")
            for k in range(2):
                last = mm(sbank("qb")[0:CH, 0:32], wxa[:, k, C:C + 1].to_broadcast([128, CH]), bdq[:, k, :],
                          start=(k == 0), stop=(k == 1))
            done(last)
            begin("kb")
            for k in range(2):
                last = mm(sbank("kb")[0:32, 0:1], bdk[:, k, :], wxa[:, k, C:C + 1], start=(k == 0), stop=(k == 1))
            done(last)
            begin("vt")
            for k in range(2):
                last = mm(sbank("vt")[:, k * (C + 1):(k + 1) * (C + 1)], bdv[:, :], wxa[:, k, :])
            done(last)
            for i in range(4):
                begin(f"u{i}", "vt")
                r = slice(LD * i, LD * (i + 1))
                for k in range(2):
                    last = mm(sbank(f"u{i}")[0:C + 1, k * C:(k + 1) * C], vt[r, k, :], wo1_n[r, k, :])
                done(last)
            begin("b1m")
            for k in range(2):
                last = mm(sbank("b1m")[:, k:k + 1], m1_n[0:C, k * 128:(k + 1) * 128], ln2b[:, :])
            done(last)
            pe.wait_ge(S["setup_done"], len(SETUP) + 1)

            def mm2(o, hi, lo, x):
                mm(o, hi, x, start=True, stop=False)
                return mm(o, lo, x, start=False, stop=True)

            def tok_part(j, q0, q1):
                if q0 == 0:
                    pe.wait_ge(S["x_loaded"], 96 * (j + 1))
                    at_least(pe, S["v_stored"], j)
                for q in range(q0, q1):
                    last = mm(bank[0][:, 0:TOK], w_tok[:, q, :], x_sb[:, :, q::PATCH],
                              start=(q == 0), stop=(q == PATCH - 1))
                if q1 == PATCH:
                    last.then_inc(S["tok_ready"], 1)

            def h0_turn(j):
                pe.wait_ge(S["tok_stored"], j + 1)
                for c in range(2):
                    last = nc.tensor.transpose(bank[0][0:CH, 256 + c * 128:256 + (c + 1) * 128],
                                               h_t[:, c * CH:(c + 1) * CH], ident[:, :])
                last.then_inc(S["h0_ready"], 1)

            def turn_norm(y, o, ln, j, ready):
                pe.wait_ge(S[ln], LN[ln[3:]] * (j + 1))
                for g in range(G):
                    last = nc.tensor.transpose(o[:, g_cols(g)], y[:, g, 0:2 * C], ident[0:CH, 0:CH])
                last.then_inc(S[ready], 1)

            def v_mm(j):
                pe.wait_ge(S["xt_split"], j + 1)
                mm2(bank[0][0:C, 0:PAIR], wv_hi[:, :], wv_lo[:, :], x_a[:, :]).then_inc(S["v_ready"], 1)

            def g_mm(j, s):
                m, k = s // 4, s % 4
                if s == 0:
                    pe.wait_ge(S["xt_split"], j + 1)
                at_least(pe, S["g_split"], 8 * j + s - 1)
                for n in (2 * k, 2 * k + 1):
                    w = slice(n * 128, (n + 1) * 128)
                    last = mm2(bank[2 + s % 2][:, (n % 2) * TOK:(n % 2 + 1) * TOK], a_hi[:, w], a_lo[:, w],
                               x_a[:, m * TOK:(m + 1) * TOK])
                last.then_inc(S["g_ready"], 1)

            def scores(j, u, k):
                m, c, s = u // 2, u % 2, 4 * u + k
                pe.wait_ge(S["g_split"], 8 * j + 4 * m + k + 1)
                at_least(pe, S["exp_done"], 16 * j + s - 1)
                if s == 0:
                    at_least(pe, S["wo_added"], j - 1)
                for n in (2 * k, 2 * k + 1):
                    r = slice(c * CH, (c + 1) * CH)
                    last = mm2(bank[4 + s % 2][0:CH, (n % 2) * TOK:(n % 2 + 1) * TOK], g_hi[m][:, n, r],
                               g_lo[m][:, n, r], x_a[:, m * TOK:(m + 1) * TOK])
                last.then_inc(S["scores_ready"], 1)

            PT_BANK = (1, 6)

            def turn_probs(j, u, k):
                c, tc, hh = u % 2, k % 2, k // 2
                t = 4 * u + k
                if k == 0:
                    pe.wait_ge(S["exp_done"], 16 * j + 4 * u + 4)
                at_least(pe, S["pt_act" if t % 2 else "pt_dve"], 8 * j + t // 2)
                p = prob[c][0:CH, :].rearrange("p (n t) -> p n t", n=HEADS)
                for q in range(4):
                    last = nc.tensor.transpose(bank[PT_BANK[t % 2]][0:CH, q * CH:(q + 1) * CH],
                                               p[:, 4 * hh + q, tc * CH:(tc + 1) * CH], ident[0:CH, 0:CH])
                last.then_inc(S["pt_ready"], 1)

            def weigh_v(j, u, k):
                m, c = u // 2, u % 2
                if k == 0:
                    pe.wait_ge(v_ld[m], 16 * (j + 1))
                    at_least(pe, S["ctx_norm"], 4 * j + u)
                if k % 2 == 0:
                    pe.wait_ge(S["pt_dve"], 8 * j + 2 * u + k // 2 + 1)
                    pe.wait_ge(S["pt_act"], 8 * j + 2 * u + k // 2 + 1)
                pt = prob_t[c][0:CH, :].rearrange("p (k n s) -> p k n s", k=2, n=HEADS)
                for n in (2 * k, 2 * k + 1):
                    for tc in range(2):
                        last = mm(bank[7][0:CH, n * C:(n + 1) * C], pt[:, tc, n, :], v_tok[:, m, tc, :],
                                  start=(tc == 0), stop=(tc == 1))
                if k == 3:
                    last.then_inc(S["pv_ready"], 1)

            def out_proj(j, g):
                c, m = g // 2, g % 2
                if g == 0:
                    for mm_ in range(2):
                        pe.wait_ge(ctx_ld[mm_], 16 * (j + 1))
                    pe.wait_ge(S["exp_done"], min(16 * j + 31, 16 * NP) if isinstance(j, int) else 16 * j + 31)
                for k in range(4):
                    last = mm(bank[4][0:CH, g * C:(g + 1) * C], ctx_r[m][:, k, c * CH:(c + 1) * CH], wo_t[:, k, :],
                              start=(k == 0), stop=(k == 3))
                if g == G - 1:
                    last.then_inc(S["wo_ready"], 1)

            def turn_a(j):
                turn_norm(flat(y_a), bank[0], "ln_a", j, "xt_ready")

            def body1(i, live):
                def at(lag, step, *args):
                    if live(lag):
                        step(i - lag, *args)

                at(3, turn_probs, 3, 2)
                at(2, scores, 0, 2)
                at(3, turn_probs, 3, 3)
                at(2, g_mm, 4)
                at(2, scores, 0, 3)
                at(2, g_mm, 5)
                at(1, tok_part, 8, 10)
                at(2, scores, 1, 0)
                at(3, weigh_v, 2, 2)
                at(1, tok_part, 10, 12)
                at(3, weigh_v, 2, 3)
                at(2, scores, 1, 1)
                at(2, turn_probs, 0, 0)
                at(2, g_mm, 6)
                at(2, turn_probs, 0, 1)
                at(2, scores, 1, 2)
                at(2, turn_probs, 0, 2)
                at(2, scores, 1, 3)
                at(3, weigh_v, 3, 0)
                at(1, tok_part, 12, 14)
                at(2, turn_probs, 0, 3)
                at(3, weigh_v, 3, 1)
                at(2, scores, 2, 0)
                at(2, g_mm, 7)
                at(2, turn_probs, 1, 0)
                at(3, weigh_v, 3, 2)
                at(2, scores, 2, 1)
                at(3, weigh_v, 3, 3)
                at(2, turn_probs, 1, 1)
                at(1, tok_part, 14, 16)
                at(2, scores, 2, 2)
                at(2, turn_probs, 1, 2)
                at(1, h0_turn)
                at(2, weigh_v, 0, 0)
                at(2, scores, 2, 3)
                at(2, weigh_v, 0, 1)
                at(2, scores, 3, 0)
                at(2, weigh_v, 0, 2)
                at(2, weigh_v, 0, 3)
                at(2, turn_probs, 1, 3)
                at(2, scores, 3, 1)
                at(2, turn_probs, 2, 0)
                at(2, weigh_v, 1, 0)
                at(2, scores, 3, 2)
                at(2, weigh_v, 1, 1)
                at(2, scores, 3, 3)
                at(1, turn_a)
                at(2, weigh_v, 1, 2)
                at(2, turn_probs, 2, 1)
                at(2, weigh_v, 1, 3)
                at(1, g_mm, 0)
                at(3, out_proj, 0)
                at(2, turn_probs, 2, 2)
                at(1, g_mm, 1)
                at(1, v_mm)
                at(3, out_proj, 1)
                at(2, weigh_v, 2, 0)
                at(1, g_mm, 2)
                at(3, out_proj, 2)
                at(0, tok_part, 0, 2)
                at(2, turn_probs, 2, 3)
                at(0, tok_part, 2, 4)
                at(3, out_proj, 3)
                at(2, turn_probs, 3, 0)
                at(1, g_mm, 3)
                at(1, scores, 0, 0)
                at(0, tok_part, 4, 6)
                at(2, turn_probs, 3, 1)
                at(1, scores, 0, 1)
                at(0, tok_part, 6, 8)
                at(2, weigh_v, 2, 1)

            run_lagged(pe, NP, DEPTH1, body1)

            def gate_mm(j):
                pe.wait_ge(S["xm_split"], j + 1)
                for g in range(G):
                    o = bank[4][0:CH, PAIR + g * EXPERTS:PAIR + (g + 1) * EXPERTS]
                    mm(o, x_m[:, g_cols(g)], wg_hi[:, :], start=True, stop=False)
                    last = mm(o, x_m[:, g_cols(g)], wg_lo[:, :], start=False, stop=True)
                last.then_inc(S["gate_ready"], 1)

            def turn_gate(j):
                wait_apart(pe, S["pe_waits"], S["gate_link"], GATE_LINKS * (j + 1))
                for g in range(G):
                    last = nc.tensor.transpose(bank[4][0:C, g_cols(g)], comb2[:, g, :], ident[0:CH, 0:CH])
                last.then_inc(S["comb_ready"], 1)

            def spread_gate(j, ep):
                if ep == 0:
                    pe.wait_ge(S["comb_stored"], j + 1)
                else:
                    pe.wait_ge(S["cb_stored"], EP * j + ep)
                mm(bank[4][:, 0:PAIR], pick_r[:, ep, :], comb_t[:, :]).then_inc(S["cb_ready"], 1)

            def ff1(j, u):
                for q in (2 * u, 2 * u + 1):
                    if q == 0:
                        pe.wait_ge(S["xm_split"], j + 1)
                    at_least(pe, S["relu_done"], HCH * j + q - 1)
                    mm2(bank[q % 2][:, 0:PAIR], w1_hi[:, q, :], w1_lo[:, q, :], x_m[:, :]).then_inc(S["ff1_ready"], 1)

            def ff2(j, ep):
                pe.wait_ge(S["relu_done"], HCH * j + 4 * ep + 4)
                if ep == 0:
                    at_least(pe, S["moe_added"], j)
                at_least(pe, S["prod_done"], EP * j + ep - 1)
                for hc in range(2):
                    for r in range(2):
                        last = mm(bank[2 + ep % 2][r * C:(r + 1) * C, 0:PAIR], w2_t[:, ep, hc, r * C:(r + 1) * C],
                                  hid[:, ep % 2, 2 * r + hc, :], start=(hc == 0), stop=(hc == 1))
                last.then_inc(S["ff2_ready"], 1)

            def moe_out(j):
                pe.wait_ge(S["prod_sum"], 3 * j + 3)
                for g in range(G):
                    last = mm(bank[2][0:CH, g * C:(g + 1) * C], prod[:, 0, g_cols(g)], ident2[:, :])
                last.then_inc(S["moe_ready"], 1)

            def l1_k(j):
                pe.wait_ge(S["l1_split"], j + 1)
                mm2(bank[5][0:32, 0:PAIR], wqk_hi[:, 32:64], wqk_lo[:, 32:64], x_l1[:, :]).then_inc(S["l1_k"], 1)

            def l1_q(j):
                pe.wait_ge(S["l1_kb"], j + 1)
                for g in range(G):
                    o = bank[5][0:CH, g * 32:(g + 1) * 32]
                    mm(o, x_l1[:, g_cols(g)], wqk_hi[:, 0:32], start=True, stop=False)
                    last = mm(o, x_l1[:, g_cols(g)], wqk_lo[:, 0:32], start=False, stop=True)
                last.then_inc(S["l1_q"], 1)

            def l1_kt(j):
                wait_apart(pe, S["pe_waits"], S["l1_klink"], KLINKS * (j + 1))
                for g in range(G):
                    c, m = g // 2, g % 2
                    last = nc.tensor.transpose(bank[5][0:CH, 128 + g * 32:128 + (g + 1) * 32],
                                               kl[:, m, c * CH:(c + 1) * CH], ident[0:32, 0:32])
                last.then_inc(S["l1_kt"], 1)

            def l1_g(j):
                pe.wait_ge(S["l1_kts"], j + 1)
                for m in range(2):
                    for c in range(2):
                        last = mm(bank[5][0:C + 1, 256 + m * 32:256 + (m + 1) * 32], n3[:, 2 * c + m, C:2 * C + 1],
                                  k_t[:, 2 * c + m, :], start=(c == 0), stop=(c == 1))
                last.then_inc(S["l1_g"], 1)

            def l1_qt(j):
                pe.wait_ge(S["l1_gs"], j + 1)
                wait_apart(pe, S["pe_waits"], S["l1_qlink"], QLINKS * (j + 1))
                q = ql[:, :, :].rearrange("p (c n) r -> p c (n r)", c=2)
                for c in range(2):
                    last = nc.tensor.transpose(bank[5][0:C, c * CH:(c + 1) * CH], q[:, c, :], ident[0:CH, 0:CH])

            def l1_m(j):
                for n in range(LH):
                    last = mm(bank[5][0:C, 320 + n * 8:320 + (n + 1) * 8], u_w[:, n, :],
                              kx[:, :, n * LR:(n + 1) * LR])
                last.then_inc(S["l1_m"], 1)

            def l1_mt(j):
                wait_apart(pe, S["pe_waits"], S["l1_ms"], j + 1)
                nc.tensor.transpose(bank[5][0:C, 384:384 + C], m_t[:, :, :, :].rearrange("p m n r -> p (m n r)"),
                                    ident[0:C, 0:C]).then_inc(S["l1_mt"], 1)

            def l1_attn(j):
                pe.wait_ge(S["l1_mts"], 2 * (j + 1))
                pe.wait_ge(S["l1_qts"], j + 1)
                for c in range(2):
                    last = mm(bank[5][0:CH, c * 128:(c + 1) * 128], q_t[:, c, :],
                              m_bd[:, :, :].rearrange("p m o -> p (m o)"))
                last.then_inc(S["l1_attn"], 1)

            def mlp_in(j, k, b, start, ready, gelu, hi, lo, x):
                if k == 0:
                    pe.wait_ge(S[start], j + 1)
                else:
                    pe.wait_ge(S[gelu], 2 * j + 1)
                mm2(bank[b][:, 0:PAIR], hi[:, k * 128:(k + 1) * 128], lo[:, k * 128:(k + 1) * 128],
                    x[:, :]).then_inc(S[ready], 1)

            def mlp_out(j, b, gelu, hid_t, w, ready):
                pe.wait_ge(S[gelu], 2 * j + 2)
                for g in range(G):
                    for k in range(2):
                        last = mm(bank[b][0:CH, g * C:(g + 1) * C], hid_t[:, k, g_cols(g)], w[:, k, :],
                                  start=(k == 0), stop=(k == 1))
                last.then_inc(S[ready], 1)

            def l3_w(j):
                pe.wait_ge(S["l3_split"], j + 1)
                mm2(bank[7][0:CH, 0:PAIR], wr_hi[:, :], wr_lo[:, :], x_l3[:, :]).then_inc(S["l3_w"], 1)

            def l3_wi(j):
                wait_apart(pe, S["pe_waits"], S["l3_wb"], j + 1)
                for g in range(G):
                    last = nc.tensor.transpose(bank[7][0:CH, 400 + g:401 + g], w_b[0:1, g_cols(g)], ident[0:1, 0:1])
                last.then_inc(S["l3_wi"], 1)

            def turn_xm(j):
                at_least(pe, S["cb_stored"], EP * j)
                turn_norm(flat(y_m), bank[4], "ln_m", j, "xm_t")

            def turn_l1(j):
                at_least(pe, S["l1_fx"], j)
                turn_norm(n3, bank[5], "ln_4", j, "l1_xt")

            def turn_l2(j):
                at_least(pe, S["l2_h4"], j)
                turn_norm(flat(y_2), bank[6], "ln_5", j, "l2_xt")

            def turn_l3(j):
                at_least(pe, S["l3_t"], j)
                turn_norm(flat(x4), bank[7], "ln_6", j, "l3_xt")

            def l1_qm(j):
                l1_qt(j)
                l1_m(j)

            def l2_in(j, k):
                mlp_in(j, k, 6, "l2_split", "l2_ff", "l2_gelu", m1_hi, m1_lo, x_l2)

            def l2_out(j):
                mlp_out(j, 6, "l2_gelu", hid2, m2_w, "l2_out")

            def l3_in(j, k):
                mlp_in(j, k, 7, "l3_wis", "l3_ff", "l3_gelu", f1_hi, f1_lo, x_l3)

            def l3_out(j):
                mlp_out(j, 7, "l3_gelu", hid3, f2_w, "l3_out")

            def body2(i, live):
                def at(lag, step, *args):
                    if live(lag):
                        step(i - lag, *args)

                at(4, l2_in, 0)
                at(3, l1_kt)
                at(2, ff2, 3)
                at(1, gate_mm)
                at(5, l3_w)
                at(4, l2_in, 1)
                at(1, ff1, 0)
                at(3, l1_g)
                at(2, moe_out)
                at(5, l3_wi)
                at(1, ff1, 1)
                at(4, l2_out)
                at(3, l1_qm)
                at(1, ff1, 2)
                at(5, l3_in, 0)
                at(1, turn_gate)
                at(3, l1_mt)
                at(1, ff1, 3)
                at(1, spread_gate, 0)
                at(3, l1_attn)
                at(1, ff2, 0)
                at(1, ff1, 4)
                at(1, spread_gate, 1)
                at(1, ff2, 1)
                at(1, spread_gate, 2)
                at(2, turn_l1)
                at(1, ff1, 5)
                at(5, l3_in, 1)
                at(3, turn_l2)
                at(2, l1_k)
                at(1, spread_gate, 3)
                at(1, ff1, 6)
                at(2, l1_q)
                at(5, l3_out)
                at(1, ff2, 2)
                at(1, ff1, 7)
                at(0, turn_xm)
                at(4, turn_l3)

            pe.wait_ge(S["wo_added"], NP)
            run_lagged(pe, NP, DEPTH, body2)

        @block.scalar
        def _(act):
            with nc.allow_non_contiguous_dma(reason="bias vectors, a few kB in all"):
                for k, (dst, src) in enumerate(weight_loads()):
                    if k % 2 == 1:
                        act.dma_start(dst, src).then_inc(S["w_first" if k < N_FIRST else "w_loaded"], 16)
            act.wait_ge(S["w_loaded"], 16 * (N_LOADS - N_FIRST))

            def hi_part(j, dst, b, ready, hi, free, free_at):
                act.wait_ge(S[ready], j + 1)
                at_least(act, S[free], free_at)
                nc.scalar.activation(dst[:, :], bank[b][:, 0:PAIR], ACT.Copy).then_inc(S[hi], 1)

            def exps(j, u, k):
                c, s = u % 2, 4 * u + k
                if k == 0:
                    at_least(act, S["pt_ready"], 16 * j + 4 * u - 4)
                    at_least(act, S["recip_done"], 4 * j + u - 1)
                act.wait_ge(S["max_ready"], 16 * j + s + 1)
                for n in (2 * k, 2 * k + 1):
                    last = nc.scalar.activation(prob[c][0:CH, n * TOK:(n + 1) * TOK],
                                                bank[4 + s % 2][0:CH, (n % 2) * TOK:(n % 2 + 1) * TOK], ACT.Exp,
                                                bias=nmax[c][:, n:n + 1], accum_out=psum_[c][:, n:n + 1])
                last.then_inc(S["exp_done"], 1)

            def store_probs(j, u, k):
                c, q = u % 2, 2 + k // 2
                if k == 1:
                    at_least(act, S["pv_ready"], 4 * j + u - 1)
                act.wait_ge(S["pt_ready"], 16 * j + 4 * u + k + 1)
                nc.scalar.activation(prob_t[c][0:CH, q * 4 * CH:(q + 1) * 4 * CH], bank[6][0:CH, 0:4 * CH],
                                     ACT.Copy).then_inc(S["pt_act"], 1)

            def store_g_hi(j, s):
                m, k = s // 4, s % 4
                act.wait_ge(S["g_ready"], 8 * j + s + 1)
                nc.scalar.activation(g_hi[m][:, 2 * k:2 * k + 2, :],
                                     bank[2 + s % 2][:, 0:PAIR].rearrange("p (n t) -> p n t", n=2),
                                     ACT.Copy).then_inc(S["g_hi_ready"], 1)

            def store_tok(j):
                act.wait_ge(S["tok_ready"], j + 1)
                at_least(act, S["h0_ready"], j)
                nc.scalar.activation(h_t[:, :], bank[0][:, 0:TOK], ACT.Identity,
                                     bias=tok_b[:, :]).then_inc(S["tok_stored"], 1)

            def hi_a(j):
                hi_part(j, x_a, 0, "xt_ready", "xt_hi", "scores_ready", 16 * j)

            def body1(i, live):
                def at(lag, step, *args):
                    if live(lag):
                        step(i - lag, *args)

                at(2, exps, 1, 3)
                at(2, store_probs, 0, 3)
                at(2, store_g_hi, 7)
                at(2, exps, 2, 0)
                at(1, store_tok)
                at(2, exps, 2, 1)
                at(2, exps, 2, 2)
                at(2, store_probs, 1, 1)
                at(2, exps, 2, 3)
                at(2, exps, 3, 0)
                at(2, exps, 3, 1)
                at(2, store_probs, 1, 3)
                at(1, hi_a)
                at(2, exps, 3, 2)
                at(1, store_g_hi, 0)
                at(2, store_probs, 2, 1)
                at(2, exps, 3, 3)
                at(1, store_g_hi, 1)
                at(2, store_probs, 2, 3)
                at(1, store_g_hi, 2)
                at(1, store_g_hi, 3)
                at(1, exps, 0, 0)
                at(2, store_probs, 3, 1)
                at(1, exps, 0, 1)
                at(1, exps, 0, 2)
                at(1, store_g_hi, 4)
                at(1, exps, 0, 3)
                at(1, store_g_hi, 5)
                at(2, store_probs, 3, 3)
                at(1, exps, 1, 0)
                at(1, exps, 1, 1)
                at(1, store_probs, 0, 1)
                at(1, store_g_hi, 6)
                at(1, exps, 1, 2)

            run_lagged(act, NP, DEPTH1, body1)

            def relu(j, q):
                ep = q // 4
                act.wait_ge(S["ff1_ready"], HCH * j + q + 1)
                if q % 4 == 0:
                    at_least(act, S["ff2_ready"], EP * j + ep - 1)
                nc.scalar.activation(hid[:, ep % 2, q % 4, :], bank[q % 2][:, 0:PAIR], ACT.Relu,
                                     bias=b1_c[:, q:q + 1]).then_inc(S["relu_done"], 1)

            def store_comb(j):
                act.wait_ge(S["comb_ready"], j + 1)
                at_least(act, S["cb_ready"], EP * j)
                nc.scalar.activation(comb_t[:, :], bank[4][0:C, 0:PAIR], ACT.Copy).then_inc(S["comb_stored"], 1)

            def store_gate(j, ep):
                act.wait_ge(S["cb_ready"], EP * j + ep + 1)
                at_least(act, S["prod_done"], EP * (j - 1) + ep + 1)
                nc.scalar.activation(comb_b[:, ep, :], bank[4][:, 0:PAIR], ACT.Copy).then_inc(S["cb_stored"], 1)

            def k_bias_add(j):
                act.wait_ge(S["l1_k"], j + 1)
                at_least(act, S["l1_kt"], j)
                nc.scalar.activation(kl[:, :, :], bank[5][0:32, 0:PAIR].rearrange("p (m t) -> p m t", m=2),
                                     ACT.Identity, bias=k_bias[:, :]).then_inc(S["l1_kb"], 1)

            def k_exp(j):
                act.wait_ge(S["l1_klink"], KLINKS * j + 1)
                for m in range(2):
                    last = nc.scalar.activation(kl[:, m, :], kl[:, m, :], ACT.Exp, bias=kmax[:, m:m + 1],
                                                accum_out=ksum[:, m:m + 1])
                last.then_inc(S["l1_kexp"], 1)

            def q_exp(j):
                act.wait_ge(S["l1_qlink"], QLINKS * j + 3)
                nc.scalar.activation(ql[:, :, :], ql[:, :, :], ACT.Exp).then_inc(S["l1_qexp"], 1)

            def gate_exp(j):
                act.wait_ge(S["gate_link"], GATE_LINKS * j + 3)
                nc.scalar.activation(gexp[:, :, :], gexp[:, :, :], ACT.Exp).then_inc(S["gate_exp"], 1)

            def router_bias(j):
                act.wait_ge(S["l3_w"], j + 1)
                at_least(act, S["l3_rank"], 9 * j)
                nc.scalar.activation(w_b[:, :], bank[7][0:CH, 0:PAIR], ACT.Identity,
                                     bias=br_b[:, :]).then_inc(S["l3_wb"], 1)

            def gelu(j, k, b, ff, done, hid_t, bias, func, out_sem):
                act.wait_ge(S[ff], 2 * j + k + 1)
                if k == 0:
                    at_least(act, S[out_sem], j)
                nc.scalar.activation(hid_t[:, k, :], bank[b][:, 0:PAIR], func,
                                     bias=bias[:, k:k + 1]).then_inc(S[done], 1)

            def l2_gelu(j, k):
                gelu(j, k, 6, "l2_ff", "l2_gelu", hid2, m1_bias, ACT.Gelu, "l2_out")

            def l3_gelu(j, k):
                gelu(j, k, 7, "l3_ff", "l3_gelu", hid3, fb1_c, ACT.Gelu_apprx_tanh, "l3_out")

            def hi_xm(j):
                hi_part(j, x_m, 4, "xm_t", "xm_hi", "ff1_ready", HCH * j)

            def hi_l1(j):
                hi_part(j, x_l1, 5, "l1_xt", "l1_hi", "l1_q", j)

            def hi_l2(j):
                hi_part(j, x_l2, 6, "l2_xt", "l2_hi", "l2_ff", 2 * j)

            def hi_l3(j):
                hi_part(j, x_l3, 7, "l3_xt", "l3_hi", "l3_ff", 2 * j)

            def body2(i, live):
                def at(lag, step, *args):
                    if live(lag):
                        step(i - lag, *args)

                at(1, relu, 11)
                at(5, l3_gelu, 1)
                at(2, k_bias_add)
                at(1, store_gate, 3)
                at(1, relu, 12)
                at(3, hi_l2)
                at(1, relu, 13)
                at(2, k_exp)
                at(2, q_exp)
                at(1, relu, 14)
                at(1, relu, 15)
                at(4, hi_l3)
                at(0, hi_xm)
                at(3, l2_gelu, 0)
                at(4, router_bias)
                at(3, l2_gelu, 1)
                at(0, relu, 0)
                at(0, relu, 1)
                at(0, gate_exp)
                at(0, relu, 2)
                at(0, relu, 3)
                at(0, relu, 4)
                at(0, relu, 5)
                at(0, store_comb)
                at(0, relu, 6)
                at(0, relu, 7)
                at(0, store_gate, 0)
                at(4, l3_gelu, 0)
                at(0, relu, 8)
                at(0, store_gate, 1)
                at(0, relu, 9)
                at(0, store_gate, 2)
                at(1, hi_l1)
                at(0, relu, 10)

            run_lagged(act, NP, DEPTH, body2)

        @block.vector
        def _(dve):
            V = nc.vector

            def tt(o, x, y, op):
                return V.tensor_tensor(o, x, y, op)

            V.memset(x_sb[32:IMG_ROW, :, :], 0.0).then_inc(S["zeroed"], 1)
            zero = Links(dve, S["setup_link"], 0, 0)
            for t in (w_tok[:], bdq[:], bdk[:], bdv[:], m_bd[:]):
                zero.mark(V.memset(t, 0.0))
            zero.mark(V.memset(comb2[:], 0.0))
            zero.mark(V.memset(n3[:, :, 2 * C:2 * C + 1], 1.0))
            zero.mark(V.memset(g1_aug[C:C + 1, :], 1.0))
            zero.wait()
            dve.wait_ge(S["consts_ready"], 14)
            zero.mark(V.tensor_copy(pick_r[:, :, :], pick[:, :, :, :].rearrange("p q r d -> p q (r d)")))
            dve.wait_ge(S["w_first"], 16 * N_FIRST)

            def start(name):
                dve.wait_ge(S["setup_mm"], idx[name] + 1)

            def finish(ins):
                ins.then_inc(S["setup_done"], 1)

            def split(hi, lo, src, scalar):
                zero.link(V.tensor_scalar(hi, src, scalar, None, ALU.mult))
                return V.scalar_tensor_tensor(out=lo, in0=src, scalar=scalar, in1=hi.bitcast(F32), op0=ALU.mult,
                                              op1=ALU.subtract)

            for b in range(2):
                start(f"tok{b}")
                o = sbank(f"tok{b}")[0:48, :].rearrange("p (q e) -> p q e", e=C)
                zero.mark(V.tensor_copy(w_tok[0:48, 8 * b:8 * b + 8, 0:C], o))
                finish(V.tensor_copy(w_tok[IMG_ROW:IMG_ROW + 48, 8 * b:8 * b + 8, C:2 * C], o))
            scale = float(np.float32(1.0) / np.sqrt(HEADS).astype(np.float32))
            for b in range(2):
                start(f"a{b}")
                w = slice(512 * b, 512 * (b + 1))
                finish(split(a_hi[:, w], a_lo[:, w], sbank(f"a{b}")[:, :], scale))
            start("wv")
            finish(split(wv_hi[:, :], wv_lo[:, :], sbank("wv")[:, 0:C], 1.0))
            start("wo")
            finish(V.tensor_copy(wo_t[:, :, :], sbank("wo")[:, 0:4 * C].rearrange("p (k o) -> p k o", k=4)))
            start("wg")
            finish(split(wg_hi[:, :], wg_lo[:, :], sbank("wg")[:, 0:EXPERTS], 1.0))
            for b in range(4):
                start(f"w1_{b}")
                w = slice(4 * b, 4 * b + 4)
                finish(split(w1_hi[:, w, :].rearrange("p q n -> p (q n)"), w1_lo[:, w, :].rearrange("p q n -> p (q n)"),
                             sbank(f"w1_{b}")[:, :], 1.0))
            for b in range(2):
                start(f"w2_{b}")
                finish(V.tensor_copy(w2_t[:, 2 * b:2 * b + 2, :, :].rearrange("p q k n -> p (q k n)"),
                                     sbank(f"w2_{b}")[:, :]))
            dve.wait_ge(S["w_loaded"], 16 * (N_LOADS - N_FIRST))
            for i in range(4):
                r = slice(LD * i, LD * (i + 1))
                for k in range(2):
                    n = 4 * k + i
                    zero.mark(V.tensor_copy(bdq[r, k, n * LR:(n + 1) * LR], q1_n[r, :]))
                    zero.mark(V.tensor_copy(bdk[r, k, n * LR:(n + 1) * LR], k1_n[r, :]))
                zero.mark(V.tensor_copy(bdv[r, r], v1_n[r, :]))
            zero.wait()
            start("wx")
            wx_t = sbank("wx")[:, 0:2 * C].rearrange("p (k c) -> p k c", k=2)
            zero.mark(V.tensor_copy(wx_dup[:, :, 0:C], wx_t))
            zero.mark(V.tensor_copy(wx_dup[:, :, C:2 * C], wx_t))
            finish(V.tensor_copy(wxa[:, :, 0:C], wx_t))
            start("bfull")
            finish(tt(wxa[:, :, C], sbank("bfull")[:, 0:2], bx_c[:, :], ALU.add))
            start("wqk")
            finish(split(wqk_hi[:, :], wqk_lo[:, :], sbank("wqk")[:, 0:64], g1_dup[:, 0:1]))
            start("qb")
            finish(V.tensor_copy(q_bias[:, :], sbank("qb")[0:CH, 0:32]))
            start("kb")
            finish(V.tensor_copy(k_bias[:, :], sbank("kb")[0:32, 0:1]))
            start("vt")
            finish(V.tensor_copy(vt[:, :, :], sbank("vt")[:, 0:2 * (C + 1)].rearrange("p (k c) -> p k c", k=2)))
            for i in range(4):
                start(f"u{i}")
                finish(V.tensor_scalar(u_w[:, i::4, :],
                                       sbank(f"u{i}")[0:C + 1, 0:2 * C].rearrange("p (k o) -> p k o", k=2),
                                       g1_aug[:, 0:1], None, ALU.mult))
            start("b1m")
            zero.mark(tt(m1_bias[:, :], sbank("b1m")[:, 0:2], mb1_c[:, :], ALU.add))
            split_m = split(m1_hi[:, :], m1_lo[:, :], m1_n[:, :], g2_dup[:, 0:1])
            zero.mark(split_m)
            zero.mark(split(f1_hi[:, :], f1_lo[:, :], f1_n[:, :], 1.0))
            zero.link(V.tensor_copy(wr_hi[:, :], wr_n[:, 0:1].to_broadcast([128, CH])))
            finish(tt(wr_lo[:, :], wr_n[:, 0:1].to_broadcast([128, CH]), wr_hi[:, :].bitcast(F32), ALU.subtract))
            zero.wait()
            V.engine_nop().then_inc(S["setup_done"], 1)

            def ln_stats(n, j, src, ready, ready_at):
                wait_apart(dve, S["dve_waits"], S[ready], ready_at)
                if n in POOL_NORMS:
                    wait_apart(dve, S["dve_waits"], S[f"ln_{n}"], LN[n] * j)
                L = Links(dve, S[f"ln_{n}"], j, LN[n])
                for g in range(G):
                    last = V.bn_stats(st[n][:, g, :], src(g))
                L.mark(last)
                wait_apart(dve, S["dve_waits"], L.sem, L.base + L.k)
                for g in range(G):
                    last = V.bn_aggr(mv[n][:, g, :], st[n][:, g, :])
                L.mark(last)

            def ln_apply(n, j, src, dst, free=None, free_at=0):
                dve.wait_ge(S[f"pow_{n}"], 2 * (j + 1))
                if free:
                    at_least(dve, S[free], free_at)
                for g in range(G):
                    o, x = dst(g), src(g)
                    if len(o.shape) == 3:
                        x = x.unsqueeze(1).to_broadcast([CH, 2, C])
                    last = V.tensor_scalar(o, x, mv[n][:, g, 0:1], rstd[n][:, g:g + 1], ALU.subtract, ALU.mult)
                last.then_inc(S[f"ln_{n}"], 1)

            def lo_part(j, dst, b, hi, split_sem):
                dve.wait_ge(S[hi], j + 1)
                tt(dst[C:128, :], bank[b][C:128, 0:PAIR], dst[C:128, :].bitcast(F32),
                   ALU.subtract).then_inc(S[split_sem], 1)

            def neg_max(j, u, k):
                c, s = u % 2, 4 * u + k
                if k == 0:
                    at_least(dve, S["exp_done"], 16 * j + 4 * u - 4)
                dve.wait_ge(S["scores_ready"], 16 * j + s + 1)
                V.tensor_reduce(nmax[c][:, 2 * k:2 * k + 2],
                                bank[4 + s % 2][0:CH, 0:PAIR].rearrange("p (n t) -> p n t", n=2), AX_X, ALU.max,
                                negate=True).then_inc(S["max_ready"], 1)

            def store_probs(j, u, k):
                c, q = u % 2, k // 2
                if k == 0:
                    at_least(dve, S["pv_ready"], 4 * j + u - 1)
                dve.wait_ge(S["pt_ready"], 16 * j + 4 * u + k + 1)
                V.tensor_copy(prob_t[c][0:CH, q * 4 * CH:(q + 1) * 4 * CH],
                              bank[1][0:CH, 0:4 * CH]).then_inc(S["pt_dve"], 1)

            def invert_sums(j, u):
                c = u % 2
                dve.wait_ge(S["exp_done"], 16 * j + 4 * u + 4)
                at_least(dve, S["ctx_norm"], 4 * j + u - 1)
                V.reciprocal(rsum[c][:, :], psum_[c][:, :]).then_inc(S["recip_done"], 1)

            def normalise(j, u):
                m, c = u // 2, u % 2
                dve.wait_ge(S["recip_done"], 4 * j + u + 1)
                dve.wait_ge(S["pv_ready"], 4 * j + u + 1)
                at_least(dve, ctx_wr[c], 16 * (2 * j + m))
                tt(ctx_sb[c][:, :].rearrange("p (n d) -> p n d", n=HEADS),
                   bank[7][0:CH, :].rearrange("p (n d) -> p n d", n=HEADS),
                   rsum[c][:, :].unsqueeze(2).to_broadcast([CH, HEADS, C]), ALU.mult).then_inc(S["ctx_norm"], 1)

            def store_v(j):
                dve.wait_ge(S["v_ready"], j + 1)
                at_least(dve, S["v_written"], 16 * j)
                V.tensor_copy(v_lin[:, :, :], bank[0][0:C, 0:PAIR].rearrange("p (m t) -> p m t", m=2))\
                    .then_inc(S["v_stored"], 1)

            def store_g_lo(j, s):
                m, k = s // 4, s % 4
                dve.wait_ge(S["g_hi_ready"], 8 * j + s + 1)
                tt(g_lo[m][:, 2 * k:2 * k + 2, :], bank[2 + s % 2][:, 0:PAIR].rearrange("p (n t) -> p n t", n=2),
                   g_hi[m][:, 2 * k:2 * k + 2, :].bitcast(F32), ALU.subtract).then_inc(S["g_split"], 1)

            def add_attention(j):
                dve.wait_ge(S["wo_ready"], j + 1)
                dve.wait_ge(S["h0_stored"], j + 1)
                tt(h[:, j], bank[4][0:CH, 0:256].rearrange("p (g c) -> p g c", g=G), h[:, j],
                   ALU.add).then_inc(S["wo_added"], 1)

            def store_h0(j):
                dve.wait_ge(S["h0_ready"], j + 1)
                V.tensor_copy(h[:, j], bank[0][0:CH, 256:512].rearrange("p (g c) -> p g c", g=G))\
                    .then_inc(S["h0_stored"], 1)

            def attn_stats(j):
                ln_stats("a", j, lambda g: h[:, j, g, :], "h0_stored", j + 1)

            def attn_apply(j):
                ln_apply("a", j, lambda g: h[:, j, g, :], lambda g: y_a[:, g, :, :], "xt_ready", j)

            def lo_a(j):
                lo_part(j, x_a, 0, "xt_hi", "xt_split")

            def body1(i, live):
                def at(lag, step, *args):
                    if live(lag):
                        step(i - lag, *args)

                at(2, neg_max, 1, 2)
                at(2, invert_sums, 0)
                at(2, store_probs, 0, 2)
                at(2, neg_max, 1, 3)
                at(2, neg_max, 2, 0)
                at(2, store_g_lo, 6)
                at(2, store_g_lo, 7)
                at(2, neg_max, 2, 1)
                at(2, store_probs, 1, 0)
                at(3, normalise, 3)
                at(2, neg_max, 2, 2)
                at(1, store_h0)
                at(1, attn_stats)
                at(2, invert_sums, 1)
                at(2, neg_max, 2, 3)
                at(2, store_probs, 1, 2)
                at(2, neg_max, 3, 0)
                at(2, normalise, 0)
                at(2, neg_max, 3, 1)
                at(1, attn_apply)
                at(2, neg_max, 3, 2)
                at(2, store_probs, 2, 0)
                at(1, lo_a)
                at(2, neg_max, 3, 3)
                at(2, normalise, 1)
                at(2, invert_sums, 2)
                at(1, store_g_lo, 0)
                at(1, store_v)
                at(2, store_probs, 2, 2)
                at(1, store_g_lo, 1)
                at(3, add_attention)
                at(1, store_g_lo, 2)
                at(1, neg_max, 0, 0)
                at(2, store_probs, 3, 0)
                at(1, neg_max, 0, 1)
                at(1, store_g_lo, 3)
                at(1, neg_max, 0, 2)
                at(2, invert_sums, 3)
                at(1, neg_max, 0, 3)
                at(2, store_probs, 3, 2)
                at(1, store_g_lo, 4)
                at(1, neg_max, 1, 0)
                at(1, store_g_lo, 5)
                at(1, neg_max, 1, 1)
                at(1, store_probs, 0, 0)
                at(2, normalise, 2)

            run_lagged(dve, NP, DEPTH1, body1)

            def weigh(j, ep):
                dve.wait_ge(S["ff2_ready"], EP * j + ep + 1)
                dve.wait_ge(S["cb_stored"], EP * j + ep + 1)
                if ep == 0:
                    at_least(dve, S["moe_ready"], j)
                V.scalar_tensor_tensor(out=prod[:, ep, :], in0=bank[2 + ep % 2][:, 0:PAIR], scalar=b2_c[:, ep:ep + 1],
                                       in1=comb_b[:, ep, :], op0=ALU.add, op1=ALU.mult).then_inc(S["prod_done"], 1)

            def gate_scores(j):
                L = Links(dve, S["gate_link"], j, GATE_LINKS)
                dve.wait_ge(S["gate_ready"], j + 1)
                L.link(tt(gs[:, :, :], bank[4][0:CH, PAIR:PAIR + 32].rearrange("p (g e) -> p g e", g=G),
                          bg_b[:, :].unsqueeze(1).to_broadcast([CH, G, EXPERTS]), ALU.add))
                L.link(V.tensor_reduce(gmax[:, :], gs[:, :, :], AX_X, ALU.max, negate=True))
                L.mark(tt(gexp[:, :, :], gs[:, :, :], gmax[:, :].unsqueeze(2).to_broadcast([CH, G, EXPERTS]), ALU.add))
                other = gs[:, :, :].unsqueeze(2).to_broadcast([CH, G, EXPERTS, EXPERTS])
                own = gs[:, :, :].unsqueeze(3).to_broadcast([CH, G, EXPERTS, EXPERTS])
                L.mark(tt(above[:, :, :, :], other, own, ALU.is_gt))
                L.mark(tt(tied[:, :, :, :], other, own, ALU.is_equal))

            def gate_weights(j):
                L = Links(dve, S["gate_link"], j, GATE_LINKS)
                L.k = 5
                dve.wait_ge(S["gate_rank"], 2 * j + 2)
                L.link(V.tensor_reduce(rank_e[:, :, :], above[:, :, :, :], AX_X, ALU.add))
                dve.wait_ge(S["gate_exp"], j + 1)
                L.link(V.scalar_tensor_tensor(out=gexp[:, :, :], in0=rank_e[:, :, :], scalar=1.5, in1=gexp[:, :, :],
                                              op0=ALU.is_lt, op1=ALU.mult))
                L.link(V.tensor_reduce(gsum[:, :], gexp[:, :, :], AX_X, ALU.add))
                L.link(V.reciprocal(gmax[:, :], gsum[:, :]))
                L.link(tt(comb[:, :, :], gexp[:, :, :], gmax[:, :].unsqueeze(2).to_broadcast([CH, G, EXPERTS]),
                          ALU.mult))
                at_least(dve, S["comb_ready"], j)
                L.link(V.tensor_copy(comb2[:, :, 0:EXPERTS].bitcast(F32R), comb[:, :, :]))
                L.mark(tt(comb2[:, :, 32:32 + EXPERTS], comb[:, :, :], comb2[:, :, 0:EXPERTS], ALU.subtract))
                L.end()

            def add_experts(j):
                dve.wait_ge(S["moe_ready"], j + 1)
                tt(h[:, j], bank[2][0:CH, 0:256].rearrange("p (g c) -> p g c", g=G), h[:, j],
                   ALU.add).then_inc(S["moe_added"], 1)

            def k_max(j):
                dve.wait_ge(S["l1_kb"], j + 1)
                V.tensor_reduce(kmax[:, :], kl[:, :, :], AX_X, ALU.max, negate=True).then_inc(S["l1_klink"], 1)

            def k_norm(j):
                dve.wait_ge(S["l1_kexp"], j + 1)
                V.reciprocal(krec[:, :], ksum[:, :]).then_inc(S["l1_klink"], 1)
                dve.wait_ge(S["l1_klink"], KLINKS * j + 2)
                tt(kl[:, :, :], kl[:, :, :], krec[:, :].unsqueeze(2).to_broadcast([32, 2, TOK]),
                   ALU.mult).then_inc(S["l1_klink"], 1)

            qv = ql[:, :, :].rearrange("p (g n) r -> p g (n r)", g=G)

            def q_shift(j):
                L = Links(dve, S["l1_qlink"], j, QLINKS)
                dve.wait_ge(S["l1_q"], j + 1)
                at_least(dve, S["l1_m"], j)
                L.link(tt(qv, bank[5][0:CH, 0:128].rearrange("p (g n) -> p g n", g=G),
                          q_bias[:, :].unsqueeze(1).to_broadcast([CH, G, 32]), ALU.add))
                L.link(V.tensor_reduce(qmax[:, :], ql[:, :, :], AX_X, ALU.max, negate=True))
                L.link(tt(ql[:, :, :], ql[:, :, :], qmax[:, :].unsqueeze(2).to_broadcast([CH, G * LH, LR]), ALU.add))

            def q_norm(j):
                L = Links(dve, S["l1_qlink"], j, QLINKS)
                L.k = 3
                dve.wait_ge(S["l1_qexp"], j + 1)
                L.link(V.tensor_reduce(qmax[:, :], ql[:, :, :], AX_X, ALU.add))
                L.link(V.reciprocal(qmax[:, :], qmax[:, :]))
                L.mark(tt(ql[:, :, :], ql[:, :, :], qmax[:, :].unsqueeze(2).to_broadcast([CH, G * LH, LR]), ALU.mult))
                L.end()

            def store(j, dst, src, ready, done, free=None):
                dve.wait_ge(S[ready], j + 1)
                if free:
                    at_least(dve, S[free], j)
                V.tensor_copy(dst, src).then_inc(S[done], 1)

            def store_m(j):
                dve.wait_ge(S["l1_mt"], j + 1)
                at_least(dve, S["l1_attn"], j)
                for m in range(2):
                    V.tensor_copy(m_bd[32 * m:32 * m + 32, m, :],
                                  bank[5][32 * m:32 * m + 32, 384:384 + C]).then_inc(S["l1_mts"], 1)

            def rank_ties(j):
                dve.wait_ge(S["l3_wis"], j + 1)
                for g in range(G):
                    c, m = g // 2, g % 2
                    V.scalar_tensor_tensor(out=tie_w[:, g, :], in0=w_b[:, m * TOK:(m + 1) * TOK], scalar=w_i[:, g:g + 1],
                                           in1=tie_tok[:, c, :], op0=ALU.is_equal, op1=ALU.mult)\
                        .then_inc(S["l3_rank"], 1)

            def rank_tokens(j):
                for g in range(G):
                    c, m = g // 2, g % 2
                    dve.wait_ge(S["l3_rank"], 9 * j + g + 1)
                    V.scalar_tensor_tensor(out=tie_w[:, g, :], in0=w_b[:, m * TOK:(m + 1) * TOK], scalar=w_i[:, g:g + 1],
                                           in1=tie_w[:, g, :], op0=ALU.is_gt, op1=ALU.add,
                                           accum_out=rank_w[:, g:g + 1]).then_inc(S["l3_rank"], 1)
                dve.wait_ge(S["l3_rank"], 9 * j + 8)
                at_least(dve, S["l3_mul"], j)
                V.scalar_tensor_tensor(out=w_sel[:, :], in0=rank_w[:, :], scalar=KEEP - 0.5, in1=w_i[:, :],
                                       op0=ALU.is_lt, op1=ALU.mult).then_inc(S["l3_rank"], 1)

            def tokens(b):
                return bank[b][0:CH, 0:256].rearrange("p (g c) -> p g c", g=G)

            def store_k_t(j):
                store(j, k_t[:, :, :], bank[5][0:CH, 128:256].rearrange("p (g n) -> p g n", g=G), "l1_kt", "l1_kts",
                      "l1_g")

            def store_kx(j):
                store(j, kx[:, :, :], bank[5][0:C + 1, 256:320].rearrange("p (m n) -> p m n", m=2), "l1_g", "l1_gs",
                      "l1_m")

            def store_qm(j):
                store(j, q_t[:, :, :], bank[5][0:C, 0:TOK].rearrange("p (c t) -> p c t", c=2), "l1_m", "l1_qts",
                      "l1_attn")
                store(j, m_t[:, :, :, :].rearrange("p m n r -> p n m r"),
                      bank[5][0:C, 320:384].rearrange("p (n m r) -> p n m r", n=LH, m=2), "l1_m", "l1_ms", "l1_mt")

            def store_w_i(j):
                store(j, w_i[:, :], bank[7][0:CH, 400:404], "l3_wi", "l3_wis")

            def add_fx(j):
                dve.wait_ge(S["l1_attn"], j + 1)
                dve.wait_ge(S["l1_x3b"], j + 1)
                at_least(dve, S["l2_base"], 2 * j)
                at_least(dve, S["ln_5"], LN["5"] * j)
                tt(fx[:, :, :], tokens(5), x3b[:, :, :], ALU.add).then_inc(S["l1_fx"], 1)

            def add_h4(j):
                dve.wait_ge(S["l2_out"], j + 1)
                dve.wait_ge(S["l2_base"], 2 * j + 2)
                at_least(dve, S["l3_base"], j)
                tt(h4[:, :, :], tokens(6), base2[:, :, :], ALU.add).then_inc(S["l2_h4"], 1)

            def add_b2(j):
                dve.wait_ge(S["l3_out"], j + 1)
                at_least(dve, S["l3_fin"], j)
                tt(o_t[:, :, :], tokens(7), fb2_b[:, :].unsqueeze(1).to_broadcast([CH, G, C]),
                   ALU.add).then_inc(S["l3_t"], 1)

            def norm_stats(j, n):
                if n == "m":
                    ln_stats(n, j, lambda g: h[:, j, g, :], "wo_added", j + 1)
                elif n == "3":
                    ln_stats(n, j, lambda g: h[:, j, g, :], "moe_added", j + 1)
                elif n == "4":
                    ln_stats(n, j, lambda g: x3[:, g, :], "ln_3", LN["3"] * (j + 1))
                elif n == "5":
                    ln_stats(n, j, lambda g: fx[:, g, :], "l1_fx", j + 1)
                else:
                    ln_stats(n, j, lambda g: h4[:, g, :], "l2_h4", j + 1)

            def norm_apply(j, n):
                if n == "4":
                    ln_apply(n, j, lambda g: x3[:, g, :],
                             lambda g: n3[:, g, 0:2 * C].rearrange("p (k c) -> p k c", k=2), "l1_g", j)
                elif n == "5":
                    ln_apply(n, j, lambda g: fx[:, g, :], lambda g: y_2[:, g, :, :], "l2_xt", j)
                else:
                    ln_apply(n, j, lambda g: h4[:, g, :], lambda g: x4[:, g, :, :], "l3_xt", j)

            def lo_xm(j):
                lo_part(j, x_m, 4, "xm_hi", "xm_split")

            def lo_l1(j):
                lo_part(j, x_l1, 5, "l1_hi", "l1_split")

            def lo_l2(j):
                lo_part(j, x_l2, 6, "l2_hi", "l2_split")

            def lo_l3(j):
                lo_part(j, x_l3, 7, "l3_hi", "l3_split")

            def body2(i, live):
                def at(lag, step, *args):
                    if live(lag):
                        step(i - lag, *args)

                at(3, k_norm)
                at(3, q_norm)
                at(5, lo_l3)
                at(1, lo_xm)
                at(2, weigh, 2)
                at(3, store_k_t)
                at(2, weigh, 3)
                at(1, gate_scores)
                at(0, norm_stats, "m")
                at(3, store_kx)
                at(2, add_experts)
                at(5, store_w_i)
                at(2, norm_stats, "3")
                at(1, gate_weights)
                at(4, add_h4)
                at(3, store_qm)
                at(4, norm_stats, "6")
                at(3, store_m)
                at(2, norm_stats, "4")
                at(3, add_fx)
                at(3, norm_stats, "5")
                at(5, rank_ties)
                at(2, norm_apply, "4")
                at(3, norm_apply, "5")
                at(1, weigh, 0)
                at(2, lo_l1)
                at(1, weigh, 1)
                at(5, rank_tokens)
                at(2, k_max)
                at(4, norm_apply, "6")
                at(2, q_shift)
                at(5, add_b2)
                at(3, lo_l2)

            run_lagged(dve, NP, DEPTH, body2)


_INS = ["x", "L0_tok_W", "L0_tok_b", "L0_attn_Wq", "L0_attn_Wk", "L0_attn_Wv", "L0_attn_Wo", "L0_ffn_Wg", "L0_ffn_bg",
        "L0_ffn_W1", "L0_ffn_b1", "L0_ffn_W2", "L0_ffn_b2", "L1_attn_ln1_g", "L1_attn_ln1_b", "L1_attn_Wx",
        "L1_attn_bx", "L1_attn_Wq", "L1_attn_Wk", "L1_attn_Wv", "L1_attn_Wo", "L1_attn_bo", "L1_attn_ln2_g",
        "L1_attn_ln2_b", "L1_attn_W1", "L1_attn_b1", "L1_attn_W2", "L1_attn_b2", "L1_ffn_attention_mask", "L1_ffn_wr",
        "L1_ffn_br", "L1_ffn_w1", "L1_ffn_b1", "L1_ffn_w2", "L1_ffn_b2"]
_UNUSED = {"L1_ffn_attention_mask"}


def kernel(**inputs):
    import numpy as _np
    import concourse.bacc as _bacc
    from concourse import mybir as _mybir
    from concourse.bass_utils import run_bass_kernel_spmd as _run

    nc = _bacc.Bacc("TRN2", target_bir_lowering=False, num_devices=1)
    arrays, args = {}, {}
    for name in _INS:
        if name in _UNUSED:
            continue
        v = _np.ascontiguousarray(inputs[name])
        arrays[f"in_{name}_dram"] = v
        args[name] = nc.dram_tensor(f"in_{name}_dram", v.shape, _mybir.dt.from_np(v.dtype), kind="ExternalInput").ap()
    shape = (inputs["x"].shape[0], TOK, C)
    out = nc.dram_tensor("out_0_dram", shape, F32, kind="ExternalOutput").ap()
    vit_tower(nc, args, out)
    r = _run(nc, [arrays], core_ids=[0])
    return r.results[0]["out_0_dram"]
```
